# Optimizing a Trainium2 kernel written in Bass

```python
import numpy as np
import jax
import jax.numpy as jnp

def _softmax(x, axis=-1):
    return jax.nn.softmax(x, axis=axis)

def _gelu(x):
    return jax.nn.gelu(x, approximate=True)

def _silu(x):
    return jax.nn.silu(x)

def _sigmoid(x):
    return jax.nn.sigmoid(x)

def _layernorm(x, axis=-1, eps=1e-05):
    m = jnp.mean(x, axis=axis, keepdims=True)
    v = jnp.var(x, axis=axis, keepdims=True)
    return (x - m) / jnp.sqrt(v + eps)

def _scatter_add(tgt, idx, src, axis=0):
    return tgt.at[idx].add(src)

def _segment_sum(src, seg, n):
    return jax.ops.segment_sum(src, seg, n)
kernel_name = 'mk_adj_preln_d4_adj_r2_0ffb12'

def setup_inputs(seed: int=0):
    np.random.seed(seed)
    _w = jnp.asarray

    def _rec_inputs():
        import jax
        import jax.numpy as jnp
        _gk = jax.random.key(seed)
        x = 7.22e-05 + 1 * jax.random.normal(jax.random.fold_in(_gk, 1), (8, 2048, 128), jnp.float32)
        _w = (1.0 + jnp.arange(2048, dtype=jnp.float32)) ** (-0.5)
        _w = _w / _w.mean()
        _pij = jnp.clip(0.0078125 * _w[:, None] * _w[None, :], 0.0, 1.0)
        _a = jax.random.uniform(jax.random.fold_in(_gk, 2), (2048, 2048)) < _pij
        _a = jnp.logical_or(_a, jnp.swapaxes(_a, -1, -2))
        _a = jnp.logical_or(_a, jnp.eye(2048, dtype=bool))
        _af = _a.astype(jnp.float32)
        _af = _af * jax.random.uniform(jax.random.fold_in(_gk, 3), (2048, 2048), jnp.float32, 0.05, 0.119748)
        adj = _af
        return (x, adj)
    x, adj = _rec_inputs()

    def _L0_gnn_setup():
        import jax, jax.numpy as jnp
        import numpy as np
        B, N, F_IN, F_OUT = (8, 2048, 128, 128)
        key = jax.random.key(seed)
        k1, k2, k3 = jax.random.split(key, 3)
        H = jax.random.normal(k1, (B, N, F_IN), dtype=jnp.float32)
        W = jax.random.normal(k2, (F_IN, F_OUT), dtype=jnp.float32) * (1.0 / np.sqrt(F_IN))
        A = jax.random.normal(k3, (N, N), dtype=jnp.float32) * (1.414 * np.sqrt(2.0 / (N + N)))
        return {'H': H, 'W': W, 'A': A}
    _L0_gnn_all = _L0_gnn_setup()
    _L0_gnn_in = {k: v for k, v in _L0_gnn_all.items() if k in ('W',)}
    del _L0_gnn_all

    def _L1_gnn_setup():
        import jax, jax.numpy as jnp
        import numpy as np
        ALPHA = 0.2
        key = jax.random.key(seed)
        k1, k2, k3, k4 = jax.random.split(key, 4)
        B, N, Fin, Fout = (8, 1024, 128, 128)
        h = jax.random.normal(k1, (B, N, Fin), dtype=jnp.float32)
        adj = jax.random.randint(k2, (N, N), 0, 2).astype(jnp.float32)
        adj = jnp.maximum(adj, jnp.eye(N, dtype=jnp.float32))

        def xavier(k, shape, gain=1.414):
            fan_in, fan_out = (shape[0], shape[1])
            a = gain * np.sqrt(6.0 / (fan_in + fan_out))
            return jax.random.uniform(k, shape, dtype=jnp.float32, minval=-a, maxval=a)
        W = xavier(k3, (Fin, Fout))
        a = xavier(k4, (2 * Fout, 1))
        return {'h': h, 'adj_matrix': adj, 'W': W, 'a': a}
    _L1_gnn_all = _L1_gnn_setup()
    _L1_gnn_in = {k: v for k, v in _L1_gnn_all.items() if k in ('W', 'a')}
    del _L1_gnn_all

    def _L2_gnn_setup():
        import jax, jax.numpy as jnp
        import numpy as np
        B, T, D, H = (64, 1024, 128, 128)
        MAX_SKIP = 4

        def _lstm_last(Wih, Whh, bih, bhh, xs):
            N, _, Hd = xs.shape
            bias = bih + bhh

            def step(carry, x_t):
                h, c = carry
                g = x_t @ Wih.T + h @ Whh.T + bias
                i, f, gg, o = jnp.split(g, 4, axis=-1)
                c = jax.nn.sigmoid(f) * c + jax.nn.sigmoid(i) * jnp.tanh(gg)
                h = jax.nn.sigmoid(o) * jnp.tanh(c)
                return ((h, c), None)
            init = (jnp.zeros((N, Hd), xs.dtype), jnp.zeros((N, Hd), xs.dtype))
            (h_last, _), _ = jax.lax.scan(step, init, jnp.swapaxes(xs, 0, 1))
            return h_last
        key = jax.random.key(seed)
        ks = jax.random.split(key, 8)
        s = 0.05
        x = jax.random.normal(ks[0], (B, T, D), jnp.float32)
        adj = jax.random.uniform(ks[1], (T, T), jnp.float32) / T
        Wg0 = jax.random.normal(ks[2], (D, H), jnp.float32) * s
        bg0 = jnp.zeros((H,), jnp.float32)
        Wg1 = jax.random.normal(ks[3], (H, H), jnp.float32) * s
        bg1 = jnp.zeros((H,), jnp.float32)
        Wih = jax.random.normal(ks[4], (MAX_SKIP, 4 * H, H), jnp.float32) * s
        Whh = jax.random.normal(ks[5], (MAX_SKIP, 4 * H, H), jnp.float32) * s
        bih = jax.random.normal(ks[6], (MAX_SKIP, 4 * H), jnp.float32) * s
        bhh = jax.random.normal(ks[7], (MAX_SKIP, 4 * H), jnp.float32) * s
        return dict(x=x, adj=adj, Wg0=Wg0, bg0=bg0, Wg1=Wg1, bg1=bg1, Wih=Wih, Whh=Whh, bih=bih, bhh=bhh)
    _L2_gnn_all = _L2_gnn_setup()
    _L2_gnn_in = {k: v for k, v in _L2_gnn_all.items() if k in ('Wg0', 'bg0', 'Wg1', 'bg1', 'Wih', 'Whh', 'bih', 'bhh')}
    del _L2_gnn_all

    def _L3_gnn_setup():
        import jax, jax.numpy as jnp
        import numpy as np
        EPS = 1e-05

        def _batchnorm(x, gamma, beta):
            mu = jnp.mean(x, axis=0)
            var = jnp.var(x, axis=0)
            return (x - mu) * jax.lax.rsqrt(var + EPS) * gamma + beta
        key = jax.random.key(seed)
        ks = jax.random.split(key, 4)
        b, n, d, h, o = (32, 1024, 128, 256, 128)
        features = jax.random.normal(ks[0], (b, n, d), dtype=jnp.float32)
        A = jax.random.uniform(ks[1], (n, n), dtype=jnp.float32)
        lim1 = float(np.sqrt(6.0 / (d + h)))
        W1 = jax.random.uniform(ks[2], (h, d), minval=-lim1, maxval=lim1, dtype=jnp.float32)
        b1 = jnp.zeros((h,), jnp.float32)
        lim2 = float(np.sqrt(6.0 / (h + o)))
        W2 = jax.random.uniform(ks[3], (o, h), minval=-lim2, maxval=lim2, dtype=jnp.float32)
        b2 = jnp.zeros((o,), jnp.float32)
        g1 = jnp.ones((h,), jnp.float32)
        be1 = jnp.zeros((h,), jnp.float32)
        g2 = jnp.ones((o,), jnp.float32)
        be2 = jnp.zeros((o,), jnp.float32)
        return {'features': features, 'A': A, 'W1': W1, 'b1': b1, 'g1': g1, 'be1': be1, 'W2': W2, 'b2': b2, 'g2': g2, 'be2': be2}
    _L3_gnn_all = _L3_gnn_setup()
    _L3_gnn_in = {k: v for k, v in _L3_gnn_all.items() if k in ('W1', 'b1', 'g1', 'be1', 'W2', 'b2', 'g2', 'be2')}
    del _L3_gnn_all
    return {'x': x, 'adj': adj, 'L0_gnn_W': _L0_gnn_in['W'], 'L1_gnn_W': _L1_gnn_in['W'], 'L1_gnn_a': _L1_gnn_in['a'], 'L2_gnn_Wg0': _L2_gnn_in['Wg0'], 'L2_gnn_bg0': _L2_gnn_in['bg0'], 'L2_gnn_Wg1': _L2_gnn_in['Wg1'], 'L2_gnn_bg1': _L2_gnn_in['bg1'], 'L2_gnn_Wih': _L2_gnn_in['Wih'], 'L2_gnn_Whh': _L2_gnn_in['Whh'], 'L2_gnn_bih': _L2_gnn_in['bih'], 'L2_gnn_bhh': _L2_gnn_in['bhh'], 'L3_gnn_W1': _L3_gnn_in['W1'], 'L3_gnn_b1': _L3_gnn_in['b1'], 'L3_gnn_g1': _L3_gnn_in['g1'], 'L3_gnn_be1': _L3_gnn_in['be1'], 'L3_gnn_W2': _L3_gnn_in['W2'], 'L3_gnn_b2': _L3_gnn_in['b2'], 'L3_gnn_g2': _L3_gnn_in['g2'], 'L3_gnn_be2': _L3_gnn_in['be2']}

def reference(x, adj, L0_gnn_W, L1_gnn_W, L1_gnn_a, L2_gnn_Wg0, L2_gnn_bg0, L2_gnn_Wg1, L2_gnn_bg1, L2_gnn_Wih, L2_gnn_Whh, L2_gnn_bih, L2_gnn_bhh, L3_gnn_W1, L3_gnn_b1, L3_gnn_g1, L3_gnn_be1, L3_gnn_W2, L3_gnn_b2, L3_gnn_g2, L3_gnn_be2):
    import jax
    import jax.numpy as jnp

    def _L0_gnn_ref(H, W, A):
        import jax, jax.numpy as jnp
        import numpy as np
        B, N, F_IN, F_OUT = (8, 2048, 128, 128)
        HW = jnp.einsum('bnf,fo->bno', H, W)
        A_norm = jax.nn.relu((A + A.T) * 0.5)
        D = jnp.sum(A_norm, axis=1)
        D_safe = jnp.where(D > 0, D, 1.0)
        d_inv_sqrt = jnp.where(D > 0, D_safe ** (-0.5), 0.0)
        DAD = d_inv_sqrt[:, None] * A_norm * d_inv_sqrt[None, :]
        L_norm = jnp.eye(N, dtype=H.dtype) - DAD
        out = jnp.einsum('nm,bmo->bno', L_norm, HW)
        return jax.nn.relu(out)

    def _L1_gnn_ref(h, adj_matrix, W, a):
        import jax, jax.numpy as jnp
        import numpy as np
        ALPHA = 0.2
        Fout = W.shape[1]
        Wh = jnp.einsum('bnf,fo->bno', h, W)
        a1, a2 = (a[:Fout, 0], a[Fout:, 0])
        s1 = Wh @ a1
        s2 = Wh @ a2
        e = s1[:, :, None] + s2[:, None, :]
        e = jnp.where(e >= 0, e, ALPHA * e)
        e = jnp.where(adj_matrix[None] == 0, -jnp.inf, e)
        attention = jax.nn.softmax(e, axis=-1)
        h_prime = jnp.einsum('bij,bjo->bio', attention, Wh)
        return h_prime

    def _L2_gnn_ref(x, adj, Wg0, bg0, Wg1, bg1, Wih, Whh, bih, bhh):
        import jax, jax.numpy as jnp
        import numpy as np
        B, T, D, H = (64, 1024, 128, 128)
        MAX_SKIP = 4

        def _lstm_last(Wih, Whh, bih, bhh, xs):
            N, _, Hd = xs.shape
            bias = bih + bhh

            def step(carry, x_t):
                h, c = carry
                g = x_t @ Wih.T + h @ Whh.T + bias
                i, f, gg, o = jnp.split(g, 4, axis=-1)
                c = jax.nn.sigmoid(f) * c + jax.nn.sigmoid(i) * jnp.tanh(gg)
                h = jax.nn.sigmoid(o) * jnp.tanh(c)
                return ((h, c), None)
            init = (jnp.zeros((N, Hd), xs.dtype), jnp.zeros((N, Hd), xs.dtype))
            (h_last, _), _ = jax.lax.scan(step, init, jnp.swapaxes(xs, 0, 1))
            return h_last
        h = jax.nn.relu(jnp.einsum('ts,bsh->bth', adj, x @ Wg0 + bg0))
        h = jax.nn.relu(jnp.einsum('ts,bsh->bth', adj, h @ Wg1 + bg1))
        Bv, Tv, Hd = h.shape
        for p in range(1, MAX_SKIP + 1):
            nw = Tv // p
            wins = h[:, :nw * p, :].reshape(Bv * nw, p, Hd)
            last = _lstm_last(Wih[p - 1], Whh[p - 1], bih[p - 1], bhh[p - 1], wins)
            idx = jnp.arange(nw) * p + (p - 1)
            h = h.at[:, idx, :].set(last.reshape(Bv, nw, Hd))
        return h

    def _L3_gnn_ref(features, A, W1, b1, g1, be1, W2, b2, g2, be2):
        import jax, jax.numpy as jnp
        import numpy as np
        EPS = 1e-05

        def _batchnorm(x, gamma, beta):
            mu = jnp.mean(x, axis=0)
            var = jnp.var(x, axis=0)
            return (x - mu) * jax.lax.rsqrt(var + EPS) * gamma + beta
        b, n, d = features.shape
        A_norm = A + jnp.eye(n, dtype=A.dtype)
        deg = jnp.sum(A_norm, axis=0) + jnp.sum(A_norm, axis=1) - jnp.diagonal(A_norm)
        dinv = jax.lax.rsqrt(deg)
        A_hat = A_norm * dinv[:, None] * dinv[None, :]
        agg = jnp.einsum('nm,bmd->bnd', A_hat, features)
        x = agg.reshape(-1, d)
        h = jax.nn.relu(_batchnorm(x @ W1.T + b1, g1, be1))
        out = h @ W2.T + b2
        out = _batchnorm(out, g2, be2)
        return out.reshape(b, n, -1)
    h = jnp.maximum(_layernorm(x, axis=-1), 0.0)
    x = x + _L0_gnn_ref(h, L0_gnn_W, adj)
    h = jnp.maximum(_layernorm(x, axis=-1), 0.0)
    x = x + _L1_gnn_ref(h, adj, L1_gnn_W, L1_gnn_a)
    h = jnp.maximum(_layernorm(x, axis=-1), 0.0)
    x = x + _L2_gnn_ref(h, adj, L2_gnn_Wg0, L2_gnn_bg0, L2_gnn_Wg1, L2_gnn_bg1, L2_gnn_Wih, L2_gnn_Whh, L2_gnn_bih, L2_gnn_bhh)
    h = jnp.maximum(_layernorm(x, axis=-1), 0.0)
    x = x + _L3_gnn_ref(h, adj, L3_gnn_W1, L3_gnn_b1, L3_gnn_g1, L3_gnn_be1, L3_gnn_W2, L3_gnn_b2, L3_gnn_g2, L3_gnn_be2)
    return x

_drawn_inputs = setup_inputs


def setup_inputs(seed=0):
    import zlib

    import numpy as np

    out = dict(_drawn_inputs(seed))
    spreads = {'L2_gnn_bg0': (0.0, 0.359),
     'L2_gnn_bg1': (0.0, 0.663),
     'L3_gnn_b1': (0.0, 0.8),
     'L3_gnn_g1': (1.0, 0.2),
     'L3_gnn_be1': (0.0, 0.1),
     'L3_gnn_b2': (0.0, 0.8),
     'L3_gnn_g2': (1.0, 0.2),
     'L3_gnn_be2': (0.0, 0.1)}
    factors = {'L2_gnn_Whh': 8.0, 'L2_gnn_bih': 3.064, 'L2_gnn_bhh': 3.108}
    for name, (base, spread) in spreads.items():
        noise = np.random.default_rng([zlib.crc32(name.encode()), seed]).standard_normal(out[name].shape)
        drawn = base * np.exp(spread * noise) if base else spread * noise
        out[name] = jnp.asarray(drawn.astype(out[name].dtype))
    for name, factor in factors.items():
        out[name] = (out[name] * factor).astype(out[name].dtype)
    return out
```

```python
import concourse.bass as bass
from concourse import mybir
from contextlib import ExitStack

F32 = mybir.dt.float32
F32R = mybir.dt.float32r
U8 = mybir.dt.uint8
ALU = mybir.AluOpType
ACT = mybir.ActivationFunctionType
AX = mybir.AxisListType

P = 128
B, N, D = 8, 2048, 128
T = N // P
W = B * D
EPS = 1e-5
ALPHA = 0.2
HID = 256
SKIP = 4
HALF = T // 2


class Tile:

    def __init__(self, off, i=None):
        self.off, self.i = off, i

    @property
    def n(self):
        return self.off if self.i is None else self.i * 2 + self.off

    @property
    def pair(self):
        return self.off // 2 if self.i is None else self.i + self.off // 2

    @property
    def par(self):
        return self.off % 2

    def __add__(self, k):
        return Tile(self.off + k, self.i)

    def __sub__(self, k):
        return Tile(self.off - k, self.i)

    def within(self, lo, hi):
        return self.i is not None or lo <= self.off < hi


def run_slots(eng, slot, n, head=2, tail=3):
    for t in range(head):
        slot(Tile(t))
    with eng.Fori(head // 2, (n - tail) // 2) as i:
        slot(Tile(0, i))
        slot(Tile(1, i))
    for t in range(n - tail, n):
        slot(Tile(t))


class Chain:

    def __init__(self, eng, sem, links):
        self.eng, self.sem, self.links = eng, sem, links

    def step(self, t):
        self.base, self.k = t * self.links, 0

    def link(self, ins):
        self.k += 1
        assert self.k <= self.links
        ins.then_inc(self.sem, 1)
        self.eng.wait_ge(self.sem, self.base + self.k)


def over(col, width):
    return col.unsqueeze(2).to_broadcast([col.shape[0], col.shape[1], width])


class Program:
    def __init__(self, nc, ctx):
        self.nc, self.ctx, self.live = nc, ctx, []

    def sem(self, name):
        self.live.append(self.nc.alloc_semaphore(name))
        return self.live[-1]

    def retire(self):
        with self.nc.Block() as block:
            @block.gpsimd
            def _(pool):
                for sem in self.live:
                    pool.sem_clear(sem)
        for sem in self.live:
            self.nc.release_semaphore(sem)
        self.live = []

    def sems(self, name, n=2):
        return [self.sem(f"{name}{k}") for k in range(n)]

    def sb(self, ctx, name, shape, dt=F32):
        return ctx.enter_context(self.nc.sbuf_tensor(name, shape, dt))

    def ps(self, ctx, name, shape):
        return ctx.enter_context(self.nc.psum_tensor(name, shape, F32))


class LayerNorm:

    LINKS = 3

    def __init__(self, prog, ctx, name, blocks):
        self.blocks = blocks
        self.stat = prog.sb(ctx, f"{name}_stat", [P, 4, blocks])
        self.half = prog.sb(ctx, f"{name}_half", [P, blocks])
        self.sq = prog.sb(ctx, f"{name}_sq", [P, blocks, D])
        self.own = prog.sem(f"{name}_own")
        self.centred = prog.sem(f"{name}_centred")
        self.squared = prog.sem(f"{name}_squared")
        self.variance = prog.sem(f"{name}_variance")
        self.rstd = prog.sem(f"{name}_rstd")
        self.half_set = prog.sem(f"{name}_half_set")

    def vector(self, dve, t, x, out, done):
        k = self.blocks
        chain = Chain(dve, self.own, self.LINKS)
        chain.step(t)
        total, mean, var, rstd = (self.stat[:, j, :] for j in range(4))
        chain.link(dve.tensor_reduce(total, x, AX.X, ALU.add))
        chain.link(dve.tensor_scalar(mean, total, 1.0 / D, None, ALU.mult))
        dve.tensor_tensor(out, x, over(mean, D), ALU.subtract).then_inc(self.centred, 1)
        dve.wait_ge(self.squared, t + 1)
        chain.link(dve.tensor_reduce(total, self.sq[:, :, :], AX.X, ALU.add))
        dve.tensor_scalar(var, total, 1.0 / D, EPS, ALU.mult, ALU.add).then_inc(self.variance, 1)
        dve.wait_ge(self.rstd, t + 1)
        dve.scalar_tensor_tensor(out, out, 0.0, over(rstd, D), ALU.max, ALU.mult).then_inc(done, 1)

    def scalar(self, act, t, out):
        act.wait_ge(self.centred, t + 1)
        act.activation(self.sq[:, :, :], out, ACT.Square).then_inc(self.squared, 1)

    def pool_setup(self, pool):
        pool.memset(self.half[:, :], -0.5).then_inc(self.half_set, 1)
        pool.wait_ge(self.half_set, 1)

    def pool(self, pool, t):
        pool.wait_ge(self.variance, t + 1)
        pool.tensor_tensor(self.stat[:, 3, :], self.stat[:, 2, :], self.half[:, :],
                           ALU.pow).then_inc(self.rstd, 1)


def prepare(prog, io, keep, x, adj, a_col, wc_t):
    nc = prog.nc
    x_tiles = x.rearrange("b (t p) f -> t p b f", p=P)
    with ExitStack() as ctx:
        a_sb = prog.sb(ctx, "a_sb", [P, T, N])
        ident = keep["ident"]
        a_loaded = prog.sem("a_loaded")
        w_loaded = prog.sem("w_loaded")

        with ExitStack() as c1:
            xt = prog.sb(c1, "p_xt", [P, 2, B, D])
            ht = prog.sb(c1, "p_ht", [P, 2, B, D])
            ln = LayerNorm(prog, c1, "pln", B)
            x_in, h_out = prog.sems("px_in"), prog.sems("ph_out")
            ln_done = prog.sem("pln_done")
            id_set = prog.sem("id_set")
            acol = prog.sb(c1, "acol", [P, 2])
            wct = prog.sb(c1, "wct", [P, D])
            spread = prog.sb(c1, "spread", [P, 2, P])
            pw = prog.ps(c1, "p_wa", [P, 2, D])
            wa_in, wa_spread, wa_summed = (prog.sem(k) for k in ("wa_in", "wa_spread", "wa_summed"))
            block = c1.enter_context(nc.Block())

            @block.tensor
            def _(pe):
                pe.wait_ge(wa_spread, 2)
                for k in range(2):
                    pe.matmul(pw[:, k], spread[:, k], wct[:, :], start=True, stop=True).then_inc(wa_summed, 1)

            @block.sync
            def _(sp):
                sp.dma_start(acol[:, :], a_col).then_inc(wa_in, 16)
                sp.dma_start(wct[:, :], wc_t).then_inc(wa_in, 16)

                def slot(t):
                    if t.within(0, T):
                        if t.within(2, T):
                            sp.wait_ge(ln_done, t.n - 1)
                        sp.dma_start(xt[:, t.par], x_tiles[t.n]).then_inc(x_in[t.par], 16)
                    if t.within(1, T + 1):
                        u = t - 1
                        sp.wait_ge(ln_done, u.n + 1)
                        sp.dma_start(io["h0"][u.n], ht[:, u.par]).then_inc(h_out[u.par], 16)
                run_slots(sp, slot, T + 1)
                for s in h_out:
                    sp.wait_ge(s, 16 * HALF)

            @block.scalar
            def _(act):
                for t in range(T):
                    act.dma_start(a_sb[:, t], adj[t * P:(t + 1) * P, :]).then_inc(a_loaded, 16)

                def slot(t):
                    ln.scalar(act, t.n, ht[:, t.par])
                run_slots(act, slot, T, 2, 2)

            @block.gpsimd
            def _(pool):
                pool.memset(ident[:, :], 0.0).then_inc(id_set, 1)
                pool.memset(keep["ones"][:, :], 1.0).then_inc(id_set, 1)
                pool.wait_ge(id_set, 2)
                pool.affine_select(out=ident[:, :], in_=ident[:, :], compare_op=ALU.not_equal, fill=1.0,
                                   base=0, pattern=[[-1, P]], channel_multiplier=1).then_inc(id_set, 1)
                ln.pool_setup(pool)

                def slot(t):
                    ln.pool(pool, t.n)
                run_slots(pool, slot, T, 2, 2)

            @block.vector
            def _(dve):
                def slot(t):
                    if t.within(2, T):
                        dve.wait_ge(h_out[t.par], t.pair * 16)
                    dve.wait_ge(x_in[t.par], t.pair * 16 + 16)
                    ln.vector(dve, t.n, xt[:, t.par], ht[:, t.par], ln_done)
                dve.wait_ge(id_set, 2)
                dve.wait_ge(wa_in, 32)
                for k in range(2):
                    dve.tensor_scalar(spread[:, k], keep["ones"][:, 0:1].to_broadcast([P, P]), acol[:, k:k + 1],
                                      None, ALU.mult).then_inc(wa_spread, 1)
                run_slots(dve, slot, T, 2, 2)
                dve.wait_ge(wa_summed, 2)
                dve.tensor_copy(keep["wa"][:, :, :], pw[:, :, :])

        with ExitStack() as c2:
            stage = prog.sb(c2, "stage", [P, 2, T, P])
            at = prog.sb(c2, "at", [P, 2, T, P])
            an = prog.sb(c2, "an", [P, T, P])
            mr = prog.sb(c2, "mr", [P, T, P], U8)
            mt = prog.sb(c2, "mt", [P, T, P], U8)
            sums = prog.sb(c2, "sums", [P, 4, T])
            small = prog.sb(c2, "small", [P, 4, T])
            pt = prog.ps(c2, "p_pt", [P, 2, HALF, P])
            pst = prog.ps(c2, "p_sum", [P, 2, 512])
            staged = prog.sem("staged")
            turned = prog.sem("turned")
            copied = prog.sem("copied")
            added = prog.sem("added")
            normed = prog.sem("normed")
            masked = prog.sem("masked")
            summed = prog.sem("summed")
            read = prog.sem("columns_summed")
            reduced = prog.sem("reduced")
            sums_read = prog.sem("sums_read")
            an_out = prog.sem("an_out")
            at_out = prog.sems("at_out")
            mask_out = prog.sem("mask_out")
            own = prog.sem("p_own")
            powered = prog.sem("powered")
            ready = prog.sem("deg_ready")
            rs_turned, rs_copied, rs_out = prog.sem("rs_turned"), prog.sem("rs_copied"), prog.sem("rs_out")
            block = c2.enter_context(nc.Block())

            @block.sync
            def _(sp):
                def slot(t):
                    sp.wait_ge(copied, t.n * 2 + 2)
                    sp.dma_start(io["adjT"][t.n], at[:, t.par]).then_inc(at_out[t.par], 16)
                    sp.wait_ge(masked, t.n + 1)
                    sp.dma_start(io["mrow"][t.n], mr[:, :, :]).then_inc(mask_out, 16)
                    sp.dma_start(io["mT"][t.n], mt[:, :, :]).then_inc(mask_out, 16)
                    sp.wait_ge(normed, t.n + 1)
                    sp.dma_start(io["anorm"][t.n], an[:, :, :]).then_inc(an_out, 16)
                run_slots(sp, slot, T, 2, 2)
                sp.wait_ge(rs_copied, 1)
                sp.dma_start(io["rsrow"], keep["rsT"][0:T, :]).then_inc(rs_out, 16)
                for s in at_out:
                    sp.wait_ge(s, 16 * HALF)
                sp.wait_ge(mask_out, 32 * T)
                sp.wait_ge(an_out, 16 * T)
                sp.wait_ge(rs_out, 16)

            @block.scalar
            def _(act):
                def slot(t):
                    if t.within(0, T):
                        if t.within(2, T):
                            act.wait_ge(turned, t.n * 2 - 2)
                            act.wait_ge(masked, t.n - 1)
                        act.wait_ge(a_loaded, 16 * T)
                        act.activation(stage[:, t.par].rearrange("p c j -> p (c j)"), a_sb[:, t.n],
                                       ACT.Copy).then_inc(staged, 1)
                    if t.within(1, T + 1):
                        u = t - 1
                        if u.within(2, T):
                            act.wait_ge(at_out[u.par], u.pair * 16)
                            act.wait_ge(summed, u.n - 1)
                            act.wait_ge(read, u.n - 1)
                        for h in range(2):
                            act.wait_ge(turned, u.n * 2 + h + 1)
                            act.activation(at[:, u.par, h * HALF:(h + 1) * HALF], pt[:, h],
                                           ACT.Copy).then_inc(copied, 1)
                run_slots(act, slot, T + 1)
                act.wait_ge(rs_turned, 1)
                act.activation(keep["rsT"][0:T, :], pst[0:T, 0, 0:P], ACT.Copy).then_inc(rs_copied, 1)

            @block.vector
            def _(dve):
                sym, row, col, dia = (sums[:, j] for j in range(4))
                chain = Chain(dve, own, 1)
                chain.step(0)
                chain.link(dve.memset(sums[:, :, :], 0.0))

                def slot(t):
                    if t.within(0, T):
                        dve.wait_ge(copied, t.n * 2 + 2)
                        if t.within(1, T):
                            dve.wait_ge(an_out, t.n * 16)
                            dve.wait_ge(summed, t.n)
                        dve.tensor_tensor(an[:, :, :], at[:, t.par], a_sb[:, :, bass.ts(t.n, P)],
                                          ALU.add).then_inc(added, 1)
                        dve.wait_ge(added, t.n + 1)
                        dve.tensor_scalar(an[:, :, :], an[:, :, :], 0.5, 0.0, ALU.mult,
                                          ALU.max).then_inc(normed, 1)
                        if t.within(1, T):
                            dve.wait_ge(mask_out, t.n * 32)
                        dve.tensor_scalar(mt[:, :, :], at[:, t.par], 0.0, None, ALU.not_equal)
                        dve.tensor_scalar(mr[:, :, :], stage[:, t.par], 0.0, None,
                                          ALU.not_equal).then_inc(masked, 1)
                        if t.within(1, T):
                            dve.wait_ge(read, t.n)
                        dve.tensor_reduce(small[:, 0], at[:, t.par], AX.X, ALU.add).then_inc(reduced, 1)
                        dve.wait_ge(reduced, t.n + 1)
                        dve.tensor_tensor(col, col, small[:, 0], ALU.add).then_inc(read, 1)
                    if t.within(1, T + 1):
                        u = t - 1
                        dve.wait_ge(summed, u.n + 1)
                        dve.tensor_scalar(sums[:, 0, bass.ds(u.n, 1)], pst[:, u.par, 0:1], 1.0, None, ALU.mult)
                        dve.tensor_scalar(sums[:, 1, bass.ds(u.n, 1)], pst[:, u.par, 1:2], 1.0, None,
                                          ALU.mult).then_inc(sums_read, 1)
                run_slots(dve, slot, T + 1)
                dve.wait_ge(an_out, 16 * T)
                for t in range(T):
                    last = dve.tensor_tensor(an[:, t, :], a_sb[:, t, t * P:(t + 1) * P], ident[:, :], ALU.mult)
                last.then_inc(ready, 1)
                dve.wait_ge(ready, 1)
                dve.tensor_reduce(dia, an[:, :, :], AX.X, ALU.add).then_inc(ready, 1)
                dve.wait_ge(read, T)
                dve.wait_ge(sums_read, T)
                dve.tensor_copy(keep["rs"][:, :], row)
                positive, safe, deg = small[:, 0], small[:, 1], small[:, 2]
                dve.tensor_scalar(positive, sym, 0.0, None, ALU.is_gt).then_inc(ready, 1)
                dve.wait_ge(ready, 3)
                dve.tensor_scalar(safe, positive, -1.0, 1.0, ALU.mult, ALU.add).then_inc(ready, 1)
                dve.tensor_tensor(small[:, 3], sym, positive, ALU.mult).then_inc(ready, 1)
                dve.wait_ge(ready, 5)
                dve.tensor_tensor(safe, safe, small[:, 3], ALU.add).then_inc(ready, 1)
                dve.scalar_tensor_tensor(deg, row, 1.0, col, ALU.add, ALU.add).then_inc(ready, 1)
                dve.wait_ge(ready, 7)
                dve.tensor_tensor(deg, deg, dia, ALU.subtract).then_inc(ready, 1)
                dve.wait_ge(powered, 3)
                dve.tensor_tensor(keep["dinv"][:, :], small[:, 3], positive, ALU.mult).then_inc(ready, 1)
                dve.wait_ge(ready, 9)
                dve.tensor_scalar(keep["ndinv"][:, :], keep["dinv"][:, :], -1.0, None, ALU.mult)

            @block.gpsimd
            def _(pool):
                pool.memset(keep["halves"][:, :], -0.5).then_inc(powered, 1)
                pool.wait_ge(powered, 1)
                pool.wait_ge(ready, 8)
                pool.tensor_tensor(small[:, 3], small[:, 1], keep["halves"][:, :], ALU.pow).then_inc(powered, 1)
                pool.tensor_tensor(keep["dinv3"][:, :], small[:, 2], keep["halves"][:, :],
                                   ALU.pow).then_inc(powered, 1)

            @block.tensor
            def _(pe):
                def slot(t):
                    if t.within(0, T):
                        pe.wait_ge(staged, t.n + 1)
                        for h in range(2):
                            if t.within(1, T):
                                pe.wait_ge(copied, t.n * 2 + h - 1)
                            for c in range(HALF):
                                last = pe.transpose(pt[:, h, c], stage[:, t.par, h * HALF + c], ident[:, :])
                            last.then_inc(turned, 1)
                    if t.within(1, T + 1):
                        u = t - 1
                        if u.within(2, T):
                            pe.wait_ge(sums_read, u.n - 1)
                        pe.wait_ge(normed, u.n + 1)
                        for c in range(T):
                            pe.matmul(pst[:, u.par, 0:1], an[:, c], keep["ones"][:, 0:1],
                                      start=(c == 0), stop=(c == T - 1))
                        for c in range(T):
                            last = pe.matmul(pst[:, u.par, 1:2], at[:, u.par, c], keep["ones"][:, 0:1],
                                             start=(c == 0), stop=(c == T - 1))
                        last.then_inc(summed, 1)
                run_slots(pe, slot, T + 1)
                pe.wait_ge(sums_read, T)
                pe.transpose(pst[0:T, 0, 0:P], sums[:, 1], ident[:, :]).then_inc(rs_turned, 1)


def product(prog, io, keep, name, adj_d, h_in, weights, kind, x_in_d=None):
    nc = prog.nc
    scale = {"L0": keep["dinv"], "L3": keep["dinv3"]}.get(kind)
    uses_h = kind in ("L0", "L3")
    uses_x = kind == "L0"
    with ExitStack() as ctx:
        n_ = lambda s: f"{name}_{s}"
        g_hi = prog.sb(ctx, n_("g_hi"), [P, T, W], F32R)
        g_lo = prog.sb(ctx, n_("g_lo"), [P, T, W], F32R)
        a_raw = prog.sb(ctx, n_("a_raw"), [P, T, P])
        a_hi = prog.sb(ctx, n_("a_hi"), [P, 2, T, P], F32R)
        a_lo = prog.sb(ctx, n_("a_lo"), [P, 2, T, P], F32R)
        v = prog.sb(ctx, n_("v"), [P, B, D])
        ut = prog.sb(ctx, n_("ut"), [P, B, P])
        ht = prog.sb(ctx, n_("ht"), [P, 2, B, D])
        xt = prog.sb(ctx, n_("xt"), [P, 2, B, D]) if uses_x else None
        hn = prog.sb(ctx, n_("hn"), [P, B, D]) if kind != "L3" else None
        wsb = prog.sb(ctx, n_("w"), [P, weights["w"].shape[1]])
        acc = prog.ps(ctx, n_("acc"), [P, 2, W])
        pt = prog.ps(ctx, n_("pt"), [P, B, P])
        po = prog.ps(ctx, n_("po"), [P, B, D])
        ln = LayerNorm(prog, ctx, n_("ln"), B) if uses_x else None
        ident = keep["ident"]

        w_in = prog.sem(n_("w_in"))
        g_in = prog.sems(n_("g_in"))
        g_high = prog.sem(n_("g_high"))
        g_low = prog.sem(n_("g_low"))
        a_in = prog.sem(n_("a_in"))
        a_high = prog.sem(n_("a_high"))
        a_low = prog.sem(n_("a_low"))
        h_in_s = prog.sems(n_("h_in"))
        x_in_s = prog.sems(n_("x_in")) if uses_x else None
        multiplied = prog.sem(n_("multiplied"))
        evacuated = prog.sem(n_("evacuated"))
        turned = prog.sem(n_("turned"))
        ut_ready = prog.sem(n_("ut_ready"))
        projected = prog.sem(n_("projected"))
        po_read = prog.sem(n_("po_read"))
        x_done = prog.sem(n_("x_done"))
        h_done = prog.sem(n_("h_done"))
        x_out = prog.sems(n_("x_out"))
        h_out = prog.sem(n_("h_out"))
        own = prog.sem(n_("own"))
        own2 = prog.sem(n_("own2"))
        halves = 2 if kind == "L3" else 1
        extra = {}
        n_w = 1
        if kind == "L0":
            extra["wa"] = keep["wa"]
        if kind == "L2a":
            extra["brow"] = prog.sb(ctx, n_("brow"), [P, D])
            n_w = 2
        if kind == "L2b":
            extra["bcol"] = prog.sb(ctx, n_("bcol"), [P, 1])
            extra["rsrow"] = prog.sb(ctx, n_("rsrow"), [P, N])
            n_w = 3
        small = prog.sb(ctx, n_("small"), [P, 2, B])
        block = ctx.enter_context(nc.Block())

        @block.sync
        def _(sp):
            sp.dma_start(a_raw[:, :, :], adj_d[0]).then_inc(a_in, 16)
            for s in range(T):
                if s >= 2:
                    sp.wait_ge(g_low, s - 1)
                sp.dma_start(ht[:, s % 2], h_in[s]).then_inc(g_in[s % 2], 16)
                if s == 1:
                    sp.dma_start(wsb[:, :], weights["w"]).then_inc(w_in, 16)
                    if kind == "L2a":
                        sp.dma_start(extra["brow"][:, :], weights["b"].partition_broadcast(P)).then_inc(w_in, 16)
                    if kind == "L2b":
                        sp.dma_start(extra["bcol"][:, :], weights["b"]).then_inc(w_in, 16)
                        sp.dma_start(extra["rsrow"][:, :],
                                     io["rsrow"].rearrange("t j -> (t j)").partition_broadcast(P)).then_inc(w_in, 16)

            def slot(t):
                if t.within(0, T - 1):
                    sp.wait_ge(a_high, t.n + 1)
                    sp.wait_ge(a_low, t.n + 1)
                    sp.dma_start(a_raw[:, :, :], adj_d[t.n + 1]).then_inc(a_in, 16)
                if t.within(0, T):
                    if uses_h:
                        if t.within(2, T):
                            sp.wait_ge(evacuated, t.n - 1)
                        else:
                            sp.wait_ge(g_low, T)
                        sp.dma_start(ht[:, t.par], h_in[t.n]).then_inc(h_in_s[t.par], 16)
                    if uses_x:
                        if t.within(2, T):
                            sp.wait_ge(x_out[t.par], t.pair * 16)
                            sp.wait_ge(h_done, t.n - 1)
                        sp.dma_start(xt[:, t.par], x_in_d[t.n]).then_inc(x_in_s[t.par], 16)
                if t.within(1, T + 1):
                    u = t - 1
                    if uses_x:
                        sp.wait_ge(x_done, u.n + 1)
                        sp.dma_start(io["x1"][u.n], xt[:, u.par]).then_inc(x_out[u.par], 16)
                    if kind in ("L0", "L2a"):
                        sp.wait_ge(h_done, u.n + 1)
                        sp.dma_start(io["h1" if kind == "L0" else "h2b"][u.n], hn[:, :, :]).then_inc(h_out, 16)
                    if kind == "L2b":
                        sp.wait_ge(h_done, u.n + 1)
                        sp.dma_start(io["hT"].rearrange("b f (t j) -> t f b j", j=P)[u.n],
                                     hn[:, :, :]).then_inc(h_out, 16)
                    if kind == "L3":
                        sp.wait_ge(ut_ready, u.n + 1)
                        sp.dma_start(io["aggT"][u.n], ut[:, :, :]).then_inc(h_out, 16)
            run_slots(sp, slot, T + 1)
            if uses_x:
                for s in x_out:
                    sp.wait_ge(s, 16 * HALF)
            sp.wait_ge(h_out, 16 * T)

        @block.scalar
        def _(act):
            def split(t):
                if t.within(2, T):
                    act.wait_ge(multiplied, t.n - 1)
                act.wait_ge(a_in, t.n * 16 + 16)
                act.activation(a_hi[:, t.par], a_raw[:, :, :], ACT.Copy).then_inc(a_high, 1)

            split(Tile(0))
            for s in range(T):
                act.wait_ge(g_in[s % 2], 16 * (s // 2 + 1))
                sc = 1.0 if scale is None else scale[:, s:s + 1]
                act.activation(g_hi[:, s], ht[:, s % 2].rearrange("p b f -> p (b f)"), ACT.Copy,
                               scale=sc).then_inc(g_high, 1)

            def slot(t):
                if t.within(0, T - 1):
                    split(t + 1)
                if t.within(1, T + 1):
                    u = t - 1
                    act.wait_ge(turned, u.n + 1)
                    if u.within(1, T):
                        act.wait_ge(projected, u.n * halves)
                        if kind == "L3":
                            act.wait_ge(h_out, u.n * 16)
                    act.activation(ut[:, :, :], pt[:, :, :], ACT.Copy).then_inc(ut_ready, 1)
                    if uses_x:
                        ln.scalar(act, u.n, hn[:, :, :])
            run_slots(act, slot, T + 1)

        if uses_x:
            @block.gpsimd
            def _(pool):
                ln.pool_setup(pool)
                run_slots(pool, lambda t: ln.pool(pool, t.n), T, 2, 2)

        @block.vector
        def _(dve):
            links = Chain(dve, own, {"L0": 4, "L2a": 1, "L2b": 1, "L3": 0}[kind])
            evac_link = Chain(dve, own2, 1)

            def split(t):
                if t.within(2, T):
                    dve.wait_ge(multiplied, t.n - 1)
                dve.wait_ge(a_high, t.n + 1)
                dve.tensor_tensor(a_lo[:, t.par], a_raw[:, :, :], a_hi[:, t.par].bitcast(F32),
                                  ALU.subtract).then_inc(a_low, 1)

            split(Tile(0))
            for s in range(T):
                dve.wait_ge(g_high, s + 1)
                h2 = ht[:, s % 2].rearrange("p b f -> p (b f)")
                if scale is None:
                    dve.tensor_tensor(g_lo[:, s], h2, g_hi[:, s].bitcast(F32), ALU.subtract).then_inc(g_low, 1)
                else:
                    dve.scalar_tensor_tensor(g_lo[:, s], h2, scale[:, s:s + 1], g_hi[:, s].bitcast(F32),
                                             ALU.mult, ALU.subtract).then_inc(g_low, 1)
            dve.wait_ge(w_in, 16 * n_w)

            def evacuate(u):
                a2 = acc[:, u.par].rearrange("p (b f) -> p b f", f=D)
                if u.within(1, T):
                    dve.wait_ge(turned, u.n)
                if uses_h:
                    dve.wait_ge(h_in_s[u.par], u.pair * 16 + 16)
                dve.wait_ge(multiplied, u.n + 1)
                if kind == "L0":
                    dve.scalar_tensor_tensor(v[:, :, :], a2, keep["ndinv"][:, bass.ds(u.n, 1)], ht[:, u.par],
                                             ALU.mult, ALU.add).then_inc(evacuated, 1)
                elif kind == "L3":
                    evac_link.step(u.n)
                    evac_link.link(dve.scalar_tensor_tensor(
                        v[:, :, :], ht[:, u.par], keep["dinv3"][:, bass.ds(u.n, 1)], a2, ALU.mult, ALU.add))
                    dve.tensor_scalar(v[:, :, :], v[:, :, :], keep["dinv3"][:, bass.ds(u.n, 1)], None,
                                      ALU.mult).then_inc(evacuated, 1)
                else:
                    dve.tensor_copy(v[:, :, :], a2).then_inc(evacuated, 1)

            def tail(u):
                links.step(u.n)
                if kind == "L0":
                    dve.wait_ge(x_in_s[u.par], u.pair * 16 + 16)
                    dve.wait_ge(projected, u.n + 1)
                    dve.scalar_tensor_tensor(xt[:, u.par], po[:, :, :], 0.0, xt[:, u.par],
                                             ALU.max, ALU.add).then_inc(x_done, 1)
                    if u.within(1, T):
                        dve.wait_ge(h_out, u.n * 16)
                    dve.wait_ge(x_done, u.n + 1)
                    ln.vector(dve, u.n, xt[:, u.par], hn[:, :, :], h_done)
                    dve.wait_ge(h_done, u.n + 1)
                    for j, col in ((0, keep["s1"]), (1, keep["s2"])):
                        wa = extra["wa"][:, j].unsqueeze(1).to_broadcast([P, B, D])
                        links.link(dve.tensor_tensor(ln.sq[:, :, :], hn[:, :, :], wa, ALU.mult))
                        links.link(dve.tensor_reduce(small[:, j, :], ln.sq[:, :, :], AX.X, ALU.add))
                        dve.tensor_scalar(col[:, :, bass.ds(u.n, 1)], small[:, j, :].unsqueeze(2), 1.0, None,
                                          ALU.mult)
                if kind in ("L2a", "L2b"):
                    dve.wait_ge(projected, u.n + 1)
                    if u.within(1, T):
                        dve.wait_ge(h_out, u.n * 16)
                    if kind == "L2a":
                        bias = extra["brow"][:, :].unsqueeze(1).to_broadcast([P, B, D])
                        s = keep["rs"][:, bass.ds(u.n, 1)]
                    else:
                        bias = extra["rsrow"][:, bass.ts(u.n, P)].unsqueeze(1).to_broadcast([P, B, P])
                        s = extra["bcol"][:, 0:1]
                    links.link(dve.scalar_tensor_tensor(hn[:, :, :], bias, s, po[:, :, :], ALU.mult, ALU.add))
                    dve.tensor_scalar(hn[:, :, :], hn[:, :, :], 0.0, None, ALU.max).then_inc(h_done, 1)
                if kind == "L3":
                    for k in range(2):
                        dve.wait_ge(projected, u.n * 2 + k + 1)
                        for c in range(2):
                            last = dve.bn_stats(keep["bn1"][:, k, bass.ds(u.n * 2 + c, 1), :].squeeze(1),
                                                po[:, 4 * c:4 * c + 4, :].rearrange("p b f -> p (b f)"))
                        last.then_inc(po_read, 1)

            def slot(t):
                if t.within(1, T + 1):
                    evacuate(t - 1)
                if t.within(0, T - 1):
                    split(t + 1)
                if t.within(1, T + 1):
                    tail(t - 1)
            run_slots(dve, slot, T + 1)

        @block.tensor
        def _(pe):
            pe.wait_ge(w_in, 16 * n_w)

            def main(t, s0, s1):
                if s0 == 0:
                    if t.within(2, T):
                        pe.wait_ge(evacuated, t.n - 1)
                    pe.wait_ge(a_low, t.n + 1)
                for s in range(s0, s1):
                    if t.i is None and t.off == 0:
                        pe.wait_ge(g_low, s + 1)
                    for lhs, rhs in ((a_hi, g_hi), (a_hi, g_lo), (a_lo, g_hi)):
                        for c in range(2):
                            last = pe.matmul(acc[:, t.par, c * 512:(c + 1) * 512], lhs[:, t.par, s],
                                             rhs[:, s, c * 512:(c + 1) * 512],
                                             start=(s == 0 and lhs is a_hi and rhs is g_hi),
                                             stop=(s == T - 1 and lhs is a_lo))
                if s1 == T:
                    last.then_inc(multiplied, 1)

            def turn(u):
                pe.wait_ge(evacuated, u.n + 1)
                if u.within(1, T):
                    pe.wait_ge(ut_ready, u.n)
                for b in range(B):
                    last = pe.transpose(pt[:, b], v[:, b], ident[:, :])
                last.then_inc(turned, 1)

            def project(u, k):
                pe.wait_ge(ut_ready, u.n + 1)
                if kind == "L3":
                    if k == 1 or u.within(1, T):
                        pe.wait_ge(po_read, u.n * 2 + k)
                elif u.within(1, T):
                    pe.wait_ge(x_done if kind == "L0" else h_done, u.n)
                if kind in ("L0", "L2a"):
                    for b in range(B):
                        last = pe.matmul(po[:, b], ut[:, b], wsb[:, :], start=True, stop=True)
                else:
                    for c in range(2):
                        last = pe.matmul(po[:, 4 * c:4 * c + 4], wsb[:, k * P:(k + 1) * P],
                                         ut[:, 4 * c:4 * c + 4], start=True, stop=True)
                last.then_inc(projected, 1)

            def slot(t):
                pieces = [(0, 5), (5, 11), (11, T)]
                for j, (s0, s1) in enumerate(pieces):
                    if t.within(0, T):
                        main(t, s0, s1)
                    if t.within(1, T + 1):
                        if j == 0:
                            turn(t - 1)
                        elif j - 1 < halves:
                            project(t - 1, j - 1)
            run_slots(pe, slot, T + 1)


def attention(prog, io, keep, weights):
    nc = prog.nc
    BANK = 3
    NBANK = -(-T // BANK)
    batch_view = lambda d: d.rearrange("t p b f -> b p t f")
    with ExitStack() as ctx:
        mrow = prog.sb(ctx, "c_mrow", [P, T, N], U8)
        mT = prog.sb(ctx, "c_mT", [P, T, T, P], U8)
        hb = prog.sb(ctx, "c_hb", [P, T, D + 1])
        s2row = prog.sb(ctx, "c_s2row", [P, N])
        rows = prog.sb(ctx, "c_rows", [P, 2, N])
        z = prog.sb(ctx, "c_z", [P, 2, N])
        e = prog.sb(ctx, "c_e", [P, 2, N])
        pr = prog.sb(ctx, "c_p", [P, 2, N])
        u = prog.sb(ctx, "c_u", [P, T, D])
        ut = prog.sb(ctx, "c_ut", [P, 4, P])
        xt = prog.sb(ctx, "c_xt", [P, T, D])
        hn = prog.sb(ctx, "c_hn", [P, HALF, D])
        wsb = prog.sb(ctx, "c_w", [P, D])
        cols = prog.sb(ctx, "c_cols", [P, 8, T])
        rcol = prog.sb(ctx, "c_rcol", [P, 2, T])
        rT = prog.sb(ctx, "c_rT", [2 * T, P])
        s2T = prog.sb(ctx, "c_s2T", [P, P])
        rec = prog.sb(ctx, "c_rec", [P, NBANK * BANK])
        acc = prog.ps(ctx, "c_acc", [P, NBANK, 512])
        pq = prog.ps(ctx, "c_pq", [P, 2, 512])
        ln = LayerNorm(prog, ctx, "cln", HALF)
        ident = keep["ident"]
        sem = lambda s: prog.sem(f"c_{s}")
        w_in, m_in = sem("w_in"), sem("m_in")
        s2_turned, s2_copied, s2_out = sem("s2_turned"), sem("s2_copied"), sem("s2_out")
        h_in, ones_set, row_in = sem("h_in"), sem("ones_set"), sem("row_in")
        max_own, maxed, r_ready = sem("max_own"), sem("maxed"), sem("r_ready")
        r_turned, r_copied, r_out, r_in = sem("r_turned"), sem("r_copied"), sem("r_out"), sem("r_in")
        z_ready, exped, masked, used = sem("z_ready"), sem("exped"), sem("masked"), sem("used")
        cols_ready = sem("cols_ready")
        rec_own, normed = sem("rec_own"), sem("normed")
        u_turned, ut_ready, projected = sem("u_turned"), sem("ut_ready"), sem("projected")
        x_in, x_done, x_out = sem("x_in"), sem("x_done"), sem("x_out")
        h_done, h_out = sem("h_done"), sem("h_out")
        block = ctx.enter_context(nc.Block())

        def bank(tile):
            return tile // BANK, (tile % BANK) * (D + 1)

        def batches(eng, slot):
            slot(0, True, False)
            slot(1, False, False)
            with eng.Fori(2, B) as b:
                slot(b, False, False)
            slot(B, False, True)

        @block.sync
        def _(sp):
            sp.dma_start(wsb[:, :], weights).then_inc(w_in, 16)
            sp.wait_ge(s2_copied, 1)
            sp.dma_start(io["s2row"].rearrange("(b t) j -> (b t) j", b=B), s2T[:, :]).then_inc(s2_out, 16)
            for t in range(T):
                sp.dma_start(mrow[:, t], io["mrow"][t].rearrange("p c j -> p (c j)")).then_inc(m_in, 16)
            for t in range(T):
                sp.dma_start(mT[:, t], io["mT"][t]).then_inc(m_in, 16)
            sp.wait_ge(s2_out, 16)

            def slot(b, first, last):
                if not last:
                    if not first:
                        sp.wait_ge(maxed, b * T)
                    sp.dma_start(s2row[:, :], io["s2row"].rearrange("(b t) j -> b (t j)", b=B)[b]
                                 .partition_broadcast(P)).then_inc(row_in, 16)
                    if not first:
                        sp.wait_ge(used, b * T)
                    sp.dma_start(hb[:, :, 0:D], batch_view(io["h1"])[b]).then_inc(h_in, 16)
                if not first:
                    if not (isinstance(b, int) and b == 1):
                        sp.wait_ge(x_out, b * 16 - 16)
                    sp.dma_start(xt[:, :, :], batch_view(io["x1"])[b - 1]).then_inc(x_in, 16)
                if not last:
                    sp.wait_ge(r_copied, b + 1)
                    sp.dma_start(io["rrow"], rT[:, :]).then_inc(r_out, 16)
                    sp.wait_ge(r_out, b * 16 + 16)
                    if not first:
                        sp.wait_ge(z_ready, b * T)
                    for k in range(2):
                        sp.dma_start(rows[:, k], io["rrow"].rearrange("(k t) j -> k (t j)", k=2)[k]
                                     .partition_broadcast(P)).then_inc(r_in, 16)
                if not first:
                    for k in range(2):
                        sp.wait_ge(h_done, b * 2 - 1 + k)
                        sp.dma_start(batch_view(io["h2"])[b - 1][:, k * HALF:(k + 1) * HALF],
                                     hn[:, :, :]).then_inc(h_out, 16)
                    sp.dma_start(batch_view(io["x2"])[b - 1], xt[:, :, :]).then_inc(x_out, 16)
            batches(sp, slot)
            sp.wait_ge(x_out, 16 * B)
            sp.wait_ge(h_out, 32 * B)

        @block.gpsimd
        def _(pool):
            ln.pool_setup(pool)
            pool.memset(hb[:, :, D:D + 1], 1.0).then_inc(ones_set, 1)
            for k in range(2):
                ln.pool(pool, k)
            with pool.Fori(1, B) as b:
                for k in range(2):
                    ln.pool(pool, b * 2 + k)

        @block.scalar
        def _(act):
            act.wait_ge(s2_turned, 1)
            act.activation(s2T[:, :], pq[:, 0, 0:P], ACT.Copy).then_inc(s2_copied, 1)

            def slot(b, first, last):
                if not last:
                    act.wait_ge(r_turned, b + 1)
                    act.activation(rT[:, :], pq[0:2 * T, 0, 0:P], ACT.Copy).then_inc(r_copied, 1)
                if not first:
                    for q in range(4):
                        act.wait_ge(u_turned, b * 4 - 3 + q)
                        act.activation(ut[:, :, :], pq[:, 0, :].rearrange("p (c j) -> p c j", j=P),
                                       ACT.Copy).then_inc(ut_ready, 1)
                        if q % 2:
                            ln.scalar(act, b * 2 - 2 + q // 2, hn[:, :, :])
                if not last:
                    for j in range(T):
                        act.wait_ge(z_ready, b * T + j + 1)
                        if j >= 2 or not first:
                            act.wait_ge(masked, b * T + j - 1)
                        act.activation(e[:, j % 2], z[:, j % 2], ACT.Exp,
                                       bias=cols[:, 1, j:j + 1]).then_inc(exped, 1)
            batches(act, slot)

        @block.vector
        def _(dve):
            low, s2b, shifted, m, tmp = (cols[:, k] for k in (0, 1, 2, 3, 4))

            def maxima(b, first):
                own = Chain(dve, max_own, 6)
                own.step(b)
                if not first:
                    dve.wait_ge(exped, b * T)
                dve.wait_ge(row_in, b * 16 + 16)
                own.link(dve.tensor_reduce(low[:, 0:1], s2row[:, :], AX.X, ALU.min))
                own.link(dve.tensor_scalar(s2row[:, :], s2row[:, :], low[:, 0:1], None, ALU.subtract))
                dve.tensor_scalar(s2b, keep["s2"][:, b, :], 1.0, None, ALU.mult)
                dve.tensor_scalar(shifted, keep["s2"][:, b, :], ALPHA - 1.0, None, ALU.mult)
                for t in range(T):
                    if t >= 2:
                        dve.wait_ge(maxed, b * T + t - 1)
                    elif not first:
                        dve.wait_ge(maxed, b * T)
                    dve.memset(cols[:, 5, t:t + 1], 0.0)
                    dve.tensor_tensor_reduce(z[:, t % 2], s2row[:, :], mrow[:, t], 1.0, 0.0,
                                             ALU.mult, ALU.max, m[:, t:t + 1]).then_inc(maxed, 1)
                dve.wait_ge(maxed, b * T + T)
                own.link(dve.scalar_tensor_tensor(tmp, m, low[:, 0:1], keep["s1"][:, b, :], ALU.add, ALU.add))
                own.link(dve.scalar_tensor_tensor(m, tmp, ALPHA, tmp, ALU.mult, ALU.max))
                dve.tensor_tensor(rcol[:, 0], keep["s1"][:, b, :], m, ALU.subtract)
                own.link(dve.tensor_scalar(tmp, keep["s1"][:, b, :], ALPHA, None, ALU.mult))
                own.link(dve.tensor_tensor(rcol[:, 1], tmp, m, ALU.subtract))

            def tail(b):
                dve.wait_ge(x_in, b * 16 + 16)
                for q in range(4):
                    k = q // 2
                    dve.wait_ge(projected, b * 4 + q + 1)
                    dve.tensor_tensor(xt[:, 4 * q:4 * q + 4], pq[:, 1, :].rearrange("p (c j) -> p c j", j=D),
                                      xt[:, 4 * q:4 * q + 4], ALU.add).then_inc(x_done, 1)
                    if q % 2:
                        dve.wait_ge(x_done, b * 4 + q + 1)
                        if q == 3 or not isinstance(b, int) or b > 0:
                            dve.wait_ge(h_out, (b * 2 + k) * 16)
                        ln.vector(dve, b * 2 + k, xt[:, k * HALF:(k + 1) * HALF], hn[:, :, :], h_done)

            def slot(b, first, last):
                if not last:
                    maxima(b, first)
                if not first:
                    tail(b - 1)
                if last:
                    return
                dve.wait_ge(r_in, b * 32 + 32)
                for j in range(T):
                    if j >= 2 or not first:
                        dve.wait_ge(exped, b * T + j - 1)
                    dve.scalar_tensor_tensor(z[:, j % 2], rows[:, 1], shifted[:, j:j + 1], rows[:, 0],
                                             ALU.add, ALU.max).then_inc(z_ready, 1)
                    if j >= 1:
                        mask(b, j - 1, first)
                mask(b, T - 1, first)
                own = Chain(dve, rec_own, NBANK)
                own.step(b)
                dve.wait_ge(used, b * T + T)
                for k in range(NBANK):
                    n = min(BANK, T - k * BANK)
                    a3 = acc[:, k, 0:n * (D + 1)].rearrange("p (c j) -> p c j", j=D + 1)
                    own.link(dve.reciprocal(rec[:, k * BANK:k * BANK + n], a3[:, :, D]))
                    dve.tensor_tensor(u[:, k * BANK:k * BANK + n], a3[:, :, 0:D],
                                      over(rec[:, k * BANK:k * BANK + n], D), ALU.mult).then_inc(normed, 1)

            def mask(b, j, first):
                dve.wait_ge(exped, b * T + j + 1)
                if j >= 2 or not first:
                    dve.wait_ge(used, b * T + j - 1)
                dve.tensor_tensor(pr[:, j % 2].rearrange("p (c i) -> p c i", i=P),
                                  e[:, j % 2].rearrange("p (c i) -> p c i", i=P), mT[:, :, j],
                                  ALU.mult).then_inc(masked, 1)

            dve.wait_ge(m_in, 32 * T)
            batches(dve, slot)

        @block.tensor
        def _(pe):
            pe.transpose(pq[:, 0, 0:P], keep["s2"][:, :, :].rearrange("p b t -> p (b t)"),
                         ident[:, :]).then_inc(s2_turned, 1)
            pe.wait_ge(w_in, 16)
            pe.wait_ge(ones_set, 1)

            def slot(b, first, last):
                if not last:
                    pe.wait_ge(max_own, b * 6 + 6)
                    if first:
                        pe.wait_ge(s2_copied, 1)
                    pe.transpose(pq[0:2 * T, 0, 0:P], rcol[:, :, :].rearrange("p k t -> p (k t)"),
                                 ident[:, :]).then_inc(r_turned, 1)
                    pe.wait_ge(r_copied, b + 1)
                if not first:
                    pe.wait_ge(normed, b * NBANK)
                    for q in range(4):
                        if q:
                            pe.wait_ge(ut_ready, b * 4 - 4 + q)
                        for c in range(4):
                            ins = pe.transpose(pq[:, 0, c * P:(c + 1) * P], u[:, 4 * q + c], ident[:, :])
                        ins.then_inc(u_turned, 1)
                        pe.wait_ge(ut_ready, b * 4 - 3 + q)
                        if q:
                            pe.wait_ge(x_done, b * 4 - 4 + q)
                        for c in range(4):
                            ins = pe.matmul(pq[:, 1, c * D:(c + 1) * D], ut[:, c], wsb[:, :],
                                            start=True, stop=True)
                        ins.then_inc(projected, 1)
                if not last:
                    pe.wait_ge(h_in, b * 16 + 16)
                    for j in range(T):
                        pe.wait_ge(masked, b * T + j + 1)
                        for t in range(T):
                            k, o = bank(t)
                            ins = pe.matmul(acc[:, k, o:o + D + 1], pr[:, j % 2, t * P:(t + 1) * P],
                                            hb[:, j], start=(j == 0 and o == 0), stop=(j == T - 1),
                                            skip_group_check=True)
                        ins.then_inc(used, 1)
            batches(pe, slot)


def lstm_units():
    units = []
    for p in range(1, SKIP + 1):
        windows = N // p
        parts = -(-windows // 512)
        size = -(-windows // parts)
        size += size % 2
        for w0 in range(0, windows, size):
            for q in range(p):
                units.append((p, w0, min(size, windows - w0), q))
    return units


def recurrences(prog, io, keep, weights):
    nc = prog.nc
    units = lstm_units()
    NU = len(units)
    GATES = {True: (2, 0, 3), False: (2, 0, 1, 3)}
    gates = [GATES[q == 0] for _, _, _, q in units]
    before = [sum(len(g) for g in gates[:k]) for k in range(NU + 1)]
    NG = before[NU]
    level_end = {p: max((k for k, u in enumerate(units) if u[0] < p), default=-1) for p in range(1, SKIP + 1)}
    with ExitStack() as ctx:
        G4 = 4 * D
        w_hi = prog.sb(ctx, "r_w_hi", [P, 2, SKIP, G4], F32R)
        w_lo = prog.sb(ctx, "r_w_lo", [P, 2, SKIP, G4], F32R)
        bias = prog.sb(ctx, "r_bias", [P, 3, SKIP, 4])
        pair = range(2)
        hx = [prog.sb(ctx, f"r_hx{k}", [P, N]) for k in pair]
        hx_hi = [prog.sb(ctx, f"r_hx_hi{k}", [P, N], F32R) for k in pair]
        hx_lo = [prog.sb(ctx, f"r_hx_lo{k}", [P, N], F32R) for k in pair]
        gate = [prog.sb(ctx, f"r_gate{k}", [P, 4, 512]) for k in pair]
        cell = [prog.sb(ctx, f"r_cell{k}", [P, 2, 512]) for k in pair]
        tc = [prog.sb(ctx, f"r_tc{k}", [P, 512]) for k in pair]
        st = [prog.sb(ctx, f"r_st{k}", [P, 512]) for k in pair]
        st_hi = [prog.sb(ctx, f"r_st_hi{k}", [P, 512], F32R) for k in pair]
        st_lo = [prog.sb(ctx, f"r_st_lo{k}", [P, 512], F32R) for k in pair]
        xt = prog.sb(ctx, "r_xt", [P, T, D])
        hn = prog.sb(ctx, "r_hn", [P, T, D])
        ps = [prog.ps(ctx, f"r_ps{k}", [P, 4, 512]) for k in pair]
        ident = keep["ident"]
        ln = LayerNorm(prog, ctx, "rln", T)
        sem, sems = (lambda s: prog.sem(f"r_{s}")), (lambda s: prog.sems(f"r_{s}"))
        w_in, b_in, w_high, w_split = sem("w_in"), sem("b_in"), sem("w_high"), sem("w_split")
        b_own, b_ready = sem("b_own"), sem("b_ready")
        h_in, h_high, h_low = sems("h_in"), sems("h_high"), sems("h_low")
        summed, activated = sems("summed"), sems("activated")
        own, cell_ready, squashed = sems("own"), sems("cell_ready"), sems("squashed")
        state, high, low = sems("state"), sems("high"), sems("low")
        turned, x_in, x_done, x_out, h_done, h_out = (sem(s) for s in (
            "turned", "x_in", "x_done", "x_out", "h_done", "h_out"))
        batch_view = lambda d: d.rearrange("t p b f -> b p t f")
        with ExitStack() as c1:
            w_raw = prog.sb(c1, "r_w_raw", [P, 2, SKIP, G4])
            block = c1.enter_context(nc.Block())

            @block.sync
            def _(sp):
                for k, name in enumerate(("wih", "whh")):
                    sp.dma_start(w_raw[:, k], weights[name]).then_inc(w_in, 16)
                for k, name in enumerate(("bih", "bhh")):
                    sp.dma_start(bias[:, k], weights[name]).then_inc(b_in, 16)

            @block.scalar
            def _(act):
                act.wait_ge(w_in, 32)
                act.activation(w_hi[:, :, :, :], w_raw[:, :, :, :], ACT.Copy).then_inc(w_high, 1)

            @block.vector
            def _(dve):
                dve.wait_ge(b_in, 32)
                dve.tensor_tensor(bias[:, 2], bias[:, 0], bias[:, 1], ALU.add).then_inc(b_ready, 1)
                dve.wait_ge(w_high, 1)
                dve.tensor_tensor(w_lo[:, :, :, :], w_raw[:, :, :, :], w_hi[:, :, :, :].bitcast(F32),
                                  ALU.subtract).then_inc(w_split, 1)
        block = ctx.enter_context(nc.Block())
        NPAIR = B // 2

        def pairs(eng, slot):
            slot(0, True)
            with eng.Fori(1, NPAIR) as i:
                slot(i, False)

        def turns():
            for n in range(NU):
                for k in pair:
                    yield n, k

        @block.sync
        def _(sp):
            def slot(i, first):
                for k in pair:
                    if not first:
                        sp.wait_ge(x_done, i * 2 - 1 + k)
                    sp.dma_start(hx[k][:, :], io["hT"][i * 2 + k]).then_inc(h_in[k], 16)
                for k in pair:
                    if not first or k:
                        sp.wait_ge(x_out, (i * 2 + k) * 16)
                        sp.wait_ge(h_done, i * 2 + k)
                    sp.dma_start(xt[:, :, :], batch_view(io["x2"])[i * 2 + k]).then_inc(x_in, 16)
                    sp.wait_ge(x_done, i * 2 + k + 1)
                    sp.dma_start(batch_view(io["x3"])[i * 2 + k], xt[:, :, :]).then_inc(x_out, 16)
                    sp.wait_ge(h_done, i * 2 + k + 1)
                    sp.dma_start(batch_view(io["h3"])[i * 2 + k], hn[:, :, :]).then_inc(h_out, 16)
            pairs(sp, slot)
            sp.wait_ge(x_out, 16 * B)
            sp.wait_ge(h_out, 16 * B)

        @block.gpsimd
        def _(pool):
            ln.pool_setup(pool)
            ln.pool(pool, 0)
            with pool.Fori(1, B) as b:
                ln.pool(pool, b)

        def places(n):
            p, w0, size, q = units[n]
            return slice(w0 * p + q, w0 * p + q + (size - 1) * p + 1, p)

        @block.scalar
        def _(act):
            def evaluate(i, n, k):
                size, last_step = units[n][2], units[n][3] == units[n][0] - 1
                for j, g in enumerate(gates[n]):
                    at = i * NG + before[n] + j
                    if j == 0 and (n > 0 or not isinstance(i, int)):
                        act.wait_ge(state[k], i * NU + n)
                    act.wait_ge(summed[k], at + 1)
                    act.activation(gate[k][:, g, 0:size], ps[k][:, g, 0:size],
                                   ACT.Tanh if g == 2 else ACT.Sigmoid,
                                   bias=bias[:, 2, units[n][0] - 1, g:g + 1]).then_inc(activated[k], 1)
                act.wait_ge(cell_ready[k], i * NU + n + 1)
                act.activation(tc[k][:, 0:size], cell[k][:, 0, 0:size], ACT.Tanh).then_inc(squashed[k], 1)

            def round_state(i, n, k):
                size, last_step = units[n][2], units[n][3] == units[n][0] - 1
                act.wait_ge(state[k], i * NU + n + 1)
                src, dst = (hx[k][:, places(n)], hx_hi[k][:, places(n)]) if last_step else \
                    (st[k][:, 0:size], st_hi[k][:, 0:size])
                act.activation(dst, src, ACT.Copy).then_inc(high[k], 1)

            def slot(i, first):
                for k in pair:
                    act.wait_ge(h_in[k], i * 16 + 16)
                    act.activation(hx_hi[k][:, :], hx[k][:, :], ACT.Copy).then_inc(h_high[k], 1)
                for n, k in turns():
                    evaluate(i, n, k)
                    round_state(i, n, k)
                for k in pair:
                    ln.scalar(act, i * 2 + k, hn[:, :, :])
            pairs(act, slot)

        @block.vector
        def _(dve):
            def update(i, n, k):
                p, _, size, q = units[n]
                c, ig = cell[k][:, 0, 0:size], cell[k][:, 1, 0:size]
                ga = lambda g: gate[k][:, g, 0:size]
                at = i * NG + before[n]
                if q == 0:
                    dve.wait_ge(activated[k], at + 2)
                    dve.tensor_tensor(c, ga(0), ga(2), ALU.mult).then_inc(cell_ready[k], 1)
                else:
                    done = sum(1 for u in units[:n] if u[3])
                    total = sum(1 for u in units if u[3])
                    own_at = (i * total + done) * 2
                    dve.wait_ge(activated[k], at + 2)
                    dve.tensor_tensor(ig, ga(0), ga(2), ALU.mult).then_inc(own[k], 1)
                    dve.wait_ge(activated[k], at + 3)
                    dve.tensor_tensor(c, ga(1), c, ALU.mult).then_inc(own[k], 1)
                    dve.wait_ge(own[k], own_at + 2)
                    dve.tensor_tensor(c, c, ig, ALU.add).then_inc(cell_ready[k], 1)

            def output(i, n, k):
                p, _, size, q = units[n]
                last_step = q == p - 1
                h = hx[k][:, places(n)] if last_step else st[k][:, 0:size]
                dve.wait_ge(activated[k], i * NG + before[n + 1])
                dve.wait_ge(squashed[k], i * NU + n + 1)
                dve.tensor_tensor(h, gate[k][:, 3, 0:size], tc[k][:, 0:size], ALU.mult).then_inc(state[k], 1)

            def low_part(i, n, k):
                p, _, size, q = units[n]
                last_step = q == p - 1
                src, hi, dst = (t[k][:, places(n)] if last_step else t[k][:, 0:size] for t in
                                ((hx, hx_hi, hx_lo) if last_step else (st, st_hi, st_lo)))
                dve.wait_ge(high[k], i * NU + n + 1)
                dve.tensor_tensor(dst, src, hi.bitcast(F32), ALU.subtract).then_inc(low[k], 1)

            def finish(i, k):
                b = i * 2 + k
                dve.wait_ge(x_in, b * 16 + 16)
                dve.wait_ge(turned, b + 1)
                dve.tensor_tensor(xt[:, :, :], ps[k][:, :, :].rearrange("p g (c f) -> p (g c) f", f=D),
                                  xt[:, :, :], ALU.add).then_inc(x_done, 1)
                if k or not isinstance(i, int):
                    dve.wait_ge(h_out, b * 16)
                dve.wait_ge(x_done, b + 1)
                ln.vector(dve, b, xt[:, :, :], hn[:, :, :], h_done)

            def slot(i, first):
                for k in pair:
                    dve.wait_ge(h_high[k], i + 1)
                    dve.tensor_tensor(hx_lo[k][:, :], hx[k][:, :], hx_hi[k][:, :].bitcast(F32),
                                      ALU.subtract).then_inc(h_low[k], 1)
                for n, k in turns():
                    update(i, n, k)
                    output(i, n, k)
                    low_part(i, n, k)
                for k in pair:
                    finish(i, k)
            pairs(dve, slot)

        @block.tensor
        def _(pe):
            def gates_of(i, n, k):
                p, _, size, q = units[n]
                if n == 0:
                    pe.wait_ge(h_low[k], i + 1)
                if level_end[p] >= 0 and q == 0:
                    pe.wait_ge(low[k], i * NU + level_end[p] + 1)
                at = i * NG + before[n]
                x_parts = [(w_hi, hx_hi), (w_hi, hx_lo), (w_lo, hx_hi)]
                h_parts = [(w_hi, st_hi), (w_hi, st_lo), (w_lo, st_hi)]
                for j, g in enumerate(gates[n]):
                    for m, (w, h) in enumerate(x_parts):
                        if m == 0 and (n > 0 or not isinstance(i, int)):
                            if j == 0:
                                pe.wait_ge(activated[k], at)
                                if n == 0:
                                    pe.wait_ge(x_done, i * 2 - 1 + k)
                        last = pe.matmul(ps[k][:, g, 0:size], w[:, 0, p - 1, g * D:(g + 1) * D],
                                         h[k][:, places(n)], start=(m == 0), stop=(q == 0 and m == 2))
                    if q == 0:
                        last.then_inc(summed[k], 1)
                if q:
                    pe.wait_ge(low[k], i * NU + n)
                    for j, g in enumerate(gates[n]):
                        for m, (w, h) in enumerate(h_parts):
                            last = pe.matmul(ps[k][:, g, 0:size], w[:, 1, p - 1, g * D:(g + 1) * D],
                                             h[k][:, 0:size], start=False, stop=(m == 2))
                        last.then_inc(summed[k], 1)

            def slot(i, first):
                for n, k in turns():
                    gates_of(i, n, k)
                for k in pair:
                    pe.wait_ge(low[k], i * NU + NU)
                    pe.wait_ge(activated[k], i * NG + NG)
                    for t in range(T):
                        last = pe.transpose(ps[k][:, t // 4, (t % 4) * D:(t % 4 + 1) * D],
                                            hx[k][:, t * P:(t + 1) * P], ident[:, :])
                    last.then_inc(turned, 1)
            pairs(pe, slot)


def perceptron(prog, io, keep, weights, out):
    nc = prog.nc
    with ExitStack() as ctx:
        w1 = prog.sb(ctx, "m_w1", [P, HID])
        w2 = prog.sb(ctx, "m_w2", [P, 2, D])
        vec = prog.sb(ctx, "m_vec", [P, 9])
        agg = prog.sb(ctx, "m_agg", [P, 2, W])
        hid = prog.sb(ctx, "m_hid", [P, 2, 2, 512])
        o2 = prog.sb(ctx, "m_o2", [P, T, W])
        bn2 = prog.sb(ctx, "m_bn2", [P, 2 * T, 6])
        mv = prog.sb(ctx, "m_mv", [P, 3, 2])
        var = prog.sb(ctx, "m_var", [P, 3])
        aff = prog.sb(ctx, "m_aff", [P, 3, 4])
        y = prog.sb(ctx, "m_y", [P, 2, W])
        xt = prog.sb(ctx, "m_xt", [P, 2, B, D])
        ph = prog.ps(ctx, "m_ph", [P, 2, 2, 512])
        po = prog.ps(ctx, "m_po", [P, 2, 512])
        pt = prog.ps(ctx, "m_pt", [P, B, D])
        sem, sems = (lambda s: prog.sem(f"m_{s}")), (lambda s: prog.sems(f"m_{s}"))
        w_in, v_in, powered, aff_own, aff_ready = (sem(s) for s in ("w_in", "v_in", "powered", "aff_own", "aff_ready"))
        agg_in, x_in, x_out = sems("agg_in"), sems("x_in"), sems("x_out")
        h_summed, h_ready, o_summed, o_read = (sem(s) for s in ("h_summed", "h_ready", "o_summed", "o_read"))
        y_ready, turned, x_done = (sem(s) for s in ("y_ready", "turned", "x_done"))
        out_tiles = out.rearrange("b (t p) f -> t p b f", p=P)
        ident = keep["ident"]
        block = ctx.enter_context(nc.Block())

        @block.sync
        def _(sp):
            sp.dma_start(w1[:, :], weights["w1"]).then_inc(w_in, 16)
            sp.dma_start(w2[:, :, :], weights["w2"]).then_inc(w_in, 16)
            sp.dma_start(vec[:, :], weights["vec"]).then_inc(v_in, 16)

            def load(t):
                if t.within(2, T):
                    sp.wait_ge(h_summed, t.n * 4 - 4)
                sp.dma_start(agg[:, t.par], io["aggT"][t.n].rearrange("p b j -> p (b j)")).then_inc(agg_in[t.par], 16)
            run_slots(sp, load, T, 2, 2)

            def slot(t):
                if t.within(0, T):
                    if t.within(2, T):
                        sp.wait_ge(x_out[t.par], t.pair * 16)
                    sp.dma_start(xt[:, t.par], io["x3"][t.n]).then_inc(x_in[t.par], 16)
                if t.within(1, T + 1):
                    u = t - 1
                    sp.wait_ge(x_done, u.n + 1)
                    sp.dma_start(out_tiles[u.n], xt[:, u.par]).then_inc(x_out[u.par], 16)
            run_slots(sp, slot, T + 1)
            for s in x_out:
                sp.wait_ge(s, 16 * HALF)

        def affine(dve, j, stats, k0):
            step = Chain(dve, aff_own, 6)
            step.step(j)
            step.link(dve.bn_aggr(mv[:, j], stats))
            step.link(dve.tensor_scalar(var[:, j:j + 1], mv[:, j, 1:2], EPS, None, ALU.add))
            step.link(dve.tensor_tensor(aff[:, j, 2:3], mv[:, j, 0:1], vec[:, k0:k0 + 1], ALU.add))
            step.link(dve.tensor_tensor(aff[:, j, 3:4], vec[:, k0:k0 + 1], aff[:, j, 2:3], ALU.subtract))
            dve.wait_ge(powered, j + 1)
            step.link(dve.tensor_tensor(aff[:, j, 0:1], var[:, j:j + 1], vec[:, k0 + 1:k0 + 2], ALU.mult))
            step.link(dve.scalar_tensor_tensor(aff[:, j, 1:2], aff[:, j, 0:1], aff[:, j, 3:4],
                                               vec[:, k0 + 2:k0 + 3], ALU.mult, ALU.add))

        @block.gpsimd
        def _(pool):
            half = keep["halves"]
            for j in range(3):
                pool.wait_ge(aff_own, 6 * j + 2)
                pool.tensor_tensor(var[:, j:j + 1], var[:, j:j + 1], half[:, 0:1], ALU.pow).then_inc(powered, 1)

        @block.scalar
        def _(act):
            act.wait_ge(aff_own, 12)

            def slot(t):
                for c in range(2):
                    n = t.n * 2 + c
                    for k in range(2):
                        act.wait_ge(h_summed, n * 2 + k + 1)
                        if t.within(1, T):
                            act.wait_ge(o_summed, n - 1)
                        act.activation(hid[:, c, k], ph[:, c, k], ACT.Relu, bias=aff[:, k, 1:2],
                                       scale=aff[:, k, 0:1]).then_inc(h_ready, 1)
            run_slots(act, slot, T, 2, 2)

        @block.vector
        def _(dve):
            dve.wait_ge(v_in, 16)
            for k in range(2):
                affine(dve, k, keep["bn1"][:, k].rearrange("p c s -> p (c s)"), 3 * k)

            def slot(t):
                for c in range(2):
                    n = t.n * 2 + c
                    dve.wait_ge(o_summed, n + 1)
                    dve.tensor_scalar(o2[:, t.n, c * 512:(c + 1) * 512], po[:, c], 1.0, None, ALU.mult)
                    dve.bn_stats(bn2[:, n], po[:, c]).then_inc(o_read, 1)
            run_slots(dve, slot, T, 2, 2)
            dve.wait_ge(o_read, 2 * T)
            affine(dve, 2, bn2[:, :, :].rearrange("p c s -> p (c s)"), 6)

            def final(t):
                if t.within(0, T):
                    if t.within(2, T):
                        dve.wait_ge(turned, t.n - 1)
                    dve.tensor_scalar(y[:, t.par], o2[:, t.n], aff[:, 2, 0:1], aff[:, 2, 1:2], ALU.mult,
                                      ALU.add).then_inc(y_ready, 1)
                if t.within(1, T + 1):
                    u = t - 1
                    dve.wait_ge(x_in[u.par], u.pair * 16 + 16)
                    dve.wait_ge(turned, u.n + 1)
                    dve.tensor_tensor(xt[:, u.par], pt[:, :, :], xt[:, u.par], ALU.add).then_inc(x_done, 1)
            run_slots(dve, final, T + 1)

        @block.tensor
        def _(pe):
            pe.wait_ge(w_in, 32)

            def slot(t):
                pe.wait_ge(agg_in[t.par], t.pair * 16 + 16)
                for c in range(2):
                    for k in range(2):
                        if t.within(1, T):
                            pe.wait_ge(h_ready, t.n * 4 + c * 2 + k - 3)
                        pe.matmul(ph[:, c, k], w1[:, k * P:(k + 1) * P], agg[:, t.par, c * 512:(c + 1) * 512],
                                  start=True, stop=True).then_inc(h_summed, 1)
                for c in range(2):
                    n = t.n * 2 + c
                    for k in range(2):
                        pe.wait_ge(h_ready, n * 2 + k + 1)
                        if k == 0 and t.within(1, T):
                            pe.wait_ge(o_read, n - 1)
                        last = pe.matmul(po[:, c], w2[:, k], hid[:, c, k], start=(k == 0), stop=(k == 1))
                    last.then_inc(o_summed, 1)
            run_slots(pe, slot, T, 2, 2)

            def final(t):
                pe.wait_ge(y_ready, t.n + 1)
                if t.within(1, T):
                    pe.wait_ge(x_done, t.n)
                for b in range(B):
                    last = pe.transpose(pt[:, b], y[:, t.par, b * P:(b + 1) * P], ident[:, :])
                last.then_inc(turned, 1)
            run_slots(pe, final, T, 2, 2)


def network(nc, x, adj, w0, wa, wcT, wc, wg0, bg0, wg1, bg1, wih, whh, bih, bhh, w1, w2, vec, out):
    with ExitStack() as ctx:
        prog = Program(nc, ctx)
        io = {}
        for name in ("h0", "x1", "h1", "x2", "h2", "h2b", "x3", "h3"):
            io[name] = nc.dram_tensor(name, [T, P, B, D], F32).ap()
        for name in ("adjT", "anorm"):
            io[name] = nc.dram_tensor(name, [T, P, T, P], F32).ap()
        for name in ("mrow", "mT"):
            io[name] = nc.dram_tensor(name, [T, P, T, P], U8).ap()
        io["hT"] = nc.dram_tensor("hT", [B, P, N], F32).ap()
        io["aggT"] = nc.dram_tensor("aggT", [T, P, B, P], F32).ap()
        io["rsrow"] = nc.dram_tensor("rsrow", [T, P], F32).ap()
        io["s2row"] = nc.dram_tensor("s2row", [B * T, P], F32).ap()
        io["rrow"] = nc.dram_tensor("rrow", [2 * T, P], F32).ap()
        keep = {k: prog.sb(ctx, f"k_{k}", s) for k, s in dict(
            ident=[P, P], ones=[P, 2], halves=[P, T], rs=[P, T], rsT=[P, P], dinv=[P, T], ndinv=[P, T],
            dinv3=[P, T], wa=[P, 2, D], s1=[P, B, T], s2=[P, B, T], bn1=[P, 2, 2 * T, 6]).items()}
        prepare(prog, io, keep, x, adj, wa, wcT)
        prog.retire()
        product(prog, io, keep, "l0", io["anorm"], io["h0"], dict(w=w0), "L0",
                x.rearrange("b (t p) f -> t p b f", p=P))
        prog.retire()
        attention(prog, io, keep, wc)
        prog.retire()
        product(prog, io, keep, "l2a", io["adjT"], io["h2"], dict(w=wg0, b=bg0), "L2a")
        prog.retire()
        product(prog, io, keep, "l2b", io["adjT"], io["h2b"], dict(w=wg1, b=bg1), "L2b")
        prog.retire()
        recurrences(prog, io, keep, dict(wih=wih, whh=whh, bih=bih, bhh=bhh))
        prog.retire()
        product(prog, io, keep, "l3", io["adjT"], io["h3"], dict(w=w1), "L3")
        prog.retire()
        perceptron(prog, io, keep, dict(w1=w1, w2=w2, vec=vec), out)


def kernel(**inputs):
    import numpy as _np
    import concourse.bacc as _bacc
    from concourse.bass_utils import run_bass_kernel_spmd as _run

    a = {k: _np.asarray(v) for k, v in inputs.items()}
    lay = {
        "x": a["x"],
        "adj": a["adj"],
        "w0": a["L0_gnn_W"],
        "wcT": a["L1_gnn_W"].T,
        "wa": a["L1_gnn_a"].reshape(2, D).T,
        "wc": a["L1_gnn_W"],
        "wg0": a["L2_gnn_Wg0"],
        "bg0": a["L2_gnn_bg0"],
        "wg1": a["L2_gnn_Wg1"],
        "bg1": a["L2_gnn_bg1"].reshape(D, 1),
        "wih": a["L2_gnn_Wih"].transpose(2, 0, 1),
        "whh": a["L2_gnn_Whh"].transpose(2, 0, 1),
        "bih": a["L2_gnn_bih"].reshape(SKIP, 4, D).transpose(2, 0, 1),
        "bhh": a["L2_gnn_bhh"].reshape(SKIP, 4, D).transpose(2, 0, 1),
        "w1": a["L3_gnn_W1"].T,
        "w2": a["L3_gnn_W2"].T.reshape(2, P, D).transpose(1, 0, 2),
        "vec": _np.stack([a[f"L3_gnn_{n}1"].reshape(2, P)[k] for k in range(2) for n in ("b", "g", "be")]
                         + [a[f"L3_gnn_{n}2"] for n in ("b", "g", "be")], axis=1),
    }
    lay = {k: _np.ascontiguousarray(v) for k, v in lay.items()}
    nc = _bacc.Bacc("TRN2", target_bir_lowering=False, num_devices=1)
    args = {k: nc.dram_tensor(f"in_{k}_dram", v.shape, mybir.dt.from_np(v.dtype), kind="ExternalInput").ap()
            for k, v in lay.items()}
    out = nc.dram_tensor("out_0_dram", (B, N, D), F32, kind="ExternalOutput").ap()
    network(nc, out=out, **args)
    r = _run(nc, [{f"in_{k}_dram": v for k, v in lay.items()}], core_ids=[0])
    return r.results[0]["out_0_dram"]
```

```python
import concourse.bass as bass
from concourse import mybir
from contextlib import ExitStack

F32 = mybir.dt.float32
F32R = mybir.dt.float32r
U8 = mybir.dt.uint8
I32 = mybir.dt.int32
ALU = mybir.AluOpType
ACT = mybir.ActivationFunctionType
AX = mybir.AxisListType

P = 128
B, N, D = 8, 2048, 128
T = N // P
W = B * D
EPS = 1e-5
ALPHA = 0.2
HID = 256
SKIP = 4
HALF = T // 2
SPREAD = 40.0


class Tile:

    def __init__(self, off, i=None):
        self.off, self.i = off, i

    @property
    def n(self):
        return self.off if self.i is None else self.i * 2 + self.off

    @property
    def pair(self):
        return self.off // 2 if self.i is None else self.i + self.off // 2

    @property
    def par(self):
        return self.off % 2

    def __add__(self, k):
        return Tile(self.off + k, self.i)

    def __sub__(self, k):
        return Tile(self.off - k, self.i)

    def within(self, lo, hi):
        return self.i is not None or lo <= self.off < hi


def run_slots(eng, slot, n, head=2, tail=3):
    for t in range(head):
        slot(Tile(t))
    with eng.Fori(head // 2, (n - tail) // 2) as i:
        slot(Tile(0, i))
        slot(Tile(1, i))
    for t in range(n - tail, n):
        slot(Tile(t))


class Chain:

    def __init__(self, eng, sem, links):
        self.eng, self.sem, self.links = eng, sem, links

    def step(self, t):
        self.base, self.k = t * self.links, 0

    def link(self, ins):
        self.k += 1
        assert self.k <= self.links
        ins.then_inc(self.sem, 1)
        self.eng.wait_ge(self.sem, self.base + self.k)


def over(col, width):
    return col.unsqueeze(2).to_broadcast([col.shape[0], col.shape[1], width])


class Program:
    def __init__(self, nc, ctx):
        self.nc, self.ctx, self.live = nc, ctx, []

    def sem(self, name):
        self.live.append(self.nc.alloc_semaphore(name))
        return self.live[-1]

    def retire(self):
        with self.nc.Block() as block:
            @block.gpsimd
            def _(pool):
                for sem in self.live:
                    pool.sem_clear(sem)
        for sem in self.live:
            self.nc.release_semaphore(sem)
        self.live = []

    def sems(self, name, n=2):
        return [self.sem(f"{name}{k}") for k in range(n)]

    def sb(self, ctx, name, shape, dt=F32):
        return ctx.enter_context(self.nc.sbuf_tensor(name, shape, dt))

    def ps(self, ctx, name, shape):
        return ctx.enter_context(self.nc.psum_tensor(name, shape, F32))


class LayerNorm:

    def __init__(self, prog, ctx, name, blocks):
        self.blocks = blocks
        self.six = prog.sb(ctx, f"{name}_six", [P, blocks, 6])
        self.carrier = prog.sb(ctx, f"{name}_carrier", [P, 1])
        self.mv = prog.sb(ctx, f"{name}_mv", [P, blocks, 2])
        self.minus_mean = prog.sb(ctx, f"{name}_minus_mean", [P, blocks])
        self.var_eps = prog.sb(ctx, f"{name}_var_eps", [P, blocks])
        self.scale = prog.sb(ctx, f"{name}_scale", [P, blocks])
        self.shift = prog.sb(ctx, f"{name}_shift", [P, blocks])
        self.half = prog.sb(ctx, f"{name}_half", [P, blocks])
        self.own = prog.sem(f"{name}_own")
        self.measured = prog.sem(f"{name}_measured")
        self.power = prog.sem(f"{name}_power")
        self.scaled = prog.sem(f"{name}_scaled")
        self.half_set = prog.sem(f"{name}_half_set")

    def vector(self, dve, t, x, later):
        chain = Chain(dve, self.own, 2)
        chain.step(t)
        for b in range(self.blocks):
            last = dve.bn_stats(self.six[:, b], x[:, b])
        chain.link(last)
        dve.memset(self.carrier[:, :], 0.0)
        for b in range(self.blocks):
            last = dve.bn_aggr(self.mv[:, b], self.six[:, b])
        chain.link(last)
        if later:
            dve.wait_ge(self.scaled, t)
        dve.tensor_scalar(self.minus_mean[:, :], self.mv[:, :, 0], -1.0, None, ALU.mult)
        dve.tensor_scalar(self.var_eps[:, :], self.mv[:, :, 1], EPS, None, ALU.add).then_inc(self.measured, 1)

    def pool_setup(self, pool):
        pool.memset(self.half[:, :], -0.5).then_inc(self.half_set, 1)
        pool.wait_ge(self.half_set, 1)

    def pool(self, pool, t, done, later):
        if later:
            pool.wait_ge(done, t)
        pool.wait_ge(self.measured, t + 1)
        pool.tensor_tensor(self.scale[:, :], self.var_eps[:, :], self.half[:, :], ALU.pow).then_inc(self.power, 1)
        pool.wait_ge(self.power, t + 1)
        pool.tensor_tensor(self.shift[:, :], self.minus_mean[:, :], self.scale[:, :],
                           ALU.mult).then_inc(self.scaled, 1)

    def scalar(self, act, t, x, out, done, part=None):
        lo, hi = part or (0, self.blocks)
        if lo == 0:
            act.wait_ge(self.scaled, t + 1)
        for b in range(lo, hi):
            last = act.activation(out[:, b], x[:, b], ACT.Relu, bias=self.shift[:, b:b + 1],
                                  scale=self.scale[:, b:b + 1])
        if hi == self.blocks:
            last.then_inc(done, 1)


def prepare(prog, io, keep, x, adj, a_col, wc_t):
    nc = prog.nc
    x_tiles = x.rearrange("b (t p) f -> t p b f", p=P)
    with ExitStack() as ctx:
        a_sb = prog.sb(ctx, "a_sb", [P, T, N])
        ident = keep["ident"]
        a_loaded = prog.sem("a_loaded")
        w_loaded = prog.sem("w_loaded")

        with ExitStack() as c1:
            xt = prog.sb(c1, "p_xt", [P, 2, B, D])
            ht = prog.sb(c1, "p_ht", [P, 2, B, D])
            ln = LayerNorm(prog, c1, "pln", B)
            x_in, h_out = prog.sems("px_in"), prog.sems("ph_out")
            ln_done = prog.sem("pln_done")
            id_set = prog.sem("id_set")
            acol = prog.sb(c1, "acol", [P, 2])
            wct = prog.sb(c1, "wct", [P, D])
            spread = prog.sb(c1, "spread", [P, 2, P])
            pw = prog.ps(c1, "p_wa", [P, 2, D])
            wa_in, wa_spread, wa_summed = (prog.sem(k) for k in ("wa_in", "wa_spread", "wa_summed"))
            block = c1.enter_context(nc.Block())

            @block.tensor
            def _(pe):
                pe.wait_ge(wa_spread, 2)
                for k in range(2):
                    pe.matmul(pw[:, k], spread[:, k], wct[:, :], start=True, stop=True).then_inc(wa_summed, 1)

            @block.sync
            def _(sp):
                sp.dma_start(acol[:, :], a_col).then_inc(wa_in, 16)
                sp.dma_start(wct[:, :], wc_t).then_inc(wa_in, 16)

                def slot(t):
                    if t.within(0, T):
                        if t.within(2, T):
                            sp.wait_ge(ln_done, t.n - 1)
                        sp.dma_start(xt[:, t.par], x_tiles[t.n]).then_inc(x_in[t.par], 16)
                    if t.within(1, T + 1):
                        u = t - 1
                        sp.wait_ge(ln_done, u.n + 1)
                        sp.dma_start(io["h0"][u.n], ht[:, u.par]).then_inc(h_out[u.par], 16)
                run_slots(sp, slot, T + 1)
                for s in h_out:
                    sp.wait_ge(s, 16 * HALF)

            @block.scalar
            def _(act):
                for t in range(T):
                    act.dma_start(a_sb[:, t], adj[t * P:(t + 1) * P, :]).then_inc(a_loaded, 16)

                def slot(t):
                    if t.within(2, T):
                        act.wait_ge(h_out[t.par], t.pair * 16)
                    ln.scalar(act, t.n, xt[:, t.par], ht[:, t.par], ln_done)
                run_slots(act, slot, T, 2, 2)

            @block.gpsimd
            def _(pool):
                pool.memset(ident[:, :], 0.0).then_inc(id_set, 1)
                pool.memset(keep["ones"][:, :], 1.0).then_inc(id_set, 1)
                pool.wait_ge(id_set, 2)
                pool.affine_select(out=ident[:, :], in_=ident[:, :], compare_op=ALU.not_equal, fill=1.0,
                                   base=0, pattern=[[-1, P]], channel_multiplier=1).then_inc(id_set, 1)
                ln.pool_setup(pool)

                def slot(t):
                    ln.pool(pool, t.n, ln_done, t.within(1, T))
                run_slots(pool, slot, T, 2, 2)

            @block.vector
            def _(dve):
                def slot(t):
                    dve.wait_ge(x_in[t.par], t.pair * 16 + 16)
                    ln.vector(dve, t.n, xt[:, t.par], t.within(1, T))
                dve.wait_ge(id_set, 2)
                dve.wait_ge(wa_in, 32)
                for k in range(2):
                    dve.tensor_scalar(spread[:, k], keep["ones"][:, 0:1].to_broadcast([P, P]), acol[:, k:k + 1],
                                      None, ALU.mult).then_inc(wa_spread, 1)
                run_slots(dve, slot, T, 2, 2)
                dve.wait_ge(wa_summed, 2)
                dve.tensor_copy(keep["wa"][:, :, :], pw[:, :, :])

        with ExitStack() as c2:
            stage = prog.sb(c2, "stage", [P, 2, T, P])
            at = prog.sb(c2, "at", [P, 2, T, P])
            an = prog.sb(c2, "an", [P, 2, T, P])
            mr = prog.sb(c2, "mr", [P, 2, T, P], U8)
            mt = prog.sb(c2, "mt", [P, 2, T, P], U8)
            sums = prog.sb(c2, "sums", [P, 4, T])
            small = prog.sb(c2, "small", [P, 4, T])
            pt = prog.ps(c2, "p_pt", [P, 2, HALF, P])
            pst = prog.ps(c2, "p_sum", [P, 2, 512])
            staged = prog.sem("staged")
            turned = prog.sem("turned")
            copied = prog.sem("copied")
            added = prog.sem("added")
            normed = prog.sem("normed")
            masked = prog.sem("masked")
            summed = prog.sem("summed")
            read = prog.sem("columns_summed")
            reduced = prog.sem("reduced")
            sums_read = prog.sem("sums_read")
            an_out = prog.sems("an_out")
            at_out = prog.sems("at_out")
            mask_out = prog.sems("mask_out")
            own = prog.sem("p_own")
            powered = prog.sem("powered")
            ready = prog.sem("deg_ready")
            rs_turned, rs_copied, rs_out = prog.sem("rs_turned"), prog.sem("rs_copied"), prog.sem("rs_out")
            block = c2.enter_context(nc.Block())

            @block.sync
            def _(sp):
                def slot(t):
                    sp.wait_ge(copied, t.n * 2 + 2)
                    sp.dma_start(io["adjT"][t.n], at[:, t.par]).then_inc(at_out[t.par], 16)
                    sp.wait_ge(masked, t.n + 1)
                    sp.dma_start(io["mrow"][t.n], mr[:, t.par]).then_inc(mask_out[t.par], 16)
                    sp.dma_start(io["mT"][t.n], mt[:, t.par]).then_inc(mask_out[t.par], 16)
                    sp.wait_ge(normed, t.n + 1)
                    sp.dma_start(io["anorm"][t.n], an[:, t.par]).then_inc(an_out[t.par], 16)
                run_slots(sp, slot, T, 2, 2)
                sp.wait_ge(rs_copied, 1)
                sp.dma_start(io["rsrow"], keep["rsT"][0:T, :]).then_inc(rs_out, 16)
                for s in at_out + an_out:
                    sp.wait_ge(s, 16 * HALF)
                for s in mask_out:
                    sp.wait_ge(s, 32 * HALF)
                sp.wait_ge(rs_out, 16)

            @block.scalar
            def _(act):
                def slot(t):
                    if t.within(0, T):
                        if t.within(2, T):
                            act.wait_ge(turned, t.n * 2 - 2)
                            act.wait_ge(masked, t.n - 1)
                        act.wait_ge(a_loaded, 16 * T)
                        act.activation(stage[:, t.par].rearrange("p c j -> p (c j)"), a_sb[:, t.n],
                                       ACT.Copy).then_inc(staged, 1)
                    if t.within(1, T + 1):
                        u = t - 1
                        if u.within(2, T):
                            act.wait_ge(at_out[u.par], u.pair * 16)
                            act.wait_ge(summed, u.n - 1)
                            act.wait_ge(read, u.n - 1)
                        for h in range(2):
                            act.wait_ge(turned, u.n * 2 + h + 1)
                            act.activation(at[:, u.par, h * HALF:(h + 1) * HALF], pt[:, h],
                                           ACT.Copy).then_inc(copied, 1)
                run_slots(act, slot, T + 1)
                act.wait_ge(rs_turned, 1)
                act.activation(keep["rsT"][0:T, :], pst[0:T, 0, 0:P], ACT.Copy).then_inc(rs_copied, 1)

            @block.vector
            def _(dve):
                sym, row, col, dia = (sums[:, j] for j in range(4))
                chain = Chain(dve, own, 1)
                chain.step(0)
                chain.link(dve.memset(sums[:, :, :], 0.0))

                def slot(t):
                    if t.within(0, T):
                        dve.wait_ge(copied, t.n * 2 + 2)
                        if t.within(2, T):
                            dve.wait_ge(an_out[t.par], t.pair * 16)
                            dve.wait_ge(summed, t.n - 1)
                        dve.tensor_tensor(an[:, t.par], at[:, t.par], a_sb[:, :, bass.ts(t.n, P)],
                                          ALU.add).then_inc(added, 1)
                        dve.wait_ge(added, t.n + 1)
                        dve.tensor_scalar(an[:, t.par], an[:, t.par], 0.5, 0.0, ALU.mult,
                                          ALU.max).then_inc(normed, 1)
                        if t.within(2, T):
                            dve.wait_ge(mask_out[t.par], t.pair * 32)
                        dve.tensor_scalar(mt[:, t.par], at[:, t.par], 0.0, None, ALU.not_equal)
                        dve.tensor_scalar(mr[:, t.par], stage[:, t.par], 0.0, None,
                                          ALU.not_equal).then_inc(masked, 1)
                        if t.within(1, T):
                            dve.wait_ge(read, t.n)
                        dve.tensor_reduce(small[:, 0], at[:, t.par], AX.X, ALU.add).then_inc(reduced, 1)
                        dve.wait_ge(reduced, t.n + 1)
                        dve.tensor_tensor(col, col, small[:, 0], ALU.add).then_inc(read, 1)
                    if t.within(1, T + 1):
                        u = t - 1
                        dve.wait_ge(summed, u.n + 1)
                        dve.tensor_scalar(sums[:, 0, bass.ds(u.n, 1)], pst[:, u.par, 0:1], 1.0, None, ALU.mult)
                        dve.tensor_scalar(sums[:, 1, bass.ds(u.n, 1)], pst[:, u.par, 1:2], 1.0, None,
                                          ALU.mult).then_inc(sums_read, 1)
                run_slots(dve, slot, T + 1)
                dve.wait_ge(an_out[0], 16 * HALF)
                dve.wait_ge(summed, T)
                for t in range(T):
                    last = dve.tensor_tensor(an[:, 0, t, :], a_sb[:, t, t * P:(t + 1) * P], ident[:, :], ALU.mult)
                last.then_inc(ready, 1)
                dve.wait_ge(ready, 1)
                dve.tensor_reduce(dia, an[:, 0], AX.X, ALU.add).then_inc(ready, 1)
                dve.wait_ge(read, T)
                dve.wait_ge(sums_read, T)
                dve.tensor_copy(keep["rs"][:, :], row)
                positive, safe, deg = small[:, 0], small[:, 1], small[:, 2]
                dve.tensor_scalar(positive, sym, 0.0, None, ALU.is_gt).then_inc(ready, 1)
                dve.wait_ge(ready, 3)
                dve.tensor_scalar(safe, positive, -1.0, 1.0, ALU.mult, ALU.add).then_inc(ready, 1)
                dve.tensor_tensor(small[:, 3], sym, positive, ALU.mult).then_inc(ready, 1)
                dve.wait_ge(ready, 5)
                dve.tensor_tensor(safe, safe, small[:, 3], ALU.add).then_inc(ready, 1)
                dve.scalar_tensor_tensor(deg, row, 1.0, col, ALU.add, ALU.add).then_inc(ready, 1)
                dve.wait_ge(ready, 7)
                dve.tensor_tensor(deg, deg, dia, ALU.subtract).then_inc(ready, 1)
                dve.wait_ge(powered, 3)
                dve.tensor_tensor(keep["dinv"][:, :], small[:, 3], positive, ALU.mult).then_inc(ready, 1)
                dve.wait_ge(ready, 9)
                dve.tensor_scalar(keep["ndinv"][:, :], keep["dinv"][:, :], -1.0, None, ALU.mult)

            @block.gpsimd
            def _(pool):
                pool.memset(keep["halves"][:, :], -0.5).then_inc(powered, 1)
                pool.wait_ge(powered, 1)
                pool.wait_ge(ready, 8)
                pool.tensor_tensor(small[:, 3], small[:, 1], keep["halves"][:, :], ALU.pow).then_inc(powered, 1)
                pool.tensor_tensor(keep["dinv3"][:, :], small[:, 2], keep["halves"][:, :],
                                   ALU.pow).then_inc(powered, 1)

            @block.tensor
            def _(pe):
                def slot(t):
                    if t.within(0, T):
                        pe.wait_ge(staged, t.n + 1)
                        for h in range(2):
                            if t.within(1, T):
                                pe.wait_ge(copied, t.n * 2 + h - 1)
                            for c in range(HALF):
                                last = pe.transpose(pt[:, h, c], stage[:, t.par, h * HALF + c], ident[:, :])
                            last.then_inc(turned, 1)
                    if t.within(1, T + 1):
                        u = t - 1
                        if u.within(2, T):
                            pe.wait_ge(sums_read, u.n - 1)
                        pe.wait_ge(normed, u.n + 1)
                        for c in range(T):
                            pe.matmul(pst[:, u.par, 0:1], an[:, u.par, c], keep["ones"][:, 0:1],
                                      start=(c == 0), stop=(c == T - 1))
                        for c in range(T):
                            last = pe.matmul(pst[:, u.par, 1:2], at[:, u.par, c], keep["ones"][:, 0:1],
                                             start=(c == 0), stop=(c == T - 1))
                        last.then_inc(summed, 1)
                run_slots(pe, slot, T + 1)
                pe.wait_ge(sums_read, T)
                pe.transpose(pst[0:T, 0, 0:P], sums[:, 1], ident[:, :]).then_inc(rs_turned, 1)


def product(prog, io, keep, name, adj_d, h_in, weights, kind, x_in_d=None):
    nc = prog.nc
    scale = {"L0": keep["dinv"], "L3": keep["dinv3"]}.get(kind)
    uses_h = kind in ("L0", "L3")
    uses_x = kind == "L0"
    with ExitStack() as ctx:
        n_ = lambda s: f"{name}_{s}"
        g_hi = prog.sb(ctx, n_("g_hi"), [P, T, W], F32R)
        g_lo = prog.sb(ctx, n_("g_lo"), [P, T, W], F32R)
        a_raw = prog.sb(ctx, n_("a_raw"), [P, T, P])
        a_hi = prog.sb(ctx, n_("a_hi"), [P, 2, T, P], F32R)
        a_lo = prog.sb(ctx, n_("a_lo"), [P, 2, T, P], F32R)
        v = prog.sb(ctx, n_("v"), [P, B, D])
        ut = prog.sb(ctx, n_("ut"), [P, B, P])
        ht = prog.sb(ctx, n_("ht"), [P, 2, B, D])
        xt = prog.sb(ctx, n_("xt"), [P, 2, B, D]) if uses_x else None
        hn = prog.sb(ctx, n_("hn"), [P, B, D]) if kind != "L3" else None
        wsb = prog.sb(ctx, n_("w"), [P, weights["w"].shape[1]])
        acc = prog.ps(ctx, n_("acc"), [P, 2, W])
        pt = prog.ps(ctx, n_("pt"), [P, B, P])
        po = prog.ps(ctx, n_("po"), [P, B, D])
        ln = LayerNorm(prog, ctx, n_("ln"), B) if uses_x else None
        tmp = prog.sb(ctx, n_("tmp"), [P, B, D]) if kind == "L0" else None
        ident = keep["ident"]
        LAG = 2 if kind == "L0" else 1
        slots = (T + LAG, 2, 2 + LAG)

        w_in = prog.sem(n_("w_in"))
        g_in = prog.sems(n_("g_in"))
        g_high = prog.sem(n_("g_high"))
        g_low = prog.sem(n_("g_low"))
        a_in = prog.sem(n_("a_in"))
        a_high = prog.sem(n_("a_high"))
        a_low = prog.sem(n_("a_low"))
        h_in_s = prog.sems(n_("h_in"))
        x_in_s = prog.sems(n_("x_in")) if uses_x else None
        multiplied = prog.sem(n_("multiplied"))
        evacuated = prog.sem(n_("evacuated"))
        turned = prog.sem(n_("turned"))
        ut_ready = prog.sem(n_("ut_ready"))
        projected = prog.sem(n_("projected"))
        po_read = prog.sem(n_("po_read"))
        x_done = prog.sem(n_("x_done"))
        h_done = prog.sem(n_("h_done"))
        x_out = prog.sems(n_("x_out"))
        h_out = prog.sem(n_("h_out"))
        own = prog.sem(n_("own"))
        own2 = prog.sem(n_("own2"))
        projected_s = prog.sem(n_("projected_s"))
        halves = 2 if kind == "L3" else 1
        extra = {}
        n_w = 1
        if kind == "L0":
            extra["wa"] = keep["wa"]
        if kind == "L2a":
            extra["brow"] = prog.sb(ctx, n_("brow"), [P, D])
            n_w = 2
        if kind == "L2b":
            extra["bcol"] = prog.sb(ctx, n_("bcol"), [P, 1])
            extra["rsrow"] = prog.sb(ctx, n_("rsrow"), [P, N])
            n_w = 3
        small = prog.sb(ctx, n_("small"), [P, 2, B])
        block = ctx.enter_context(nc.Block())

        @block.sync
        def _(sp):
            sp.dma_start(a_raw[:, :, :], adj_d[0]).then_inc(a_in, 16)
            for s in range(T):
                if s >= 2:
                    sp.wait_ge(g_low, s - 1)
                sp.dma_start(ht[:, s % 2], h_in[s]).then_inc(g_in[s % 2], 16)
                if s == 1:
                    sp.dma_start(wsb[:, :], weights["w"]).then_inc(w_in, 16)
                    if kind == "L2a":
                        sp.dma_start(extra["brow"][:, :], weights["b"].partition_broadcast(P)).then_inc(w_in, 16)
                    if kind == "L2b":
                        sp.dma_start(extra["bcol"][:, :], weights["b"]).then_inc(w_in, 16)
                        sp.dma_start(extra["rsrow"][:, :],
                                     io["rsrow"].rearrange("t j -> (t j)").partition_broadcast(P)).then_inc(w_in, 16)

            def slot(t):
                if t.within(0, T - 1):
                    sp.wait_ge(a_high, t.n + 1)
                    sp.wait_ge(a_low, t.n + 1)
                    sp.dma_start(a_raw[:, :, :], adj_d[t.n + 1]).then_inc(a_in, 16)
                if t.within(LAG, T + LAG):
                    u = t - LAG
                    if uses_x:
                        sp.wait_ge(x_done, u.n + 1)
                        sp.dma_start(io["x1"][u.n], xt[:, u.par]).then_inc(x_out[u.par], 16)
                    if kind in ("L0", "L2a"):
                        sp.wait_ge(h_done, u.n + 1)
                        sp.dma_start(io["h1" if kind == "L0" else "h2b"][u.n], hn[:, :, :]).then_inc(h_out, 16)
                    if kind == "L2b":
                        sp.wait_ge(h_done, u.n + 1)
                        sp.dma_start(io["hT"].rearrange("b f (t j) -> t f b j", j=P)[u.n],
                                     hn[:, :, :]).then_inc(h_out, 16)
                    if kind == "L3":
                        sp.wait_ge(ut_ready, u.n + 1)
                        sp.dma_start(io["aggT"][u.n], ut[:, :, :]).then_inc(h_out, 16)
                if t.within(0, T):
                    if uses_h:
                        if t.within(2, T):
                            sp.wait_ge(evacuated, t.n - 1)
                        else:
                            sp.wait_ge(g_low, T)
                        sp.dma_start(ht[:, t.par], h_in[t.n]).then_inc(h_in_s[t.par], 16)
                    if uses_x:
                        if t.within(2, T):
                            sp.wait_ge(x_out[t.par], t.pair * 16)
                            sp.wait_ge(h_done, t.n - 1)
                        sp.dma_start(xt[:, t.par], x_in_d[t.n]).then_inc(x_in_s[t.par], 16)
            run_slots(sp, slot, *slots)
            if uses_x:
                for s in x_out:
                    sp.wait_ge(s, 16 * HALF)
            sp.wait_ge(h_out, 16 * T)

        @block.scalar
        def _(act):
            def split(t):
                if t.within(2, T):
                    act.wait_ge(multiplied, t.n - 1)
                act.wait_ge(a_in, t.n * 16 + 16)
                act.activation(a_hi[:, t.par], a_raw[:, :, :], ACT.Copy).then_inc(a_high, 1)

            split(Tile(0))
            for s in range(T):
                act.wait_ge(g_in[s % 2], 16 * (s // 2 + 1))
                sc = 1.0 if scale is None else scale[:, s:s + 1]
                act.activation(g_hi[:, s], ht[:, s % 2].rearrange("p b f -> p (b f)"), ACT.Copy,
                               scale=sc).then_inc(g_high, 1)

            def slot(t):
                if t.within(0, T - 1):
                    split(t + 1)
                if uses_x and t.within(LAG, T + LAG):
                    u = t - LAG
                    if u.within(1, T):
                        act.wait_ge(h_out, u.n * 16)
                        act.wait_ge(projected_s, u.n)
                    ln.scalar(act, u.n, xt[:, u.par], hn[:, :, :], h_done)
                if t.within(1, T + 1):
                    u = t - 1
                    act.wait_ge(turned, u.n + 1)
                    if u.within(1, T):
                        act.wait_ge(projected, u.n * halves)
                        if kind == "L3":
                            act.wait_ge(h_out, u.n * 16)
                    act.activation(ut[:, :, :], pt[:, :, :], ACT.Copy).then_inc(ut_ready, 1)
            run_slots(act, slot, *slots)

        if uses_x:
            @block.gpsimd
            def _(pool):
                ln.pool_setup(pool)
                run_slots(pool, lambda t: ln.pool(pool, t.n, h_done, t.within(1, T)), T, 2, 2)

        @block.vector
        def _(dve):
            links = Chain(dve, own, {"L0": 4, "L2a": 1, "L2b": 1, "L3": 0}[kind])
            evac_link = Chain(dve, own2, 1)

            def split(t):
                if t.within(2, T):
                    dve.wait_ge(multiplied, t.n - 1)
                dve.wait_ge(a_high, t.n + 1)
                dve.tensor_tensor(a_lo[:, t.par], a_raw[:, :, :], a_hi[:, t.par].bitcast(F32),
                                  ALU.subtract).then_inc(a_low, 1)

            split(Tile(0))
            for s in range(T):
                dve.wait_ge(g_high, s + 1)
                h2 = ht[:, s % 2].rearrange("p b f -> p (b f)")
                if scale is None:
                    dve.tensor_tensor(g_lo[:, s], h2, g_hi[:, s].bitcast(F32), ALU.subtract).then_inc(g_low, 1)
                else:
                    dve.scalar_tensor_tensor(g_lo[:, s], h2, scale[:, s:s + 1], g_hi[:, s].bitcast(F32),
                                             ALU.mult, ALU.subtract).then_inc(g_low, 1)
            dve.wait_ge(w_in, 16 * n_w)

            def evacuate(u):
                a2 = acc[:, u.par].rearrange("p (b f) -> p b f", f=D)
                if u.within(1, T):
                    dve.wait_ge(turned, u.n)
                if uses_h:
                    dve.wait_ge(h_in_s[u.par], u.pair * 16 + 16)
                dve.wait_ge(multiplied, u.n + 1)
                if kind == "L0":
                    dve.scalar_tensor_tensor(v[:, :, :], a2, keep["ndinv"][:, bass.ds(u.n, 1)], ht[:, u.par],
                                             ALU.mult, ALU.add).then_inc(evacuated, 1)
                elif kind == "L3":
                    evac_link.step(u.n)
                    evac_link.link(dve.scalar_tensor_tensor(
                        v[:, :, :], ht[:, u.par], keep["dinv3"][:, bass.ds(u.n, 1)], a2, ALU.mult, ALU.add))
                    dve.tensor_scalar(v[:, :, :], v[:, :, :], keep["dinv3"][:, bass.ds(u.n, 1)], None,
                                      ALU.mult).then_inc(evacuated, 1)
                else:
                    dve.tensor_copy(v[:, :, :], a2).then_inc(evacuated, 1)

            def tail(u, part):
                if kind == "L0" and part == 1:
                    links.step(u.n)
                    dve.wait_ge(h_done, u.n + 1)
                    for j, col in ((0, keep["s1"]), (1, keep["s2"])):
                        wa = extra["wa"][:, j].unsqueeze(1).to_broadcast([P, B, D])
                        links.link(dve.tensor_tensor(tmp[:, :, :], hn[:, :, :], wa, ALU.mult))
                        links.link(dve.tensor_reduce(small[:, j, :], tmp[:, :, :], AX.X, ALU.add))
                        ins = dve.tensor_scalar(col[:, :, bass.ds(u.n, 1)], small[:, j, :].unsqueeze(2), 1.0,
                                                None, ALU.mult)
                    ins.then_inc(projected_s, 1)
                if part == 1:
                    return
                links.step(u.n)
                if kind == "L0":
                    dve.wait_ge(x_in_s[u.par], u.pair * 16 + 16)
                    dve.wait_ge(projected, u.n + 1)
                    dve.scalar_tensor_tensor(xt[:, u.par], po[:, :, :], 0.0, xt[:, u.par],
                                             ALU.max, ALU.add).then_inc(x_done, 1)
                    dve.wait_ge(x_done, u.n + 1)
                    ln.vector(dve, u.n, xt[:, u.par], u.within(1, T))
                if kind in ("L2a", "L2b"):
                    dve.wait_ge(projected, u.n + 1)
                    if u.within(1, T):
                        dve.wait_ge(h_out, u.n * 16)
                    if kind == "L2a":
                        bias = extra["brow"][:, :].unsqueeze(1).to_broadcast([P, B, D])
                        s = keep["rs"][:, bass.ds(u.n, 1)]
                    else:
                        bias = extra["rsrow"][:, bass.ts(u.n, P)].unsqueeze(1).to_broadcast([P, B, P])
                        s = extra["bcol"][:, 0:1]
                    links.link(dve.scalar_tensor_tensor(hn[:, :, :], bias, s, po[:, :, :], ALU.mult, ALU.add))
                    dve.tensor_scalar(hn[:, :, :], hn[:, :, :], 0.0, None, ALU.max).then_inc(h_done, 1)
                if kind == "L3":
                    for k in range(2):
                        dve.wait_ge(projected, u.n * 2 + k + 1)
                        for c in range(2):
                            last = dve.bn_stats(keep["bn1"][:, k, bass.ds(u.n * 2 + c, 1), :].squeeze(1),
                                                po[:, 4 * c:4 * c + 4, :].rearrange("p b f -> p (b f)"))
                        last.then_inc(po_read, 1)

            def slot(t):
                if t.within(1, T + 1):
                    evacuate(t - 1)
                if t.within(LAG, T + LAG):
                    tail(t - LAG, 0)
                if t.within(0, T - 1):
                    split(t + 1)
                if t.within(LAG, T + LAG):
                    tail(t - LAG, 1)
            run_slots(dve, slot, *slots)

        @block.tensor
        def _(pe):
            pe.wait_ge(w_in, 16 * n_w)

            def main(t, s0, s1):
                if s0 == 0:
                    if t.within(2, T):
                        pe.wait_ge(evacuated, t.n - 1)
                    pe.wait_ge(a_low, t.n + 1)
                for s in range(s0, s1):
                    if t.i is None and t.off == 0:
                        pe.wait_ge(g_low, s + 1)
                    for lhs, rhs in ((a_hi, g_hi), (a_hi, g_lo), (a_lo, g_hi)):
                        for c in range(2):
                            last = pe.matmul(acc[:, t.par, c * 512:(c + 1) * 512], lhs[:, t.par, s],
                                             rhs[:, s, c * 512:(c + 1) * 512],
                                             start=(s == 0 and lhs is a_hi and rhs is g_hi),
                                             stop=(s == T - 1 and lhs is a_lo))
                if s1 == T:
                    last.then_inc(multiplied, 1)

            def turn(u):
                pe.wait_ge(evacuated, u.n + 1)
                if u.within(1, T):
                    pe.wait_ge(ut_ready, u.n)
                for b in range(B):
                    last = pe.transpose(pt[:, b], v[:, b], ident[:, :])
                last.then_inc(turned, 1)

            def project(u, k):
                pe.wait_ge(ut_ready, u.n + 1)
                if kind == "L3":
                    if k == 1 or u.within(1, T):
                        pe.wait_ge(po_read, u.n * 2 + k)
                elif u.within(1, T):
                    pe.wait_ge(x_done if kind == "L0" else h_done, u.n)
                if kind in ("L0", "L2a"):
                    for b in range(B):
                        last = pe.matmul(po[:, b], ut[:, b], wsb[:, :], start=True, stop=True)
                else:
                    for c in range(2):
                        last = pe.matmul(po[:, 4 * c:4 * c + 4], wsb[:, k * P:(k + 1) * P],
                                         ut[:, 4 * c:4 * c + 4], start=True, stop=True)
                last.then_inc(projected, 1)

            def slot(t):
                pieces = [(0, 5), (5, 11), (11, T)]
                for j, (s0, s1) in enumerate(pieces):
                    if t.within(0, T):
                        main(t, s0, s1)
                    if t.within(1, T + 1):
                        if j == 0:
                            turn(t - 1)
                        elif j - 1 < halves:
                            project(t - 1, j - 1)
            run_slots(pe, slot, *slots)


def attention(prog, io, keep, weights):
    nc = prog.nc
    BANK = 3
    NBANK = -(-T // BANK)
    QUARTERS, QT = 4, T // 4
    TURN, PROJECT, COPY, ADD = ([k + 2 * q for q in range(QUARTERS)] for k in (2, 3, 4, 5))
    MEASURE, NORMALISE, MAXIMA, TURN_ROWS, COPY_ROWS = 12, {13: (0, 6), 14: (6, 11), 15: (11, 16)}, 8, 10, 11
    batch_view = lambda d: d.rearrange("t p b f -> b p t f")
    with ExitStack() as ctx:
        mrow = prog.sb(ctx, "c_mrow", [P, T, N], U8)
        mT = prog.sb(ctx, "c_mT", [P, T, T, P], U8)
        hb = prog.sb(ctx, "c_hb", [P, 2, T, D + 1])
        s2row = prog.sb(ctx, "c_s2row", [P, N])
        rows = prog.sb(ctx, "c_rows", [P, 2, 2, N])
        z = prog.sb(ctx, "c_z", [P, 2, N])
        e = prog.sb(ctx, "c_e", [P, 2, N])
        pr = prog.sb(ctx, "c_p", [P, 2, N])
        u = prog.sb(ctx, "c_u", [P, T, D])
        ut = prog.sb(ctx, "c_ut", [P, QT, P])
        xt = prog.sb(ctx, "c_xt", [P, T, D])
        hn = prog.sb(ctx, "c_hn", [P, T, D])
        wsb = prog.sb(ctx, "c_w", [P, D])
        cols = prog.sb(ctx, "c_cols", [P, 2, 2, T])
        mtmp = prog.sb(ctx, "c_mtmp", [P, 3, T])
        low = prog.sb(ctx, "c_low", [P, 2])
        rcol = prog.sb(ctx, "c_rcol", [P, 2, T])
        rT = prog.sb(ctx, "c_rT", [2 * T, P])
        s2T = prog.sb(ctx, "c_s2T", [P, P])
        rec = prog.sb(ctx, "c_rec", [P, NBANK * BANK])
        ends = prog.sb(ctx, "c_ends", [P, 2])
        all_ends = prog.sb(ctx, "c_all_ends", [P, B, T, 2])
        bounds = prog.sb(ctx, "c_bounds", [P, 3, B])
        wide = prog.sb(ctx, "c_wide", [P, 1])
        is_wide = prog.sb(ctx, "c_is_wide", [P, 1], I32)
        acc = prog.ps(ctx, "c_acc", [P, NBANK, 512])
        pq = prog.ps(ctx, "c_pq", [P, 2, 512])
        ln = LayerNorm(prog, ctx, "cln", T)
        ident = keep["ident"]
        sem, sems = (lambda s: prog.sem(f"c_{s}")), (lambda s: prog.sems(f"c_{s}"))
        w_in, ones_set, mT_in, mrow_in = sem("w_in"), sem("ones_set"), sem("mT_in"), sem("mrow_in")
        s2_turned, s2_copied, s2_out = sem("s2_turned"), sem("s2_copied"), sem("s2_out")
        ends_ready, ends_out, ends_in, bounds_ready = (sem(k) for k in (
            "ends_ready", "ends_out", "ends_in", "bounds_ready"))
        h_in, row_in = sems("h_in"), sem("row_in")
        max_own, maxed = sem("max_own"), sem("maxed")
        r_turned, r_copied, r_out, r_in = sem("r_turned"), sem("r_copied"), sem("r_out"), sems("r_in")
        z_ready, exped, masked, used = sem("z_ready"), sem("exped"), sem("masked"), sem("used")
        rec_own, normed = sem("rec_own"), sem("normed")
        u_turned, ut_ready, projected = sem("u_turned"), sem("ut_ready"), sem("projected")
        x_in, x_done, x_out = sem("x_in"), sem("x_done"), sem("x_out")
        h_done, h_out = sem("h_done"), sem("h_out")
        block = ctx.enter_context(nc.Block())

        def batches(eng, slot):
            run_slots(eng, slot, B + 1, 2, 3)

        @block.sync
        def _(sp):
            sp.dma_start(wsb[:, :], weights).then_inc(w_in, 16)
            sp.wait_ge(s2_copied, 1)
            sp.dma_start(io["s2row"], s2T[:, :]).then_inc(s2_out, 16)
            sp.wait_ge(ends_ready, 2)
            sp.dma_start(io["ends"], ends[:, :]).then_inc(ends_out, 16)
            sp.wait_ge(ends_out, 16)
            sp.dma_start(all_ends[:, :, :, :].rearrange("p b t k -> p (b t k)"),
                         io["ends"].rearrange("r k -> (r k)").partition_broadcast(P)).then_inc(ends_in, 16)
            sp.wait_ge(s2_out, 16)

            def inputs(b):
                if b.within(1, B):
                    sp.wait_ge(maxed, b.n * (T + 1))
                sp.dma_start(s2row[:, :], io["s2row"].rearrange("(b t) j -> b (t j)", b=B)[b.n]
                             .partition_broadcast(P)).then_inc(row_in, 16)
                if b.within(2, B):
                    sp.wait_ge(used, b.n * T - T)
                sp.dma_start(hb[:, b.par, :, 0:D], batch_view(io["h1"])[b.n]).then_inc(h_in[b.par], 16)

            def spread_rows(b):
                sp.wait_ge(r_copied, b.n + 1)
                sp.dma_start(io["rrow"], rT[:, :]).then_inc(r_out, 16)
                sp.wait_ge(r_out, b.n * 16 + 16)
                if b.within(2, B):
                    sp.wait_ge(z_ready, b.n * T - T)
                for k in range(2):
                    sp.dma_start(rows[:, b.par, k], io["rrow"].rearrange("(k t) j -> k (t j)", k=2)[k]
                                 .partition_broadcast(P)).then_inc(r_in[b.par], 16)

            def store(b):
                sp.wait_ge(h_done, b.n + 1)
                sp.dma_start(batch_view(io["h2"])[b.n], hn[:, :, :]).then_inc(h_out, 16)
                sp.dma_start(batch_view(io["x2"])[b.n], xt[:, :, :]).then_inc(x_out, 16)

            inputs(Tile(0))
            spread_rows(Tile(0))

            def slot(b):
                if b.within(0, B - 1):
                    inputs(b + 1)
                if b.within(2, B + 1):
                    store(b - 2)
                if b.within(1, B + 1):
                    if b.within(2, B + 1):
                        sp.wait_ge(x_out, b.n * 16 - 16)
                    sp.dma_start(xt[:, :, :], batch_view(io["x1"])[b.n - 1]).then_inc(x_in, 16)
                if b.within(0, B - 1):
                    spread_rows(b + 1)
            batches(sp, slot)
            store(Tile(B - 1))
            sp.wait_ge(mrow_in, 16 * T)
            sp.wait_ge(x_out, 16 * B)
            sp.wait_ge(h_out, 16 * B)

        @block.gpsimd
        def _(pool):
            ln.pool_setup(pool)
            pool.memset(hb[:, :, :, D:D + 1], 1.0).then_inc(ones_set, 1)
            run_slots(pool, lambda b: ln.pool(pool, b.n, h_done, b.within(1, B)), B, 2, 2)

        @block.scalar
        def _(act):
            for t in range(T):
                act.dma_start(mT[:, t], io["mT"][t]).then_inc(mT_in, 16)
            for t in range(T):
                act.dma_start(mrow[:, t], io["mrow"][t].rearrange("p c j -> p (c j)")).then_inc(mrow_in, 16)
            act.wait_ge(s2_turned, 1)
            act.activation(s2T[:, :], pq[:, 0, 0:P], ACT.Copy).then_inc(s2_copied, 1)

            def copy_rows(b):
                act.wait_ge(r_turned, b.n + 1)
                act.activation(rT[:, :], pq[0:2 * T, 0, 0:P], ACT.Copy).then_inc(r_copied, 1)

            def copy_turned(b, q):
                act.wait_ge(u_turned, b.n * QUARTERS + q + 1)
                act.activation(ut[:, :, :], pq[:, 0, :].rearrange("p (c j) -> p c j", j=P),
                               ACT.Copy).then_inc(ut_ready, 1)

            def normalise(b, blocks):
                if blocks[0] == 0 and b.within(1, B):
                    act.wait_ge(h_out, b.n * 16)
                ln.scalar(act, b.n, xt[:, :, :], hn[:, :, :], h_done, blocks)

            copy_rows(Tile(0))

            def slot(b):
                for j in range(T):
                    if b.within(0, B):
                        act.wait_ge(z_ready, b.n * T + j + 1)
                        if j >= 2 or b.within(1, B):
                            act.wait_ge(masked, b.n * T + j - 1)
                        act.activation(e[:, j % 2], z[:, j % 2], ACT.Exp,
                                       bias=cols[:, b.par, 0, j:j + 1]).then_inc(exped, 1)
                    if b.within(1, B + 1) and j in COPY:
                        copy_turned(b - 1, COPY.index(j))
                    if b.within(0, B - 1) and j == COPY_ROWS:
                        copy_rows(b + 1)
                    if b.within(1, B + 1) and j in NORMALISE:
                        normalise(b - 1, NORMALISE[j])
            batches(act, slot)

        @block.vector
        def _(dve):
            greatest, least, distance = (bounds[:, k] for k in range(3))

            dve.wait_ge(s2_copied, 1)
            dve.tensor_reduce(ends[:, 0:1], s2T[:, :], AX.X, ALU.max).then_inc(ends_ready, 1)
            dve.tensor_reduce(ends[:, 1:2], s2T[:, :], AX.X, ALU.min).then_inc(ends_ready, 1)
            dve.wait_ge(ends_in, 16)
            dve.tensor_reduce(greatest, all_ends[:, :, :, 0], AX.X, ALU.max)
            dve.tensor_reduce(least, all_ends[:, :, :, 1], AX.X, ALU.min).then_inc(bounds_ready, 1)
            dve.wait_ge(bounds_ready, 1)
            dve.tensor_tensor(distance, greatest, least, ALU.subtract).then_inc(bounds_ready, 1)
            dve.wait_ge(bounds_ready, 2)
            dve.tensor_reduce(wide[:, :], distance, AX.X, ALU.max).then_inc(bounds_ready, 1)
            dve.wait_ge(bounds_ready, 3)
            dve.tensor_scalar(is_wide[:, :], wide[:, :], SPREAD, None, ALU.is_gt).then_inc(bounds_ready, 1)
            dve.wait_ge(bounds_ready, 4)
            wide_flag = dve.value_load(is_wide[0:1, 0:1], min_val=0, max_val=1)

            def maxima(b):
                m, tmp, carrier = (mtmp[:, k] for k in range(3))
                s1, s2 = keep["s1"][:, b.n, :], keep["s2"][:, b.n, :]
                own = Chain(dve, max_own, 5)
                own.step(b.n)
                own.link(dve.tensor_scalar(low[:, 0:2], bounds[:, 1:3, bass.ds(b.n, 1)].squeeze(2), 1.0, None,
                                           ALU.mult))
                if b.within(2, B):
                    dve.wait_ge(exped, b.n * T - T)
                dve.tensor_scalar(cols[:, b.par, 0], s2, 1.0, None, ALU.mult)
                dve.wait_ge(row_in, b.n * 16 + 16)
                dve.tensor_scalar(cols[:, b.par, 1], s2, ALPHA - 1.0, None, ALU.mult)
                with dve.If(wide_flag == 0):
                    dve.tensor_scalar(m, keep["ones"][:, 0:1].to_broadcast([P, T]), low[:, 1:2], None,
                                      ALU.mult).then_inc(maxed, T + 1)
                with dve.Else():
                    dve.wait_ge(mrow_in, 16 * T)
                    dve.tensor_scalar(s2row[:, :], s2row[:, :], low[:, 0:1], None,
                                      ALU.subtract).then_inc(maxed, 1)
                    for t in range(T):
                        dve.wait_ge(maxed, b.n * (T + 1) + t + 1)
                        dve.memset(carrier[:, t:t + 1], 0.0)
                        dve.tensor_tensor_reduce(rows[:, b.par, t % 2], s2row[:, :], mrow[:, t], 1.0, 0.0,
                                                 ALU.mult, ALU.max, m[:, t:t + 1]).then_inc(maxed, 1)
                dve.wait_ge(maxed, (b.n + 1) * (T + 1))
                own.link(dve.scalar_tensor_tensor(tmp, m, low[:, 0:1], s1, ALU.add, ALU.add))
                own.link(dve.scalar_tensor_tensor(m, tmp, ALPHA, tmp, ALU.mult, ALU.max))
                dve.tensor_tensor(rcol[:, 0], s1, m, ALU.subtract)
                own.link(dve.tensor_scalar(tmp, s1, ALPHA, None, ALU.mult))
                own.link(dve.tensor_tensor(rcol[:, 1], tmp, m, ALU.subtract))

            def exponents(b, j):
                if j == 0:
                    dve.wait_ge(r_in[b.par], b.pair * 32 + 32)
                if j >= 2 or b.within(1, B):
                    dve.wait_ge(exped, b.n * T + j - 1)
                dve.scalar_tensor_tensor(z[:, j % 2], rows[:, b.par, 1], cols[:, b.par, 1, j:j + 1],
                                         rows[:, b.par, 0], ALU.add, ALU.max).then_inc(z_ready, 1)

            def mask(b, j):
                if j == 0 and b.off == 0 and b.i is None:
                    dve.wait_ge(mT_in, 16 * T)
                dve.wait_ge(exped, b.n * T + j + 1)
                if j >= 2 or b.within(1, B):
                    dve.wait_ge(used, b.n * T + j - 1)
                dve.tensor_tensor(pr[:, j % 2].rearrange("p (c i) -> p c i", i=P),
                                  e[:, j % 2].rearrange("p (c i) -> p c i", i=P), mT[:, :, j],
                                  ALU.mult).then_inc(masked, 1)

            def divide(b):
                own = Chain(dve, rec_own, NBANK)
                own.step(b.n)
                dve.wait_ge(used, b.n * T + T)
                for k in range(NBANK):
                    n = min(BANK, T - k * BANK)
                    a3 = acc[:, k, 0:n * (D + 1)].rearrange("p (c j) -> p c j", j=D + 1)
                    own.link(dve.reciprocal(rec[:, k * BANK:k * BANK + n], a3[:, :, D]))
                    dve.tensor_tensor(u[:, k * BANK:k * BANK + n], a3[:, :, 0:D],
                                      over(rec[:, k * BANK:k * BANK + n], D), ALU.mult).then_inc(normed, 1)

            def add(b, q):
                if q == 0:
                    dve.wait_ge(x_in, b.n * 16 + 16)
                dve.wait_ge(projected, b.n * QUARTERS + q + 1)
                xq = xt[:, QT * q:QT * q + QT]
                dve.tensor_tensor(xq, pq[:, 1, :].rearrange("p (c j) -> p c j", j=D), xq, ALU.add)\
                   .then_inc(x_done, 1)

            maxima(Tile(0))

            def slot(b):
                for j in range(T):
                    if b.within(0, B):
                        exponents(b, j)
                        if j >= 2:
                            mask(b, j - 1)
                    if b.within(1, B + 1) and j == 0:
                        mask(b - 1, T - 1)
                    if b.within(1, B + 1) and j == 1:
                        divide(b - 1)
                    if b.within(0, B) and j == 1:
                        mask(b, 0)
                    if b.within(1, B + 1) and j in ADD:
                        add(b - 1, ADD.index(j))
                    if b.within(1, B + 1) and j == MEASURE:
                        dve.wait_ge(x_done, b.n * QUARTERS)
                        ln.vector(dve, b.n - 1, xt[:, :, :], b.within(2, B + 1))
                    if b.within(0, B - 1) and j == MAXIMA:
                        maxima(b + 1)
            batches(dve, slot)

        @block.tensor
        def _(pe):
            pe.transpose(pq[:, 0, 0:P], keep["s2"][:, :, :].rearrange("p b t -> p (b t)"),
                         ident[:, :]).then_inc(s2_turned, 1)
            pe.wait_ge(w_in, 16)
            pe.wait_ge(ones_set, 1)
            pe.wait_ge(s2_copied, 1)

            def turn_rows(b):
                pe.wait_ge(max_own, b.n * 5 + 5)
                pe.transpose(pq[0:2 * T, 0, 0:P], rcol[:, :, :].rearrange("p k t -> p (k t)"),
                             ident[:, :]).then_inc(r_turned, 1)

            def accumulate(b, j):
                if j == 0:
                    pe.wait_ge(h_in[b.par], b.pair * 16 + 16)
                    if b.within(1, B):
                        pe.wait_ge(normed, b.n * NBANK)
                pe.wait_ge(masked, b.n * T + j + 1)
                for t in range(T):
                    k, o = t // BANK, (t % BANK) * (D + 1)
                    last = pe.matmul(acc[:, k, o:o + D + 1], pr[:, j % 2, t * P:(t + 1) * P],
                                     hb[:, b.par, j], start=(j == 0 and o == 0), stop=(j == T - 1),
                                     skip_group_check=True)
                last.then_inc(used, 1)

            def turn(b, q):
                if q == 0:
                    pe.wait_ge(normed, (b.n + 1) * NBANK)
                    pe.wait_ge(r_copied, b.n + 1)
                for c in range(QT):
                    last = pe.transpose(pq[:, 0, c * P:(c + 1) * P], u[:, QT * q + c], ident[:, :])
                last.then_inc(u_turned, 1)

            def project(b, q):
                pe.wait_ge(ut_ready, b.n * QUARTERS + q + 1)
                if q:
                    pe.wait_ge(x_done, b.n * QUARTERS + q)
                for c in range(QT):
                    last = pe.matmul(pq[:, 1, c * D:(c + 1) * D], ut[:, c], wsb[:, :], start=True, stop=True)
                last.then_inc(projected, 1)

            turn_rows(Tile(0))

            def slot(b):
                for j in range(T):
                    if b.within(0, B):
                        accumulate(b, j)
                    if b.within(1, B + 1) and j in TURN:
                        turn(b - 1, TURN.index(j))
                    if b.within(1, B + 1) and j in PROJECT:
                        project(b - 1, PROJECT.index(j))
                    if b.within(0, B - 1) and j == TURN_ROWS:
                        turn_rows(b + 1)
            batches(pe, slot)


def lstm_units():
    units = []
    for p in range(1, SKIP + 1):
        windows = N // p
        parts = -(-windows // 512)
        size = -(-windows // parts)
        size += size % 2
        for w0 in range(0, windows, size):
            for q in range(p):
                units.append((p, w0, min(size, windows - w0), q))
    return units


def recurrences(prog, io, keep, weights):
    nc = prog.nc
    units = lstm_units()
    NU = len(units)
    GATES = {True: (2, 0, 3), False: (2, 0, 1, 3)}
    gates = [GATES[q == 0] for _, _, _, q in units]
    before = [sum(len(g) for g in gates[:k]) for k in range(NU + 1)]
    NG = before[NU]
    level_end = {p: max((k for k, u in enumerate(units) if u[0] < p), default=-1) for p in range(1, SKIP + 1)}
    with ExitStack() as ctx:
        G4 = 4 * D
        w_hi = prog.sb(ctx, "r_w_hi", [P, 2, SKIP, G4], F32R)
        w_lo = prog.sb(ctx, "r_w_lo", [P, 2, SKIP, G4], F32R)
        bias = prog.sb(ctx, "r_bias", [P, 3, SKIP, 4])
        pair = range(2)
        hx = [prog.sb(ctx, f"r_hx{k}", [P, N]) for k in pair]
        hx_hi = [prog.sb(ctx, f"r_hx_hi{k}", [P, N], F32R) for k in pair]
        hx_lo = [prog.sb(ctx, f"r_hx_lo{k}", [P, N], F32R) for k in pair]
        gate = [prog.sb(ctx, f"r_gate{k}", [P, 4, 512]) for k in pair]
        cell = [prog.sb(ctx, f"r_cell{k}", [P, 2, 512]) for k in pair]
        tc = [prog.sb(ctx, f"r_tc{k}", [P, 512]) for k in pair]
        st = [prog.sb(ctx, f"r_st{k}", [P, 512]) for k in pair]
        st_hi = [prog.sb(ctx, f"r_st_hi{k}", [P, 512], F32R) for k in pair]
        st_lo = [prog.sb(ctx, f"r_st_lo{k}", [P, 512], F32R) for k in pair]
        xt = prog.sb(ctx, "r_xt", [P, T, D])
        hn = prog.sb(ctx, "r_hn", [P, T, D])
        ps = [prog.ps(ctx, f"r_ps{k}", [P, 4, 512]) for k in pair]
        ident = keep["ident"]
        ln = LayerNorm(prog, ctx, "rln", T)
        sem, sems = (lambda s: prog.sem(f"r_{s}")), (lambda s: prog.sems(f"r_{s}"))
        w_in, b_in, w_high, w_split = sem("w_in"), sem("b_in"), sem("w_high"), sem("w_split")
        b_own, b_ready = sem("b_own"), sem("b_ready")
        h_in, h_high, h_low = sems("h_in"), sems("h_high"), sems("h_low")
        summed, activated = sems("summed"), sems("activated")
        own, cell_ready, squashed = sems("own"), sems("cell_ready"), sems("squashed")
        state, high, low = sems("state"), sems("high"), sems("low")
        turned, x_in, x_done, x_out, h_done, h_out = (sem(s) for s in (
            "turned", "x_in", "x_done", "x_out", "h_done", "h_out"))
        batch_view = lambda d: d.rearrange("t p b f -> b p t f")
        with ExitStack() as c1:
            w_raw = prog.sb(c1, "r_w_raw", [P, 2, SKIP, G4])
            block = c1.enter_context(nc.Block())

            @block.sync
            def _(sp):
                for k, name in enumerate(("wih", "whh")):
                    sp.dma_start(w_raw[:, k], weights[name]).then_inc(w_in, 16)
                for k, name in enumerate(("bih", "bhh")):
                    sp.dma_start(bias[:, k], weights[name]).then_inc(b_in, 16)

            @block.scalar
            def _(act):
                act.wait_ge(w_in, 32)
                act.activation(w_hi[:, :, :, :], w_raw[:, :, :, :], ACT.Copy).then_inc(w_high, 1)

            @block.vector
            def _(dve):
                dve.wait_ge(b_in, 32)
                dve.tensor_tensor(bias[:, 2], bias[:, 0], bias[:, 1], ALU.add).then_inc(b_ready, 1)
                dve.wait_ge(w_high, 1)
                dve.tensor_tensor(w_lo[:, :, :, :], w_raw[:, :, :, :], w_hi[:, :, :, :].bitcast(F32),
                                  ALU.subtract).then_inc(w_split, 1)
        block = ctx.enter_context(nc.Block())
        NPAIR = B // 2

        def pairs(eng, slot):
            slot(0, True)
            with eng.Fori(1, NPAIR) as i:
                slot(i, False)

        def turns():
            for n in range(NU):
                for k in pair:
                    yield n, k

        @block.sync
        def _(sp):
            def slot(i, first):
                for k in pair:
                    if not first:
                        sp.wait_ge(x_done, i * 2 - 1 + k)
                    sp.dma_start(hx[k][:, :], io["hT"][i * 2 + k]).then_inc(h_in[k], 16)
                for k in pair:
                    if not first or k:
                        sp.wait_ge(x_out, (i * 2 + k) * 16)
                        sp.wait_ge(h_done, i * 2 + k)
                    sp.dma_start(xt[:, :, :], batch_view(io["x2"])[i * 2 + k]).then_inc(x_in, 16)
                    sp.wait_ge(x_done, i * 2 + k + 1)
                    sp.dma_start(batch_view(io["x3"])[i * 2 + k], xt[:, :, :]).then_inc(x_out, 16)
                    sp.wait_ge(h_done, i * 2 + k + 1)
                    sp.dma_start(batch_view(io["h3"])[i * 2 + k], hn[:, :, :]).then_inc(h_out, 16)
            pairs(sp, slot)
            sp.wait_ge(x_out, 16 * B)
            sp.wait_ge(h_out, 16 * B)

        @block.gpsimd
        def _(pool):
            ln.pool_setup(pool)
            ln.pool(pool, 0, h_done, False)
            with pool.Fori(1, B) as b:
                ln.pool(pool, b, h_done, True)

        def places(n):
            p, w0, size, q = units[n]
            return slice(w0 * p + q, w0 * p + q + (size - 1) * p + 1, p)

        @block.scalar
        def _(act):
            def evaluate(i, n, k):
                size, last_step = units[n][2], units[n][3] == units[n][0] - 1
                for j, g in enumerate(gates[n]):
                    at = i * NG + before[n] + j
                    if j == 0 and (n > 0 or not isinstance(i, int)):
                        act.wait_ge(state[k], i * NU + n)
                    act.wait_ge(summed[k], at + 1)
                    act.activation(gate[k][:, g, 0:size], ps[k][:, g, 0:size],
                                   ACT.Tanh if g == 2 else ACT.Sigmoid,
                                   bias=bias[:, 2, units[n][0] - 1, g:g + 1]).then_inc(activated[k], 1)
                act.wait_ge(cell_ready[k], i * NU + n + 1)
                act.activation(tc[k][:, 0:size], cell[k][:, 0, 0:size], ACT.Tanh).then_inc(squashed[k], 1)

            def round_state(i, n, k):
                size, last_step = units[n][2], units[n][3] == units[n][0] - 1
                act.wait_ge(state[k], i * NU + n + 1)
                src, dst = (hx[k][:, places(n)], hx_hi[k][:, places(n)]) if last_step else \
                    (st[k][:, 0:size], st_hi[k][:, 0:size])
                act.activation(dst, src, ACT.Copy).then_inc(high[k], 1)

            def slot(i, first):
                for k in pair:
                    act.wait_ge(h_in[k], i * 16 + 16)
                    act.activation(hx_hi[k][:, :], hx[k][:, :], ACT.Copy).then_inc(h_high[k], 1)
                for n, k in turns():
                    evaluate(i, n, k)
                    round_state(i, n, k)
                for k in pair:
                    if k or not first:
                        act.wait_ge(h_out, (i * 2 + k) * 16)
                    ln.scalar(act, i * 2 + k, xt[:, :, :], hn[:, :, :], h_done)
            pairs(act, slot)

        @block.vector
        def _(dve):
            def update(i, n, k):
                p, _, size, q = units[n]
                c, ig = cell[k][:, 0, 0:size], cell[k][:, 1, 0:size]
                ga = lambda g: gate[k][:, g, 0:size]
                at = i * NG + before[n]
                if q == 0:
                    dve.wait_ge(activated[k], at + 2)
                    dve.tensor_tensor(c, ga(0), ga(2), ALU.mult).then_inc(cell_ready[k], 1)
                else:
                    done = sum(1 for u in units[:n] if u[3])
                    total = sum(1 for u in units if u[3])
                    own_at = (i * total + done) * 2
                    dve.wait_ge(activated[k], at + 2)
                    dve.tensor_tensor(ig, ga(0), ga(2), ALU.mult).then_inc(own[k], 1)
                    dve.wait_ge(activated[k], at + 3)
                    dve.tensor_tensor(c, ga(1), c, ALU.mult).then_inc(own[k], 1)
                    dve.wait_ge(own[k], own_at + 2)
                    dve.tensor_tensor(c, c, ig, ALU.add).then_inc(cell_ready[k], 1)

            def output(i, n, k):
                p, _, size, q = units[n]
                last_step = q == p - 1
                h = hx[k][:, places(n)] if last_step else st[k][:, 0:size]
                dve.wait_ge(activated[k], i * NG + before[n + 1])
                dve.wait_ge(squashed[k], i * NU + n + 1)
                dve.tensor_tensor(h, gate[k][:, 3, 0:size], tc[k][:, 0:size], ALU.mult).then_inc(state[k], 1)

            def low_part(i, n, k):
                p, _, size, q = units[n]
                last_step = q == p - 1
                src, hi, dst = (t[k][:, places(n)] if last_step else t[k][:, 0:size] for t in
                                ((hx, hx_hi, hx_lo) if last_step else (st, st_hi, st_lo)))
                dve.wait_ge(high[k], i * NU + n + 1)
                dve.tensor_tensor(dst, src, hi.bitcast(F32), ALU.subtract).then_inc(low[k], 1)

            def finish(i, k):
                b = i * 2 + k
                dve.wait_ge(x_in, b * 16 + 16)
                dve.wait_ge(turned, b + 1)
                dve.tensor_tensor(xt[:, :, :], ps[k][:, :, :].rearrange("p g (c f) -> p (g c) f", f=D),
                                  xt[:, :, :], ALU.add).then_inc(x_done, 1)
                dve.wait_ge(x_done, b + 1)
                ln.vector(dve, b, xt[:, :, :], k or not isinstance(i, int))

            def slot(i, first):
                for k in pair:
                    dve.wait_ge(h_high[k], i + 1)
                    dve.tensor_tensor(hx_lo[k][:, :], hx[k][:, :], hx_hi[k][:, :].bitcast(F32),
                                      ALU.subtract).then_inc(h_low[k], 1)
                for n, k in turns():
                    update(i, n, k)
                    output(i, n, k)
                    low_part(i, n, k)
                for k in pair:
                    finish(i, k)
            pairs(dve, slot)

        @block.tensor
        def _(pe):
            def gates_of(i, n, k):
                p, _, size, q = units[n]
                if n == 0:
                    pe.wait_ge(h_low[k], i + 1)
                if level_end[p] >= 0 and q == 0:
                    pe.wait_ge(low[k], i * NU + level_end[p] + 1)
                at = i * NG + before[n]
                x_parts = [(w_hi, hx_hi), (w_hi, hx_lo), (w_lo, hx_hi)]
                h_parts = [(w_hi, st_hi), (w_hi, st_lo), (w_lo, st_hi)]
                for j, g in enumerate(gates[n]):
                    for m, (w, h) in enumerate(x_parts):
                        if m == 0 and (n > 0 or not isinstance(i, int)):
                            if j == 0:
                                pe.wait_ge(activated[k], at)
                                if n == 0:
                                    pe.wait_ge(x_done, i * 2 - 1 + k)
                        last = pe.matmul(ps[k][:, g, 0:size], w[:, 0, p - 1, g * D:(g + 1) * D],
                                         h[k][:, places(n)], start=(m == 0), stop=(q == 0 and m == 2))
                    if q == 0:
                        last.then_inc(summed[k], 1)
                if q:
                    pe.wait_ge(low[k], i * NU + n)
                    for j, g in enumerate(gates[n]):
                        for m, (w, h) in enumerate(h_parts):
                            last = pe.matmul(ps[k][:, g, 0:size], w[:, 1, p - 1, g * D:(g + 1) * D],
                                             h[k][:, 0:size], start=False, stop=(m == 2))
                        last.then_inc(summed[k], 1)

            def slot(i, first):
                for n, k in turns():
                    gates_of(i, n, k)
                for k in pair:
                    pe.wait_ge(low[k], i * NU + NU)
                    pe.wait_ge(activated[k], i * NG + NG)
                    for t in range(T):
                        last = pe.transpose(ps[k][:, t // 4, (t % 4) * D:(t % 4 + 1) * D],
                                            hx[k][:, t * P:(t + 1) * P], ident[:, :])
                    last.then_inc(turned, 1)
            pairs(pe, slot)


def perceptron(prog, io, keep, weights, out):
    nc = prog.nc
    with ExitStack() as ctx:
        w1 = prog.sb(ctx, "m_w1", [P, HID])
        w2 = prog.sb(ctx, "m_w2", [P, 2, D])
        vec = prog.sb(ctx, "m_vec", [P, 9])
        agg = prog.sb(ctx, "m_agg", [P, 2, W])
        hid = prog.sb(ctx, "m_hid", [P, 2, 2, 512])
        o2 = prog.sb(ctx, "m_o2", [P, T, W])
        bn2 = prog.sb(ctx, "m_bn2", [P, 2 * T, 6])
        mv = prog.sb(ctx, "m_mv", [P, 3, 2])
        var = prog.sb(ctx, "m_var", [P, 3])
        aff = prog.sb(ctx, "m_aff", [P, 3, 4])
        y = prog.sb(ctx, "m_y", [P, 2, W])
        xt = prog.sb(ctx, "m_xt", [P, 2, B, D])
        ph = prog.ps(ctx, "m_ph", [P, 2, 2, 512])
        po = prog.ps(ctx, "m_po", [P, 2, 512])
        pt = prog.ps(ctx, "m_pt", [P, B, D])
        sem, sems = (lambda s: prog.sem(f"m_{s}")), (lambda s: prog.sems(f"m_{s}"))
        w_in, v_in, powered, aff_own, aff_ready = (sem(s) for s in ("w_in", "v_in", "powered", "aff_own", "aff_ready"))
        agg_in, x_in, x_out = sems("agg_in"), sems("x_in"), sems("x_out")
        h_summed, h_ready, o_summed, o_read = (sem(s) for s in ("h_summed", "h_ready", "o_summed", "o_read"))
        y_ready, turned, x_done = (sem(s) for s in ("y_ready", "turned", "x_done"))
        out_tiles = out.rearrange("b (t p) f -> t p b f", p=P)
        ident = keep["ident"]
        block = ctx.enter_context(nc.Block())

        @block.sync
        def _(sp):
            sp.dma_start(w1[:, :], weights["w1"]).then_inc(w_in, 16)
            sp.dma_start(w2[:, :, :], weights["w2"]).then_inc(w_in, 16)
            sp.dma_start(vec[:, :], weights["vec"]).then_inc(v_in, 16)

            def load(t):
                if t.within(2, T):
                    sp.wait_ge(h_summed, t.n * 4 - 4)
                sp.dma_start(agg[:, t.par], io["aggT"][t.n].rearrange("p b j -> p (b j)")).then_inc(agg_in[t.par], 16)
            run_slots(sp, load, T, 2, 2)

            def slot(t):
                if t.within(0, T):
                    if t.within(2, T):
                        sp.wait_ge(x_out[t.par], t.pair * 16)
                    sp.dma_start(xt[:, t.par], io["x3"][t.n]).then_inc(x_in[t.par], 16)
                if t.within(1, T + 1):
                    u = t - 1
                    sp.wait_ge(x_done, u.n + 1)
                    sp.dma_start(out_tiles[u.n], xt[:, u.par]).then_inc(x_out[u.par], 16)
            run_slots(sp, slot, T + 1)
            for s in x_out:
                sp.wait_ge(s, 16 * HALF)

        def affine(dve, j, stats, k0):
            step = Chain(dve, aff_own, 6)
            step.step(j)
            step.link(dve.bn_aggr(mv[:, j], stats))
            step.link(dve.tensor_scalar(var[:, j:j + 1], mv[:, j, 1:2], EPS, None, ALU.add))
            step.link(dve.tensor_tensor(aff[:, j, 2:3], mv[:, j, 0:1], vec[:, k0:k0 + 1], ALU.add))
            step.link(dve.tensor_tensor(aff[:, j, 3:4], vec[:, k0:k0 + 1], aff[:, j, 2:3], ALU.subtract))
            dve.wait_ge(powered, j + 1)
            step.link(dve.tensor_tensor(aff[:, j, 0:1], var[:, j:j + 1], vec[:, k0 + 1:k0 + 2], ALU.mult))
            step.link(dve.scalar_tensor_tensor(aff[:, j, 1:2], aff[:, j, 0:1], aff[:, j, 3:4],
                                               vec[:, k0 + 2:k0 + 3], ALU.mult, ALU.add))

        @block.gpsimd
        def _(pool):
            half = keep["halves"]
            for j in range(3):
                pool.wait_ge(aff_own, 6 * j + 2)
                pool.tensor_tensor(var[:, j:j + 1], var[:, j:j + 1], half[:, 0:1], ALU.pow).then_inc(powered, 1)

        @block.scalar
        def _(act):
            act.wait_ge(aff_own, 12)

            def slot(t):
                for c in range(2):
                    n = t.n * 2 + c
                    for k in range(2):
                        act.wait_ge(h_summed, n * 2 + k + 1)
                        if t.within(1, T):
                            act.wait_ge(o_summed, n - 1)
                        act.activation(hid[:, c, k], ph[:, c, k], ACT.Relu, bias=aff[:, k, 1:2],
                                       scale=aff[:, k, 0:1]).then_inc(h_ready, 1)
            run_slots(act, slot, T, 2, 2)

        @block.vector
        def _(dve):
            dve.wait_ge(v_in, 16)
            for k in range(2):
                affine(dve, k, keep["bn1"][:, k].rearrange("p c s -> p (c s)"), 3 * k)

            def slot(t):
                for c in range(2):
                    n = t.n * 2 + c
                    dve.wait_ge(o_summed, n + 1)
                    dve.tensor_scalar(o2[:, t.n, c * 512:(c + 1) * 512], po[:, c], 1.0, None, ALU.mult)
                    dve.bn_stats(bn2[:, n], po[:, c]).then_inc(o_read, 1)
            run_slots(dve, slot, T, 2, 2)
            dve.wait_ge(o_read, 2 * T)
            affine(dve, 2, bn2[:, :, :].rearrange("p c s -> p (c s)"), 6)

            def final(t):
                if t.within(0, T):
                    if t.within(2, T):
                        dve.wait_ge(turned, t.n - 1)
                    dve.tensor_scalar(y[:, t.par], o2[:, t.n], aff[:, 2, 0:1], aff[:, 2, 1:2], ALU.mult,
                                      ALU.add).then_inc(y_ready, 1)
                if t.within(1, T + 1):
                    u = t - 1
                    dve.wait_ge(x_in[u.par], u.pair * 16 + 16)
                    dve.wait_ge(turned, u.n + 1)
                    dve.tensor_tensor(xt[:, u.par], pt[:, :, :], xt[:, u.par], ALU.add).then_inc(x_done, 1)
            run_slots(dve, final, T + 1)

        @block.tensor
        def _(pe):
            pe.wait_ge(w_in, 32)

            def slot(t):
                pe.wait_ge(agg_in[t.par], t.pair * 16 + 16)
                for c in range(2):
                    for k in range(2):
                        if t.within(1, T):
                            pe.wait_ge(h_ready, t.n * 4 + c * 2 + k - 3)
                        pe.matmul(ph[:, c, k], w1[:, k * P:(k + 1) * P], agg[:, t.par, c * 512:(c + 1) * 512],
                                  start=True, stop=True).then_inc(h_summed, 1)
                for c in range(2):
                    n = t.n * 2 + c
                    for k in range(2):
                        pe.wait_ge(h_ready, n * 2 + k + 1)
                        if k == 0 and t.within(1, T):
                            pe.wait_ge(o_read, n - 1)
                        last = pe.matmul(po[:, c], w2[:, k], hid[:, c, k], start=(k == 0), stop=(k == 1))
                    last.then_inc(o_summed, 1)
            run_slots(pe, slot, T, 2, 2)

            def final(t):
                pe.wait_ge(y_ready, t.n + 1)
                if t.within(1, T):
                    pe.wait_ge(x_done, t.n)
                for b in range(B):
                    last = pe.transpose(pt[:, b], y[:, t.par, b * P:(b + 1) * P], ident[:, :])
                last.then_inc(turned, 1)
            run_slots(pe, final, T, 2, 2)


def network(nc, x, adj, w0, wa, wcT, wc, wg0, bg0, wg1, bg1, wih, whh, bih, bhh, w1, w2, vec, out):
    with ExitStack() as ctx:
        prog = Program(nc, ctx)
        io = {}
        io["ends"] = nc.dram_tensor("ends", [B * T, 2], F32).ap()
        for name in ("h0", "x1", "h1", "x2", "h2", "h2b", "x3", "h3"):
            io[name] = nc.dram_tensor(name, [T, P, B, D], F32).ap()
        for name in ("adjT", "anorm"):
            io[name] = nc.dram_tensor(name, [T, P, T, P], F32).ap()
        for name in ("mrow", "mT"):
            io[name] = nc.dram_tensor(name, [T, P, T, P], U8).ap()
        io["hT"] = nc.dram_tensor("hT", [B, P, N], F32).ap()
        io["aggT"] = nc.dram_tensor("aggT", [T, P, B, P], F32).ap()
        io["rsrow"] = nc.dram_tensor("rsrow", [T, P], F32).ap()
        io["s2row"] = nc.dram_tensor("s2row", [B * T, P], F32).ap()
        io["rrow"] = nc.dram_tensor("rrow", [2 * T, P], F32).ap()
        keep = {k: prog.sb(ctx, f"k_{k}", s) for k, s in dict(
            ident=[P, P], ones=[P, 2], halves=[P, T], rs=[P, T], rsT=[P, P], dinv=[P, T], ndinv=[P, T],
            dinv3=[P, T], wa=[P, 2, D], s1=[P, B, T], s2=[P, B, T], bn1=[P, 2, 2 * T, 6]).items()}
        prepare(prog, io, keep, x, adj, wa, wcT)
        prog.retire()
        product(prog, io, keep, "l0", io["anorm"], io["h0"], dict(w=w0), "L0",
                x.rearrange("b (t p) f -> t p b f", p=P))
        prog.retire()
        attention(prog, io, keep, wc)
        prog.retire()
        product(prog, io, keep, "l2a", io["adjT"], io["h2"], dict(w=wg0, b=bg0), "L2a")
        prog.retire()
        product(prog, io, keep, "l2b", io["adjT"], io["h2b"], dict(w=wg1, b=bg1), "L2b")
        prog.retire()
        recurrences(prog, io, keep, dict(wih=wih, whh=whh, bih=bih, bhh=bhh))
        prog.retire()
        product(prog, io, keep, "l3", io["adjT"], io["h3"], dict(w=w1), "L3")
        prog.retire()
        perceptron(prog, io, keep, dict(w1=w1, w2=w2, vec=vec), out)


def kernel(**inputs):
    import numpy as _np
    import concourse.bacc as _bacc
    from concourse.bass_utils import run_bass_kernel_spmd as _run

    a = {k: _np.asarray(v) for k, v in inputs.items()}
    lay = {
        "x": a["x"],
        "adj": a["adj"],
        "w0": a["L0_gnn_W"],
        "wcT": a["L1_gnn_W"].T,
        "wa": a["L1_gnn_a"].reshape(2, D).T,
        "wc": a["L1_gnn_W"],
        "wg0": a["L2_gnn_Wg0"],
        "bg0": a["L2_gnn_bg0"],
        "wg1": a["L2_gnn_Wg1"],
        "bg1": a["L2_gnn_bg1"].reshape(D, 1),
        "wih": a["L2_gnn_Wih"].transpose(2, 0, 1),
        "whh": a["L2_gnn_Whh"].transpose(2, 0, 1),
        "bih": a["L2_gnn_bih"].reshape(SKIP, 4, D).transpose(2, 0, 1),
        "bhh": a["L2_gnn_bhh"].reshape(SKIP, 4, D).transpose(2, 0, 1),
        "w1": a["L3_gnn_W1"].T,
        "w2": a["L3_gnn_W2"].T.reshape(2, P, D).transpose(1, 0, 2),
        "vec": _np.stack([a[f"L3_gnn_{n}1"].reshape(2, P)[k] for k in range(2) for n in ("b", "g", "be")]
                         + [a[f"L3_gnn_{n}2"] for n in ("b", "g", "be")], axis=1),
    }
    lay = {k: _np.ascontiguousarray(v) for k, v in lay.items()}
    nc = _bacc.Bacc("TRN2", target_bir_lowering=False, num_devices=1)
    args = {k: nc.dram_tensor(f"in_{k}_dram", v.shape, mybir.dt.from_np(v.dtype), kind="ExternalInput").ap()
            for k, v in lay.items()}
    out = nc.dram_tensor("out_0_dram", (B, N, D), F32, kind="ExternalOutput").ap()
    network(nc, out=out, **args)
    r = _run(nc, [{f"in_{k}_dram": v for k, v in lay.items()}], core_ids=[0])
    return r.results[0]["out_0_dram"]
```

```python
import concourse.bass as bass
from concourse import mybir
from contextlib import ExitStack

F32 = mybir.dt.float32
F32R = mybir.dt.float32r
U8 = mybir.dt.uint8
I32 = mybir.dt.int32
ALU = mybir.AluOpType
ACT = mybir.ActivationFunctionType
AX = mybir.AxisListType

P = 128
B, N, D = 8, 2048, 128
T = N // P
W = B * D
EPS = 1e-5
ALPHA = 0.2
HID = 256
SKIP = 4
HALF = T // 2
SPREAD = 40.0


class Tile:

    def __init__(self, off, i=None):
        self.off, self.i = off, i

    @property
    def n(self):
        return self.off if self.i is None else self.i * 2 + self.off

    @property
    def pair(self):
        return self.off // 2 if self.i is None else self.i + self.off // 2

    @property
    def par(self):
        return self.off % 2

    def __add__(self, k):
        return Tile(self.off + k, self.i)

    def __sub__(self, k):
        return Tile(self.off - k, self.i)

    def within(self, lo, hi):
        return self.i is not None or lo <= self.off < hi


def run_slots(eng, slot, n, head=2, tail=3):
    for t in range(head):
        slot(Tile(t))
    with eng.Fori(head // 2, (n - tail) // 2) as i:
        slot(Tile(0, i))
        slot(Tile(1, i))
    for t in range(n - tail, n):
        slot(Tile(t))


class Chain:

    def __init__(self, eng, sem, links):
        self.eng, self.sem, self.links = eng, sem, links

    def step(self, t):
        self.base, self.k = t * self.links, 0

    def link(self, ins):
        self.k += 1
        assert self.k <= self.links
        ins.then_inc(self.sem, 1)
        self.eng.wait_ge(self.sem, self.base + self.k)


def over(col, width):
    return col.unsqueeze(2).to_broadcast([col.shape[0], col.shape[1], width])


class Program:
    def __init__(self, nc, ctx):
        self.nc, self.ctx, self.live = nc, ctx, []

    def sem(self, name):
        self.live.append(self.nc.alloc_semaphore(name))
        return self.live[-1]

    def retire(self):
        with self.nc.Block() as block:
            @block.gpsimd
            def _(pool):
                for sem in self.live:
                    pool.sem_clear(sem)
        for sem in self.live:
            self.nc.release_semaphore(sem)
        self.live = []

    def sems(self, name, n=2):
        return [self.sem(f"{name}{k}") for k in range(n)]

    def sb(self, ctx, name, shape, dt=F32):
        return ctx.enter_context(self.nc.sbuf_tensor(name, shape, dt))

    def ps(self, ctx, name, shape):
        return ctx.enter_context(self.nc.psum_tensor(name, shape, F32))


class LayerNorm:

    def __init__(self, prog, ctx, name, blocks):
        self.blocks = blocks
        self.six = prog.sb(ctx, f"{name}_six", [P, blocks, 6])
        self.carrier = prog.sb(ctx, f"{name}_carrier", [P, 1])
        self.mv = prog.sb(ctx, f"{name}_mv", [P, blocks, 2])
        self.minus_mean = prog.sb(ctx, f"{name}_minus_mean", [P, blocks])
        self.var_eps = prog.sb(ctx, f"{name}_var_eps", [P, blocks])
        self.scale = prog.sb(ctx, f"{name}_scale", [P, blocks])
        self.shift = prog.sb(ctx, f"{name}_shift", [P, blocks])
        self.half = prog.sb(ctx, f"{name}_half", [P, blocks])
        self.own = prog.sem(f"{name}_own")
        self.measured = prog.sem(f"{name}_measured")
        self.power = prog.sem(f"{name}_power")
        self.scaled = prog.sem(f"{name}_scaled")
        self.half_set = prog.sem(f"{name}_half_set")

    def vector(self, dve, t, x, later, part=None):
        lo, hi = part or (0, self.blocks)
        for b in range(lo, hi):
            last = dve.bn_stats(self.six[:, b], x[:, b])
        if hi < self.blocks:
            return
        chain = Chain(dve, self.own, 2)
        chain.step(t)
        chain.link(last)
        dve.memset(self.carrier[:, :], 0.0)
        for b in range(self.blocks):
            last = dve.bn_aggr(self.mv[:, b], self.six[:, b])
        chain.link(last)
        if later:
            dve.wait_ge(self.scaled, t)
        dve.tensor_scalar(self.minus_mean[:, :], self.mv[:, :, 0], -1.0, None, ALU.mult)
        dve.tensor_scalar(self.var_eps[:, :], self.mv[:, :, 1], EPS, None, ALU.add).then_inc(self.measured, 1)

    def pool_setup(self, pool):
        pool.memset(self.half[:, :], -0.5).then_inc(self.half_set, 1)
        pool.wait_ge(self.half_set, 1)

    def pool(self, pool, t, done, later):
        if later:
            pool.wait_ge(done, t)
        pool.wait_ge(self.measured, t + 1)
        pool.tensor_tensor(self.scale[:, :], self.var_eps[:, :], self.half[:, :], ALU.pow).then_inc(self.power, 1)
        pool.wait_ge(self.power, t + 1)
        pool.tensor_tensor(self.shift[:, :], self.minus_mean[:, :], self.scale[:, :],
                           ALU.mult).then_inc(self.scaled, 1)

    def scalar(self, act, t, x, out, done, part=None):
        lo, hi = part or (0, self.blocks)
        if lo == 0:
            act.wait_ge(self.scaled, t + 1)
        for b in range(lo, hi):
            last = act.activation(out[:, b], x[:, b], ACT.Relu, bias=self.shift[:, b:b + 1],
                                  scale=self.scale[:, b:b + 1])
        if hi == self.blocks:
            last.then_inc(done, 1)


def prepare(prog, io, keep, x, adj, a_col, wc_t):
    nc = prog.nc
    x_tiles = x.rearrange("b (t p) f -> t p b f", p=P)
    adj_tiles = adj.rearrange("(t p) n -> t p n", p=P)
    with ExitStack() as ctx:
        a_sb = prog.sb(ctx, "a_sb", [P, T, N])
        ident = keep["ident"]
        a_loaded = prog.sem("a_loaded")
        xt = prog.sb(ctx, "p_xt", [P, 2, B, D])
        ht = prog.sb(ctx, "p_ht", [P, 2, B, D])
        ln = LayerNorm(prog, ctx, "pln", B)
        x_in, h_out = prog.sems("px_in"), prog.sems("ph_out")
        ln_done = prog.sem("pln_done")

        with ExitStack() as c1:
            id_set = prog.sem("id_set")
            acol = prog.sb(c1, "acol", [P, 2])
            wct = prog.sb(c1, "wct", [P, D])
            spread = prog.sb(c1, "spread", [P, 2, P])
            pw = prog.ps(c1, "p_wa", [P, 2, D])
            wa_in, wa_spread, wa_summed = (prog.sem(k) for k in ("wa_in", "wa_spread", "wa_summed"))
            block = c1.enter_context(nc.Block())

            @block.tensor
            def _(pe):
                pe.wait_ge(wa_spread, 2)
                for k in range(2):
                    pe.matmul(pw[:, k], spread[:, k], wct[:, :], start=True, stop=True).then_inc(wa_summed, 1)

            @block.sync
            def _(sp):
                sp.dma_start(acol[:, :], a_col).then_inc(wa_in, 16)
                sp.dma_start(wct[:, :], wc_t).then_inc(wa_in, 16)

                for t in range(2):
                    sp.dma_start(xt[:, t], x_tiles[t]).then_inc(x_in[t], 16)
                for t in range(T):
                    sp.dma_start(a_sb[:, t], adj_tiles[t]).then_inc(a_loaded, 16)

            @block.gpsimd
            def _(pool):
                pool.memset(ident[:, :], 0.0).then_inc(id_set, 1)
                pool.memset(keep["ones"][:, :], 1.0).then_inc(id_set, 1)
                pool.wait_ge(id_set, 2)
                pool.affine_select(out=ident[:, :], in_=ident[:, :], compare_op=ALU.not_equal, fill=1.0,
                                   base=0, pattern=[[-1, P]], channel_multiplier=1).then_inc(id_set, 1)

            @block.vector
            def _(dve):
                dve.wait_ge(id_set, 2)
                dve.wait_ge(wa_in, 32)
                for k in range(2):
                    dve.tensor_scalar(spread[:, k], keep["ones"][:, 0:1].to_broadcast([P, P]), acol[:, k:k + 1],
                                      None, ALU.mult).then_inc(wa_spread, 1)
                dve.wait_ge(wa_summed, 2)
                dve.tensor_copy(keep["wa"][:, :, :], pw[:, :, :])

        with ExitStack() as c2:
            stage = prog.sb(c2, "stage", [P, 2, T, P])
            at = prog.sb(c2, "at", [P, 2, T, P])
            an = prog.sb(c2, "an", [P, 2, T, P])
            mt = prog.sb(c2, "mt", [P, 2, T, P], U8)
            sums = prog.sb(c2, "sums", [P, 4, T])
            part = prog.sb(c2, "part", [P, 2, T])
            small = prog.sb(c2, "small", [P, 4, T])
            pt = prog.ps(c2, "p_pt", [P, 2, HALF, P])
            pst = prog.ps(c2, "p_sum", [P, 512])
            staged = prog.sem("staged")
            turned = prog.sem("turned")
            copied = prog.sem("copied")
            added = prog.sem("added")
            normed = prog.sem("normed")
            masked = prog.sem("masked")
            totalled = prog.sem("totalled")
            an_out = prog.sems("an_out")
            at_out = prog.sems("at_out")
            mask_out = prog.sems("mask_out")
            powered = prog.sem("powered")
            ready = prog.sem("deg_ready")
            rs_turned, rs_copied, rs_out = prog.sem("rs_turned"), prog.sem("rs_copied"), prog.sem("rs_out")
            block = c2.enter_context(nc.Block())

            @block.sync
            def _(sp):
                def slot(t):
                    if t.within(0, T):
                        if t.within(2, T):
                            sp.wait_ge(ln_done, t.n - 1)
                            sp.dma_start(xt[:, t.par], x_tiles[t.n]).then_inc(x_in[t.par], 16)
                        sp.wait_ge(copied, t.n * 2 + 2)
                        sp.dma_start(io["adjT"][t.n], at[:, t.par]).then_inc(at_out[t.par], 16)
                        sp.wait_ge(normed, t.n + 1)
                        sp.dma_start(io["anorm"][t.n], an[:, t.par]).then_inc(an_out[t.par], 16)
                        sp.wait_ge(masked, t.n + 1)
                        sp.dma_start(io["mT"][t.n], mt[:, t.par]).then_inc(mask_out[t.par], 16)
                    if t.within(1, T + 1):
                        u = t - 1
                        sp.wait_ge(ln_done, u.n + 1)
                        sp.dma_start(io["h0"][u.n], ht[:, u.par]).then_inc(h_out[u.par], 16)
                run_slots(sp, slot, T + 1)
                sp.wait_ge(rs_copied, 1)
                sp.dma_start(io["rsrow"], keep["rsT"][0:T, :]).then_inc(rs_out, 16)
                for s in at_out + an_out + mask_out + h_out:
                    sp.wait_ge(s, 16 * HALF)
                sp.wait_ge(rs_out, 16)

            @block.scalar
            def _(act):
                def slot(t):
                    if t.within(0, T):
                        if t.within(2, T):
                            act.wait_ge(turned, t.n * 2 - 2)
                        act.wait_ge(a_loaded, 16 * T)
                        act.activation(stage[:, t.par].rearrange("p c j -> p (c j)"), a_sb[:, t.n],
                                       ACT.Copy, accum_out=sums[:, 1, bass.ds(t.n, 1)]).then_inc(staged, 1)
                    if t.within(1, T + 1):
                        u = t - 1
                        if u.within(2, T):
                            act.wait_ge(at_out[u.par], u.pair * 16)
                            act.wait_ge(totalled, u.n * 3 - 3)
                        for h in range(2):
                            act.wait_ge(turned, u.n * 2 + h + 1)
                            for c in range(HALF):
                                k = h * HALF + c
                                last = act.activation(at[:, u.par, k], pt[:, h, c], ACT.Copy,
                                                      accum_out=part[:, u.par, k:k + 1])
                            last.then_inc(copied, 1)
                    if t.within(2, T + 2):
                        u = t - 2
                        if u.within(2, T):
                            act.wait_ge(h_out[u.par], u.pair * 16)
                        ln.scalar(act, u.n, xt[:, u.par], ht[:, u.par], ln_done)
                run_slots(act, slot, T + 2, 2, 4)
                act.wait_ge(rs_turned, 1)
                act.activation(keep["rsT"][0:T, :], pst[0:T, 0:P], ACT.Copy).then_inc(rs_copied, 1)

            @block.vector
            def _(dve):
                sym, row, dia, col = (sums[:, j] for j in range(4))
                dve.memset(sym, 0.0)
                dve.memset(col, 0.0).then_inc(ready, 1)

                dve.wait_ge(a_loaded, 16 * T)
                for t in range(T):
                    last = dve.tensor_tensor(an[:, 0, t, :], a_sb[:, t, t * P:(t + 1) * P], ident[:, :], ALU.mult)
                last.then_inc(ready, 1)
                dve.wait_ge(ready, 2)
                dve.tensor_reduce(dia, an[:, 0], AX.X, ALU.add).then_inc(ready, 1)

                def slot(t):
                    if t.within(0, T):
                        dve.wait_ge(copied, t.n * 2 + 2)
                        if t.within(2, T):
                            dve.wait_ge(an_out[t.par], t.pair * 16)
                        dve.tensor_tensor(an[:, t.par], at[:, t.par], a_sb[:, :, bass.ts(t.n, P)],
                                          ALU.add).then_inc(added, 1)
                        dve.wait_ge(added, t.n + 1)
                        dve.tensor_scalar(an[:, t.par], an[:, t.par], 0.5, 0.0, ALU.mult,
                                          ALU.max).then_inc(normed, 1)
                        if t.within(2, T):
                            dve.wait_ge(mask_out[t.par], t.pair * 16)
                        dve.tensor_scalar(mt[:, t.par], at[:, t.par], 0.0, None, ALU.not_equal).then_inc(masked, 1)
                        if t.within(1, T):
                            dve.wait_ge(totalled, t.n * 3)
                        dve.wait_ge(normed, t.n + 1)
                        dve.tensor_reduce(small[:, 0], an[:, t.par], AX.X, ALU.add).then_inc(totalled, 1)
                        dve.tensor_tensor(col, col, part[:, t.par], ALU.add).then_inc(totalled, 1)
                        dve.wait_ge(totalled, t.n * 3 + 2)
                        dve.tensor_tensor(sym, sym, small[:, 0], ALU.add).then_inc(totalled, 1)
                        dve.wait_ge(x_in[t.par], t.pair * 16 + 16)
                        ln.vector(dve, t.n, xt[:, t.par], t.within(1, T))
                dve.wait_ge(ready, 3)
                run_slots(dve, slot, T, 2, 2)
                dve.wait_ge(staged, T)
                dve.wait_ge(totalled, 3 * T)
                dve.tensor_copy(keep["rs"][:, :], row)
                positive, safe, deg = small[:, 0], small[:, 1], small[:, 2]
                dve.tensor_scalar(positive, sym, 0.0, None, ALU.is_gt).then_inc(ready, 1)
                dve.wait_ge(ready, 4)
                dve.tensor_scalar(safe, positive, -1.0, 1.0, ALU.mult, ALU.add).then_inc(ready, 1)
                dve.tensor_tensor(small[:, 3], sym, positive, ALU.mult).then_inc(ready, 1)
                dve.wait_ge(ready, 6)
                dve.tensor_tensor(safe, safe, small[:, 3], ALU.add).then_inc(ready, 1)
                dve.scalar_tensor_tensor(deg, row, 1.0, col, ALU.add, ALU.add).then_inc(ready, 1)
                dve.wait_ge(ready, 8)
                dve.tensor_tensor(keep["deg3"][:, :], deg, dia, ALU.subtract).then_inc(ready, 1)
                dve.wait_ge(powered, 2)
                dve.tensor_tensor(keep["dinv"][:, :], small[:, 3], positive, ALU.mult).then_inc(ready, 1)
                dve.wait_ge(ready, 10)
                dve.tensor_scalar(keep["ndinv"][:, :], keep["dinv"][:, :], -1.0, None, ALU.mult)

            @block.gpsimd
            def _(pool):
                pool.memset(keep["halves"][:, :], -0.5).then_inc(powered, 1)
                pool.wait_ge(powered, 1)
                ln.pool_setup(pool)
                run_slots(pool, lambda t: ln.pool(pool, t.n, ln_done, t.within(1, T)), T, 2, 2)
                pool.wait_ge(ready, 9)
                pool.tensor_tensor(small[:, 3], small[:, 1], keep["halves"][:, :], ALU.pow).then_inc(powered, 1)

            @block.tensor
            def _(pe):
                def slot(t):
                    if t.within(0, T):
                        pe.wait_ge(staged, t.n + 1)
                        for h in range(2):
                            if t.within(1, T):
                                pe.wait_ge(copied, t.n * 2 + h - 1)
                            for c in range(HALF):
                                last = pe.transpose(pt[:, h, c], stage[:, t.par, h * HALF + c], ident[:, :])
                            last.then_inc(turned, 1)
                run_slots(pe, slot, T, 2, 2)
                pe.wait_ge(staged, T)
                pe.transpose(pst[0:T, 0:P], sums[:, 1], ident[:, :]).then_inc(rs_turned, 1)


def product(prog, io, keep, name, adj_d, h_in, weights, kind, x_in_d=None):
    nc = prog.nc
    scale = {"L0": keep["dinv"], "L3": keep["dinv3"]}.get(kind)
    uses_h = kind in ("L0", "L3")
    uses_x = kind == "L0"
    with ExitStack() as ctx:
        n_ = lambda s: f"{name}_{s}"
        g_hi = prog.sb(ctx, n_("g_hi"), [P, T, W], F32R)
        g_lo = prog.sb(ctx, n_("g_lo"), [P, T, W], F32R)
        a_raw = prog.sb(ctx, n_("a_raw"), [P, T, P])
        a_hi = prog.sb(ctx, n_("a_hi"), [P, 2, T, P], F32R)
        a_lo = prog.sb(ctx, n_("a_lo"), [P, 2, T, P], F32R)
        v = prog.sb(ctx, n_("v"), [P, B, D])
        ut = prog.sb(ctx, n_("ut"), [P, B, P])
        ht = prog.sb(ctx, n_("ht"), [P, 2, B, D])
        xt = prog.sb(ctx, n_("xt"), [P, 2, B, D]) if uses_x else None
        hn = prog.sb(ctx, n_("hn"), [P, B, D]) if kind != "L3" else None
        wsb = prog.sb(ctx, n_("w"), [P, weights["w"].shape[1]])
        acc = prog.ps(ctx, n_("acc"), [P, 2, W])
        pt = prog.ps(ctx, n_("pt"), [P, B, P])
        po = prog.ps(ctx, n_("po"), [P, B, D])
        ln = LayerNorm(prog, ctx, n_("ln"), B) if uses_x else None
        tmp = prog.sb(ctx, n_("tmp"), [P, B, D]) if kind == "L0" else None
        zt = prog.sb(ctx, n_("zt"), [P, 2, W]) if kind == "L3" else None
        ident = keep["ident"]
        ring = [ht[:, 0], ht[:, 1], v, ut]
        LAG = 2 if kind == "L0" else 1
        slots = (T + LAG, 2, 2 + LAG)

        w_in = prog.sem(n_("w_in"))
        g_in = prog.sems(n_("g_in"), 4)
        g_high = prog.sem(n_("g_high"))
        g_low = prog.sem(n_("g_low"))
        a_in = prog.sem(n_("a_in"))
        a_high = prog.sem(n_("a_high"))
        a_low = prog.sem(n_("a_low"))
        h_in_s = prog.sems(n_("h_in"))
        x_in_s = prog.sems(n_("x_in")) if uses_x else None
        multiplied = prog.sem(n_("multiplied"))
        evacuated = prog.sem(n_("evacuated"))
        turned = prog.sem(n_("turned"))
        ut_ready = prog.sem(n_("ut_ready"))
        projected = prog.sem(n_("projected"))
        po_read = prog.sem(n_("po_read"))
        x_done = prog.sem(n_("x_done"))
        h_done = prog.sem(n_("h_done"))
        x_out = prog.sems(n_("x_out"))
        h_out = prog.sem(n_("h_out"))
        own = prog.sem(n_("own"))
        own2 = prog.sem(n_("own2"))
        projected_s = prog.sem(n_("projected_s"))
        halves = 2 if kind == "L3" else 1
        extra = {}
        n_w = 1
        if kind == "L0":
            extra["wa"] = keep["wa"]
        if kind == "L2a":
            extra["brow"] = prog.sb(ctx, n_("brow"), [P, D])
            n_w = 2
        if kind == "L2b":
            extra["bcol"] = prog.sb(ctx, n_("bcol"), [P, 1])
            extra["rsrow"] = prog.sb(ctx, n_("rsrow"), [P, N])
            n_w = 3
        small = prog.sb(ctx, n_("small"), [P, 2, B])
        block = ctx.enter_context(nc.Block())

        @block.sync
        def _(sp):
            sp.dma_start(a_raw[:, :, :], adj_d[0]).then_inc(a_in, 16)
            for s in range(T):
                if s >= 4:
                    sp.wait_ge(g_low, s - 3)
                sp.dma_start(ring[s % 4][:, :, :], h_in[s]).then_inc(g_in[s % 4], 16)
                if s == 1:
                    sp.dma_start(wsb[:, :], weights["w"]).then_inc(w_in, 16)
                    if kind == "L2a":
                        sp.dma_start(extra["brow"][:, :], weights["b"].partition_broadcast(P)).then_inc(w_in, 16)
                    if kind == "L2b":
                        sp.dma_start(extra["bcol"][:, :], weights["b"]).then_inc(w_in, 16)
                        sp.dma_start(extra["rsrow"][:, :],
                                     io["rsrow"].rearrange("t j -> (t j)").partition_broadcast(P)).then_inc(w_in, 16)

            def slot(t):
                if t.within(0, T - 1):
                    sp.wait_ge(a_high, t.n + 1)
                    sp.wait_ge(a_low, t.n + 1)
                    sp.dma_start(a_raw[:, :, :], adj_d[t.n + 1]).then_inc(a_in, 16)
                if t.within(0, T):
                    if uses_h:
                        if t.within(2, T):
                            sp.wait_ge(evacuated, t.n - 1)
                        else:
                            sp.wait_ge(g_low, T)
                        sp.dma_start(ht[:, t.par], h_in[t.n]).then_inc(h_in_s[t.par], 16)
                if t.within(LAG, T + LAG):
                    u = t - LAG
                    if uses_x:
                        sp.wait_ge(x_done, u.n + 1)
                        sp.dma_start(io["x1"][u.n], xt[:, u.par]).then_inc(x_out[u.par], 16)
                    if kind in ("L0", "L2a"):
                        sp.wait_ge(h_done, u.n + 1)
                        sp.dma_start(io["h1" if kind == "L0" else "h2b"][u.n], hn[:, :, :]).then_inc(h_out, 16)
                    if kind == "L2b":
                        sp.wait_ge(h_done, u.n + 1)
                        sp.dma_start(io["hT"].rearrange("b f (t j) -> t f b j", j=P)[u.n],
                                     hn[:, :, :]).then_inc(h_out, 16)
                    if kind == "L3":
                        sp.wait_ge(po_read, u.n * 2 + 2)
                        sp.dma_start(io["z1"][u.n], zt[:, :, :]).then_inc(h_out, 16)
                if t.within(0, T):
                    if uses_x:
                        if t.within(2, T):
                            sp.wait_ge(x_out[t.par], t.pair * 16)
                            sp.wait_ge(h_done, t.n - 1)
                        sp.dma_start(xt[:, t.par], x_in_d[t.n]).then_inc(x_in_s[t.par], 16)
            run_slots(sp, slot, *slots)
            if uses_x:
                for s in x_out:
                    sp.wait_ge(s, 16 * HALF)
            sp.wait_ge(h_out, 16 * T)

        @block.scalar
        def _(act):
            def split(t):
                if t.within(2, T):
                    act.wait_ge(multiplied, t.n - 1)
                act.wait_ge(a_in, t.n * 16 + 16)
                act.activation(a_hi[:, t.par], a_raw[:, :, :], ACT.Copy).then_inc(a_high, 1)

            split(Tile(0))
            for s in range(T):
                act.wait_ge(g_in[s % 4], 16 * (s // 4 + 1))
                sc = 1.0 if scale is None else scale[:, s:s + 1]
                act.activation(g_hi[:, s], ring[s % 4][:, :, :].rearrange("p b f -> p (b f)"), ACT.Copy,
                               scale=sc).then_inc(g_high, 1)

            def slot(t):
                if t.within(0, T - 1):
                    split(t + 1)
                if uses_x and t.within(LAG, T + LAG):
                    u = t - LAG
                    if u.within(1, T):
                        act.wait_ge(h_out, u.n * 16)
                        act.wait_ge(projected_s, u.n)
                    ln.scalar(act, u.n, xt[:, u.par], hn[:, :, :], h_done)
                if t.within(1, T + 1):
                    u = t - 1
                    act.wait_ge(turned, u.n + 1)
                    if u.within(1, T):
                        act.wait_ge(projected, u.n * halves)
                    act.activation(ut[:, :, :], pt[:, :, :], ACT.Copy).then_inc(ut_ready, 1)
            run_slots(act, slot, *slots)

        if uses_x:
            @block.gpsimd
            def _(pool):
                ln.pool_setup(pool)
                pool.tensor_tensor(keep["dinv3"][:, :], keep["deg3"][:, :], keep["halves"][:, :], ALU.pow)
                run_slots(pool, lambda t: ln.pool(pool, t.n, h_done, t.within(1, T)), T, 2, 2)

        @block.vector
        def _(dve):
            links = Chain(dve, own, {"L0": 4, "L2a": 1, "L2b": 1, "L3": 0}[kind])
            evac_link = Chain(dve, own2, 1)

            def split(t):
                if t.within(2, T):
                    dve.wait_ge(multiplied, t.n - 1)
                dve.wait_ge(a_high, t.n + 1)
                dve.tensor_tensor(a_lo[:, t.par], a_raw[:, :, :], a_hi[:, t.par].bitcast(F32),
                                  ALU.subtract).then_inc(a_low, 1)

            split(Tile(0))
            for s in range(T):
                dve.wait_ge(g_high, s + 1)
                h2 = ring[s % 4][:, :, :].rearrange("p b f -> p (b f)")
                if scale is None:
                    dve.tensor_tensor(g_lo[:, s], h2, g_hi[:, s].bitcast(F32), ALU.subtract).then_inc(g_low, 1)
                else:
                    dve.scalar_tensor_tensor(g_lo[:, s], h2, scale[:, s:s + 1], g_hi[:, s].bitcast(F32),
                                             ALU.mult, ALU.subtract).then_inc(g_low, 1)
            dve.wait_ge(w_in, 16 * n_w)

            def evacuate(u):
                a2 = acc[:, u.par].rearrange("p (b f) -> p b f", f=D)
                if u.within(1, T):
                    dve.wait_ge(turned, u.n)
                if uses_h:
                    dve.wait_ge(h_in_s[u.par], u.pair * 16 + 16)
                dve.wait_ge(multiplied, u.n + 1)
                if kind == "L0":
                    dve.scalar_tensor_tensor(v[:, :, :], a2, keep["ndinv"][:, bass.ds(u.n, 1)], ht[:, u.par],
                                             ALU.mult, ALU.add).then_inc(evacuated, 1)
                elif kind == "L3":
                    evac_link.step(u.n)
                    evac_link.link(dve.scalar_tensor_tensor(
                        v[:, :, :], ht[:, u.par], keep["dinv3"][:, bass.ds(u.n, 1)], a2, ALU.mult, ALU.add))
                    dve.tensor_scalar(v[:, :, :], v[:, :, :], keep["dinv3"][:, bass.ds(u.n, 1)], None,
                                      ALU.mult).then_inc(evacuated, 1)
                else:
                    dve.tensor_copy(v[:, :, :], a2).then_inc(evacuated, 1)

            def tail(u, part):
                if kind == "L0" and part == 1:
                    links.step(u.n)
                    dve.wait_ge(h_done, u.n + 1)
                    for j, col in ((0, keep["s1"]), (1, keep["s2"])):
                        wa = extra["wa"][:, j].unsqueeze(1).to_broadcast([P, B, D])
                        links.link(dve.tensor_tensor(tmp[:, :, :], hn[:, :, :], wa, ALU.mult))
                        links.link(dve.tensor_reduce(small[:, j, :], tmp[:, :, :], AX.X, ALU.add))
                        ins = dve.tensor_scalar(col[:, :, bass.ds(u.n, 1)], small[:, j, :].unsqueeze(2), 1.0,
                                                None, ALU.mult)
                    ins.then_inc(projected_s, 1)
                if part == 1:
                    return
                links.step(u.n)
                if kind == "L0":
                    dve.wait_ge(x_in_s[u.par], u.pair * 16 + 16)
                    dve.wait_ge(projected, u.n + 1)
                    dve.scalar_tensor_tensor(xt[:, u.par], po[:, :, :], 0.0, xt[:, u.par],
                                             ALU.max, ALU.add).then_inc(x_done, 1)
                    dve.wait_ge(x_done, u.n + 1)
                    ln.vector(dve, u.n, xt[:, u.par], u.within(1, T))
                if kind in ("L2a", "L2b"):
                    dve.wait_ge(projected, u.n + 1)
                    if u.within(1, T):
                        dve.wait_ge(h_out, u.n * 16)
                    if kind == "L2a":
                        bias = extra["brow"][:, :].unsqueeze(1).to_broadcast([P, B, D])
                        s = keep["rs"][:, bass.ds(u.n, 1)]
                    else:
                        bias = extra["rsrow"][:, bass.ts(u.n, P)].unsqueeze(1).to_broadcast([P, B, P])
                        s = extra["bcol"][:, 0:1]
                    links.link(dve.scalar_tensor_tensor(hn[:, :, :], bias, s, po[:, :, :], ALU.mult, ALU.add))
                    dve.tensor_scalar(hn[:, :, :], hn[:, :, :], 0.0, None, ALU.max).then_inc(h_done, 1)
                if kind == "L3":
                    for k in range(2):
                        if k == 0 and u.within(1, T):
                            dve.wait_ge(h_out, u.n * 16)
                        dve.wait_ge(projected, u.n * 2 + k + 1)
                        dve.tensor_copy(zt[:, k], po[:, :, :].rearrange("p b f -> p (b f)"))
                        for c in range(2):
                            last = dve.bn_stats(keep["bn1"][:, k, bass.ds(u.n * 2 + c, 1), :].squeeze(1),
                                                po[:, 4 * c:4 * c + 4, :].rearrange("p b f -> p (b f)"))
                        last.then_inc(po_read, 1)

            def slot(t):
                if t.within(1, T + 1):
                    evacuate(t - 1)
                if kind == "L0" and t.within(LAG, T + LAG):
                    tail(t - LAG, 0)
                if t.within(0, T - 1):
                    split(t + 1)
                if t.within(LAG, T + LAG):
                    tail(t - LAG, 1 if kind == "L0" else 0)
            run_slots(dve, slot, *slots)

        @block.tensor
        def _(pe):
            pe.wait_ge(w_in, 16 * n_w)

            def main(t, s0, s1):
                if s0 == 0:
                    if t.within(2, T):
                        pe.wait_ge(evacuated, t.n - 1)
                    pe.wait_ge(a_low, t.n + 1)
                for s in range(s0, s1):
                    if t.i is None and t.off == 0:
                        pe.wait_ge(g_low, s + 1)
                    for lhs, rhs in ((a_hi, g_hi), (a_hi, g_lo), (a_lo, g_hi)):
                        for c in range(2):
                            last = pe.matmul(acc[:, t.par, c * 512:(c + 1) * 512], lhs[:, t.par, s],
                                             rhs[:, s, c * 512:(c + 1) * 512],
                                             start=(s == 0 and lhs is a_hi and rhs is g_hi),
                                             stop=(s == T - 1 and lhs is a_lo))
                if s1 == T:
                    last.then_inc(multiplied, 1)

            def turn(u):
                pe.wait_ge(evacuated, u.n + 1)
                if u.within(1, T):
                    pe.wait_ge(ut_ready, u.n)
                for b in range(B):
                    last = pe.transpose(pt[:, b], v[:, b], ident[:, :])
                last.then_inc(turned, 1)

            def project(u, k):
                pe.wait_ge(ut_ready, u.n + 1)
                if kind == "L3":
                    if k == 1 or u.within(1, T):
                        pe.wait_ge(po_read, u.n * 2 + k)
                elif u.within(1, T):
                    pe.wait_ge(x_done if kind == "L0" else h_done, u.n)
                if kind in ("L0", "L2a"):
                    for b in range(B):
                        last = pe.matmul(po[:, b], ut[:, b], wsb[:, :], start=True, stop=True)
                else:
                    for c in range(2):
                        last = pe.matmul(po[:, 4 * c:4 * c + 4], wsb[:, k * P:(k + 1) * P],
                                         ut[:, 4 * c:4 * c + 4], start=True, stop=True)
                last.then_inc(projected, 1)

            def slot(t):
                pieces = [(0, 5), (5, 11), (11, T)]
                for j, (s0, s1) in enumerate(pieces):
                    if t.within(0, T):
                        main(t, s0, s1)
                    if t.within(1, T + 1):
                        if j == 0:
                            turn(t - 1)
                        elif j - 1 < halves:
                            project(t - 1, j - 1)
            run_slots(pe, slot, *slots)


def attention(prog, io, keep, weights):
    nc = prog.nc
    with ExitStack() as ctx:
        mT = prog.sb(ctx, "c_mT", [P, T, T, P], U8)
        wsb = prog.sb(ctx, "c_w", [P, D])
        bounds = prog.sb(ctx, "c_bounds", [P, 3, B])
        is_wide = prog.sb(ctx, "c_is_wide", [P, 1], I32)
        factors = prog.sb(ctx, "c_factors", [P, 3, B, T])
        w_in, mT_in = prog.sem("c_w_in"), prog.sem("c_mT_in")
        shared = dict(mT=mT, wsb=wsb, bounds=bounds, is_wide=is_wide, factors=factors, mT_in=mT_in, w_in=w_in)
        attention_ranges(prog, io, keep, weights, shared)
        attention_near(prog, io, keep, shared)
        attention_wide(prog, io, keep, shared)


def attention_ranges(prog, io, keep, weights, shared):
    nc = prog.nc
    bounds, factors = shared["bounds"], shared["factors"]
    with ExitStack() as ctx:
        ends = prog.sb(ctx, "g_ends", [P, 2, B])
        ends_T = prog.sb(ctx, "g_ends_T", [2 * B, 1])
        apart = prog.sb(ctx, "g_apart", [2 * B, 2 * B])
        ones = prog.sb(ctx, "g_ones", [2 * B, P])
        s2T = prog.sb(ctx, "g_s2T", [P, P])
        dist = prog.sb(ctx, "g_dist", [P, 2, B, T])
        erow = prog.sb(ctx, "g_erow", [P, 2, B, T])
        wide = prog.sb(ctx, "g_wide", [P, 1])
        ps = prog.ps(ctx, "g_ps", [P, 3, 512])
        names = ("s2_turned", "s2_copied", "ends_own", "ends_turned", "ones_set", "spread", "known", "drawn",
                 "e_ready", "e_turned", "e_copied", "stored")
        s = {k: prog.sem(f"g_{k}") for k in names}
        s1, s2 = keep["s1"], keep["s2"]
        ident = keep["ident"]
        block = ctx.enter_context(nc.Block())

        @block.sync
        def _(sp):
            sp.dma_start(shared["wsb"][:, :], weights).then_inc(shared["w_in"], 16)
            sp.wait_ge(s["s2_copied"], 1)
            sp.dma_start(io["s2row"], s2T[:, :]).then_inc(s["stored"], 16)
            sp.wait_ge(s["e_copied"], 1)
            sp.dma_start(io["erow"], erow[:, 1].rearrange("p b t -> p (b t)")).then_inc(s["stored"], 16)
            sp.wait_ge(s["stored"], 32)

        @block.gpsimd
        def _(pool):
            pool.memset(ones[:, :], 1.0).then_inc(s["ones_set"], 1)

        @block.scalar
        def _(act):
            for t in range(T):
                act.dma_start(shared["mT"][:, t], io["mT"][t]).then_inc(shared["mT_in"], 16)
            act.wait_ge(s["s2_turned"], 1)
            act.activation(s2T[:, :], ps[:, 0, 0:P], ACT.Copy).then_inc(s["s2_copied"], 1)
            act.wait_ge(s["drawn"], 3)
            act.activation(erow[:, 0], dist[:, 0], ACT.Exp).then_inc(s["e_ready"], 1)
            act.activation(factors[:, 0], dist[:, 1], ACT.Exp).then_inc(s["e_ready"], 1)
            act.activation(factors[:, 2], dist[:, 1], ACT.Exp, scale=ALPHA)
            act.wait_ge(s["e_turned"], 1)
            act.activation(erow[:, 1].rearrange("p b t -> p (b t)"), ps[:, 0, 0:P],
                           ACT.Copy).then_inc(s["e_copied"], 1)

        @block.tensor
        def _(pe):
            pe.transpose(ps[:, 0, 0:P], s2[:, :, :].rearrange("p b t -> p (b t)"),
                         ident[:, :]).then_inc(s["s2_turned"], 1)
            pe.wait_ge(s["ends_own"], 3)
            pe.transpose(ps[0:2 * B, 1, 0:P], ends[:, :, :].rearrange("p k b -> p (k b)"),
                         ident[:, :]).then_inc(s["ends_turned"], 1)
            pe.wait_ge(s["ones_set"], 1)
            pe.wait_ge(s["ends_own"], 5)
            pe.matmul(ps[:, 2, 0:2 * B], ones[:, :], apart[:, :], start=True, stop=True).then_inc(s["spread"], 1)
            pe.wait_ge(s["e_ready"], 1)
            pe.wait_ge(s["s2_copied"], 1)
            pe.transpose(ps[:, 0, 0:P], erow[:, 0].rearrange("p b t -> p (b t)"),
                         ident[:, :]).then_inc(s["e_turned"], 1)

        @block.vector
        def _(dve):
            own = s["ends_own"]
            dve.tensor_reduce(ends[:, 0], s2[:, :, :], AX.X, ALU.max).then_inc(own, 1)
            dve.tensor_reduce(ends[:, 1], s2[:, :, :], AX.X, ALU.min).then_inc(own, 1)
            dve.wait_ge(own, 2)
            dve.tensor_scalar(ends[:, 1], ends[:, 1], -1.0, None, ALU.mult).then_inc(own, 1)
            dve.wait_ge(s["ends_turned"], 1)
            dve.tensor_reduce(ends_T[:, :], ps[0:2 * B, 1, 0:P], AX.X, ALU.max).then_inc(own, 1)
            dve.wait_ge(own, 4)
            dve.tensor_scalar(apart[:, :], ident[0:2 * B, 0:2 * B], ends_T[:, 0:1], None, ALU.mult).then_inc(own, 1)
            dve.wait_ge(s["spread"], 1)
            dve.tensor_scalar(bounds[:, 0], ps[:, 2, 0:B], 1.0, None, ALU.mult).then_inc(s["known"], 1)
            dve.tensor_scalar(bounds[:, 1], ps[:, 2, B:2 * B], -1.0, None, ALU.mult).then_inc(s["known"], 1)
            dve.wait_ge(s["known"], 2)
            dve.tensor_tensor(dist[:, 0], s1[:, :, :], over(bounds[:, 0], T), ALU.add).then_inc(s["drawn"], 1)
            dve.tensor_tensor(dist[:, 1], s2[:, :, :], over(bounds[:, 0], T), ALU.subtract).then_inc(s["drawn"], 1)
            dve.wait_ge(s["drawn"], 2)
            dve.tensor_scalar(dist[:, 0], dist[:, 0], 0.0, ALPHA - 1.0, ALU.max, ALU.mult).then_inc(s["drawn"], 1)
            dve.tensor_tensor(bounds[:, 2], bounds[:, 0], bounds[:, 1], ALU.subtract).then_inc(s["known"], 1)
            dve.wait_ge(s["known"], 3)
            dve.tensor_reduce(wide[:, :], bounds[:, 2], AX.X, ALU.max).then_inc(s["known"], 1)
            dve.wait_ge(s["known"], 4)
            dve.tensor_scalar(shared["is_wide"][:, :], wide[:, :], SPREAD, None, ALU.is_gt)
            dve.wait_ge(s["e_ready"], 2)
            dve.tensor_scalar(factors[:, 1], factors[:, 0], -1.0, None, ALU.mult)


def wide_flag(eng, shared):
    return eng.value_load(shared["is_wide"][0:1, 0:1], min_val=0, max_val=1)


def attention_near(prog, io, keep, shared):
    nc = prog.nc
    BANK = 3
    NBANK = -(-T // BANK)
    DEPTH = 4
    QUARTERS, QT = 4, T // 4
    TURN, PROJECT, ADD, COPY = ([k + 2 * q for q in range(QUARTERS)] for k in (1, 2, 4, 4))
    DIVIDE, COLUMNS = 2, 8
    NORMALISE = {13: (0, 6), 14: (6, 11), 15: (11, 16)}
    batch_view = lambda d: d.rearrange("t p b f -> b p t f")
    mT, factors, wsb = shared["mT"], shared["factors"], shared["wsb"]
    with ExitStack() as ctx:
        hb = prog.sb(ctx, "n_hb", [P, 2, T, D + 1])
        row = prog.sb(ctx, "n_row", [P, 2, N])
        cols = prog.sb(ctx, "n_cols", [P, 2, 3, T])
        e = prog.sb(ctx, "n_e", [P, DEPTH, N])
        pr = prog.sb(ctx, "n_p", [P, DEPTH, N])
        u = prog.sb(ctx, "n_u", [P, T, D])
        ut = prog.sb(ctx, "n_ut", [P, QT, P])
        xt = prog.sb(ctx, "n_xt", [P, T, D])
        hn = prog.sb(ctx, "n_hn", [P, T, D])
        rec = prog.sb(ctx, "n_rec", [P, NBANK * BANK])
        acc = prog.ps(ctx, "n_acc", [P, NBANK, 512])
        pq = prog.ps(ctx, "n_pq", [P, 2, 512])
        ln = LayerNorm(prog, ctx, "nln", T)
        ident = keep["ident"]
        sem, sems = (lambda s: prog.sem(f"n_{s}")), (lambda s: prog.sems(f"n_{s}"))
        ones_set, cols_set = sem("ones_set"), sem("cols_set")
        h_in, r_in = sems("h_in"), sems("r_in")
        raised, masked, used = sem("raised"), sem("masked"), sem("used")
        rec_own, normed = sem("rec_own"), sem("normed")
        u_turned, ut_ready, projected = sem("u_turned"), sem("ut_ready"), sem("projected")
        x_in, x_done, x_out = sem("x_in"), sem("x_done"), sem("x_out")
        h_done, h_out = sem("h_done"), sem("h_out")
        block = ctx.enter_context(nc.Block())

        def batches(eng, slot):
            run_slots(eng, slot, B + 1, 2, 3)

        @block.sync
        def _(sp):
            with sp.If(wide_flag(sp, shared) == 0):
                def inputs(b):
                    if b.within(2, B):
                        sp.wait_ge(raised, b.n * T - T)
                    sp.dma_start(row[:, b.par], io["erow"].rearrange("(b t) j -> b (t j)", b=B)[b.n]
                                 .partition_broadcast(P)).then_inc(r_in[b.par], 16)
                    if b.within(2, B):
                        sp.wait_ge(used, b.n * T - T)
                    sp.dma_start(hb[:, b.par, :, 0:D], batch_view(io["h1"])[b.n]).then_inc(h_in[b.par], 16)

                def store(b):
                    sp.wait_ge(x_done, b.n * QUARTERS + QUARTERS)
                    sp.dma_start(batch_view(io["x2"])[b.n], xt[:, :, :]).then_inc(x_out, 16)
                    sp.wait_ge(h_done, b.n + 1)
                    sp.dma_start(batch_view(io["h2"])[b.n], hn[:, :, :]).then_inc(h_out, 16)

                inputs(Tile(0))

                def slot(b):
                    if b.within(0, B - 1):
                        inputs(b + 1)
                    if b.within(2, B + 1):
                        store(b - 2)
                    if b.within(1, B + 1):
                        if b.within(2, B + 1):
                            sp.wait_ge(x_out, b.n * 16 - 16)
                        sp.dma_start(xt[:, :, :], batch_view(io["x1"])[b.n - 1]).then_inc(x_in, 16)
                batches(sp, slot)
                store(Tile(B - 1))
                sp.wait_ge(x_out, 16 * B)
                sp.wait_ge(h_out, 16 * B)

        @block.gpsimd
        def _(pool):
            with pool.If(wide_flag(pool, shared) == 0):
                ln.pool_setup(pool)
                pool.memset(hb[:, :, :, D:D + 1], 1.0).then_inc(ones_set, 1)
                run_slots(pool, lambda b: ln.pool(pool, b.n, h_done, b.within(1, B)), B, 2, 2)

        @block.scalar
        def _(act):
            with act.If(wide_flag(act, shared) == 0):
                def copy_turned(b, q):
                    act.wait_ge(u_turned, b.n * QUARTERS + q + 1)
                    act.activation(ut[:, :, :], pq[:, 0, :].rearrange("p (c j) -> p c j", j=P),
                                   ACT.Copy).then_inc(ut_ready, 1)

                def normalise(b, blocks):
                    if blocks[0] == 0 and b.within(1, B):
                        act.wait_ge(h_out, b.n * 16)
                    ln.scalar(act, b.n, xt[:, :, :], hn[:, :, :], h_done, blocks)

                def raise_over(b, j):
                    if j == 0:
                        act.wait_ge(cols_set, b.n + 1)
                        act.wait_ge(r_in[b.par], b.pair * 16 + 16)
                    if j >= DEPTH or b.within(1, B):
                        act.wait_ge(masked, b.n * T + j - DEPTH + 1)
                    act.activation(e[:, j % DEPTH], row[:, b.par], ACT.Relu, bias=cols[:, b.par, 1, j:j + 1],
                                   scale=cols[:, b.par, 2, j:j + 1]).then_inc(raised, 1)

                def slot(b):
                    for j in range(T):
                        if b.within(0, B):
                            raise_over(b, j)
                        if b.within(1, B + 1) and j in COPY:
                            copy_turned(b - 1, COPY.index(j))
                        if b.within(1, B + 1) and j in NORMALISE:
                            normalise(b - 1, NORMALISE[j])
                batches(act, slot)

        @block.vector
        def _(dve):
            with dve.If(wide_flag(dve, shared) == 0):
                def columns(b):
                    if b.within(2, B):
                        dve.wait_ge(raised, b.n * T - T)
                    dve.tensor_scalar(cols[:, b.par], factors[:, :, b.n, :], 1.0, None, ALU.mult)\
                       .then_inc(cols_set, 1)

                def mask(b, j):
                    if j == 0:
                        dve.wait_ge(cols_set, b.n + 1)
                        if b.i is None and b.off == 0:
                            dve.wait_ge(shared["mT_in"], 16 * T)
                    if j >= DEPTH or b.within(1, B):
                        dve.wait_ge(used, b.n * T + j - DEPTH + 1)
                    dve.wait_ge(raised, b.n * T + j + 1)
                    dve.scalar_tensor_tensor(pr[:, j % DEPTH].rearrange("p (c i) -> p c i", i=P),
                                             e[:, j % DEPTH].rearrange("p (c i) -> p c i", i=P),
                                             cols[:, b.par, 0, j:j + 1], mT[:, :, j],
                                             ALU.add, ALU.mult).then_inc(masked, 1)

                def divide(b):
                    own = Chain(dve, rec_own, NBANK)
                    own.step(b.n)
                    dve.wait_ge(used, b.n * T + T)
                    for k in range(NBANK):
                        n = min(BANK, T - k * BANK)
                        if k == 0 and b.within(1, B):
                            dve.wait_ge(u_turned, b.n * QUARTERS)
                        a3 = acc[:, k, 0:n * (D + 1)].rearrange("p (c j) -> p c j", j=D + 1)
                        own.link(dve.reciprocal(rec[:, k * BANK:k * BANK + n], a3[:, :, D]))
                        dve.tensor_tensor(u[:, k * BANK:k * BANK + n], a3[:, :, 0:D],
                                          over(rec[:, k * BANK:k * BANK + n], D), ALU.mult).then_inc(normed, 1)

                def add(b, q):
                    if q == 0:
                        dve.wait_ge(x_in, b.n * 16 + 16)
                    dve.wait_ge(projected, b.n * QUARTERS + q + 1)
                    xq = xt[:, QT * q:QT * q + QT]
                    dve.tensor_tensor(xq, pq[:, 1, :].rearrange("p (c j) -> p c j", j=D), xq, ALU.add)\
                       .then_inc(x_done, 1)

                columns(Tile(0))

                def slot(b):
                    for j in range(T):
                        if b.within(0, B):
                            mask(b, j)
                        if b.within(1, B + 1) and j == DIVIDE:
                            divide(b - 1)
                        if b.within(1, B + 1) and j in ADD:
                            q = ADD.index(j)
                            add(b - 1, q)
                            dve.wait_ge(x_done, b.n * QUARTERS - QUARTERS + q + 1)
                            ln.vector(dve, b.n - 1, xt[:, :, :], b.within(2, B + 1), (QT * q, QT * q + QT))
                        if b.within(0, B - 1) and j == COLUMNS:
                            columns(b + 1)
                batches(dve, slot)

        @block.tensor
        def _(pe):
            with pe.If(wide_flag(pe, shared) == 0):
                pe.wait_ge(shared["w_in"], 16)
                pe.wait_ge(ones_set, 1)

                def accumulate(b, j):
                    if j == 0:
                        pe.wait_ge(h_in[b.par], b.pair * 16 + 16)
                    pe.wait_ge(masked, b.n * T + j + 1)
                    for t in range(T):
                        k, o = t // BANK, (t % BANK) * (D + 1)
                        if j == 0 and o == 0 and b.within(1, B):
                            pe.wait_ge(normed, (b.n - 1) * NBANK + k + 1)
                        last = pe.matmul(acc[:, k, o:o + D + 1], pr[:, j % DEPTH, t * P:(t + 1) * P],
                                         hb[:, b.par, j], start=(j == 0 and o == 0), stop=(j == T - 1),
                                         skip_group_check=True)
                    last.then_inc(used, 1)

                def turn(b, q):
                    if q == 0:
                        pe.wait_ge(normed, (b.n + 1) * NBANK)
                    for c in range(QT):
                        last = pe.transpose(pq[:, 0, c * P:(c + 1) * P], u[:, QT * q + c], ident[:, :])
                    last.then_inc(u_turned, 1)

                def project(b, q):
                    pe.wait_ge(ut_ready, b.n * QUARTERS + q + 1)
                    if q or b.within(1, B):
                        pe.wait_ge(x_done, b.n * QUARTERS + q)
                    for c in range(QT):
                        last = pe.matmul(pq[:, 1, c * D:(c + 1) * D], ut[:, c], wsb[:, :], start=True, stop=True)
                    last.then_inc(projected, 1)

                def slot(b):
                    for j in range(T):
                        if b.within(0, B):
                            accumulate(b, j)
                        if b.within(1, B + 1) and j in TURN:
                            turn(b - 1, TURN.index(j))
                        if b.within(1, B + 1) and j in PROJECT:
                            project(b - 1, PROJECT.index(j))
                batches(pe, slot)


def attention_wide(prog, io, keep, shared):
    nc = prog.nc
    BANK = 3
    NBANK = -(-T // BANK)
    QUARTERS, QT = 4, T // 4
    TURN, PROJECT, COPY, ADD = ([k + 2 * q for q in range(QUARTERS)] for k in (2, 3, 4, 5))
    MEASURE, NORMALISE, MAXIMA, TURN_ROWS, COPY_ROWS = 12, {13: (0, 6), 14: (6, 11), 15: (11, 16)}, 8, 10, 11
    batch_view = lambda d: d.rearrange("t p b f -> b p t f")
    mT, wsb, bounds = shared["mT"], shared["wsb"], shared["bounds"]
    with ExitStack() as ctx:
        mrow = prog.sb(ctx, "c_mrow", [P, T, N], U8)
        hb = prog.sb(ctx, "c_hb", [P, 2, T, D + 1])
        s2row = prog.sb(ctx, "c_s2row", [P, N])
        rows = prog.sb(ctx, "c_rows", [P, 2, 2, N])
        z = prog.sb(ctx, "c_z", [P, 2, N])
        e = prog.sb(ctx, "c_e", [P, 2, N])
        pr = prog.sb(ctx, "c_p", [P, 2, N])
        u = prog.sb(ctx, "c_u", [P, T, D])
        ut = prog.sb(ctx, "c_ut", [P, QT, P])
        xt = prog.sb(ctx, "c_xt", [P, T, D])
        hn = prog.sb(ctx, "c_hn", [P, T, D])
        cols = prog.sb(ctx, "c_cols", [P, 2, 2, T])
        mtmp = prog.sb(ctx, "c_mtmp", [P, 3, T])
        low = prog.sb(ctx, "c_low", [P, 2])
        rcol = prog.sb(ctx, "c_rcol", [P, 2, T])
        rT = prog.sb(ctx, "c_rT", [2 * T, P])
        rec = prog.sb(ctx, "c_rec", [P, NBANK * BANK])
        acc = prog.ps(ctx, "c_acc", [P, NBANK, 512])
        pq = prog.ps(ctx, "c_pq", [P, 2, 512])
        ln = LayerNorm(prog, ctx, "cln", T)
        ident = keep["ident"]
        sem, sems = (lambda s: prog.sem(f"c_{s}")), (lambda s: prog.sems(f"c_{s}"))
        ones_set, mrow_set, adj_in = sem("ones_set"), sem("mrow_set"), sems("adj_in")
        h_in, row_in = sems("h_in"), sem("row_in")
        max_own, maxed = sem("max_own"), sem("maxed")
        r_turned, r_copied, r_out, r_in = sem("r_turned"), sem("r_copied"), sem("r_out"), sems("r_in")
        z_ready, exped, masked, used = sem("z_ready"), sem("exped"), sem("masked"), sem("used")
        rec_own, normed = sem("rec_own"), sem("normed")
        u_turned, ut_ready, projected = sem("u_turned"), sem("ut_ready"), sem("projected")
        x_in, x_done, x_out = sem("x_in"), sem("x_done"), sem("x_out")
        h_done, h_out = sem("h_done"), sem("h_out")
        block = ctx.enter_context(nc.Block())

        def batches(eng, slot):
            run_slots(eng, slot, B + 1, 2, 3)

        @block.sync
        def _(sp):
            with sp.If(wide_flag(sp, shared) == 1):
                def inputs(b):
                    if b.within(1, B):
                        sp.wait_ge(maxed, b.n * (T + 1))
                    sp.dma_start(s2row[:, :], io["s2row"].rearrange("(b t) j -> b (t j)", b=B)[b.n]
                                 .partition_broadcast(P)).then_inc(row_in, 16)
                    if b.within(2, B):
                        sp.wait_ge(used, b.n * T - T)
                    sp.dma_start(hb[:, b.par, :, 0:D], batch_view(io["h1"])[b.n]).then_inc(h_in[b.par], 16)

                def spread_rows(b):
                    sp.wait_ge(r_copied, b.n + 1)
                    sp.dma_start(io["rrow"], rT[:, :]).then_inc(r_out, 16)
                    sp.wait_ge(r_out, b.n * 16 + 16)
                    if b.within(2, B):
                        sp.wait_ge(z_ready, b.n * T - T)
                    for k in range(2):
                        sp.dma_start(rows[:, b.par, k], io["rrow"].rearrange("(k t) j -> k (t j)", k=2)[k]
                                     .partition_broadcast(P)).then_inc(r_in[b.par], 16)

                def store(b):
                    sp.wait_ge(h_done, b.n + 1)
                    sp.dma_start(batch_view(io["h2"])[b.n], hn[:, :, :]).then_inc(h_out, 16)
                    sp.dma_start(batch_view(io["x2"])[b.n], xt[:, :, :]).then_inc(x_out, 16)

                inputs(Tile(0))
                spread_rows(Tile(0))

                def slot(b):
                    if b.within(0, B - 1):
                        inputs(b + 1)
                    if b.within(2, B + 1):
                        store(b - 2)
                    if b.within(1, B + 1):
                        if b.within(2, B + 1):
                            sp.wait_ge(x_out, b.n * 16 - 16)
                        sp.dma_start(xt[:, :, :], batch_view(io["x1"])[b.n - 1]).then_inc(x_in, 16)
                    if b.within(0, B - 1):
                        spread_rows(b + 1)
                batches(sp, slot)
                store(Tile(B - 1))
                sp.wait_ge(x_out, 16 * B)
                sp.wait_ge(h_out, 16 * B)

        @block.gpsimd
        def _(pool):
            with pool.If(wide_flag(pool, shared) == 1):
                ln.pool_setup(pool)
                pool.memset(hb[:, :, :, D:D + 1], 1.0).then_inc(ones_set, 1)
                run_slots(pool, lambda b: ln.pool(pool, b.n, h_done, b.within(1, B)), B, 2, 2)

        @block.scalar
        def _(act):
            with act.If(wide_flag(act, shared) == 1):
                for t in range(T):
                    if t >= 2:
                        act.wait_ge(mrow_set, t - 1)
                    act.dma_start(pr[:, t % 2], io["adj"][t * P:(t + 1) * P, :]).then_inc(adj_in[t % 2], 16)

                def copy_rows(b):
                    act.wait_ge(r_turned, b.n + 1)
                    act.activation(rT[:, :], pq[0:2 * T, 0, 0:P], ACT.Copy).then_inc(r_copied, 1)

                def copy_turned(b, q):
                    act.wait_ge(u_turned, b.n * QUARTERS + q + 1)
                    act.activation(ut[:, :, :], pq[:, 0, :].rearrange("p (c j) -> p c j", j=P),
                                   ACT.Copy).then_inc(ut_ready, 1)

                def normalise(b, blocks):
                    if blocks[0] == 0 and b.within(1, B):
                        act.wait_ge(h_out, b.n * 16)
                    ln.scalar(act, b.n, xt[:, :, :], hn[:, :, :], h_done, blocks)

                copy_rows(Tile(0))

                def slot(b):
                    for j in range(T):
                        if b.within(0, B):
                            act.wait_ge(z_ready, b.n * T + j + 1)
                            if j >= 2 or b.within(1, B):
                                act.wait_ge(masked, b.n * T + j - 1)
                            act.activation(e[:, j % 2], z[:, j % 2], ACT.Exp,
                                           bias=cols[:, b.par, 0, j:j + 1]).then_inc(exped, 1)
                        if b.within(1, B + 1) and j in COPY:
                            copy_turned(b - 1, COPY.index(j))
                        if b.within(0, B - 1) and j == COPY_ROWS:
                            copy_rows(b + 1)
                        if b.within(1, B + 1) and j in NORMALISE:
                            normalise(b - 1, NORMALISE[j])
                batches(act, slot)

        @block.vector
        def _(dve):
            with dve.If(wide_flag(dve, shared) == 1):
                def maxima(b):
                    m, tmp, carrier = (mtmp[:, k] for k in range(3))
                    s1, s2 = keep["s1"][:, b.n, :], keep["s2"][:, b.n, :]
                    own = Chain(dve, max_own, 5)
                    own.step(b.n)
                    own.link(dve.tensor_scalar(low[:, 0:2], bounds[:, 1:3, bass.ds(b.n, 1)].squeeze(2), 1.0, None,
                                               ALU.mult))
                    if b.within(2, B):
                        dve.wait_ge(exped, b.n * T - T)
                    dve.tensor_scalar(cols[:, b.par, 0], s2, 1.0, None, ALU.mult)
                    dve.wait_ge(row_in, b.n * 16 + 16)
                    dve.tensor_scalar(cols[:, b.par, 1], s2, ALPHA - 1.0, None, ALU.mult)
                    dve.tensor_scalar(s2row[:, :], s2row[:, :], low[:, 0:1], None,
                                      ALU.subtract).then_inc(maxed, 1)
                    for t in range(T):
                        dve.wait_ge(maxed, b.n * (T + 1) + t + 1)
                        dve.memset(carrier[:, t:t + 1], 0.0)
                        dve.tensor_tensor_reduce(rows[:, b.par, t % 2], s2row[:, :], mrow[:, t], 1.0, 0.0,
                                                 ALU.mult, ALU.max, m[:, t:t + 1]).then_inc(maxed, 1)
                    dve.wait_ge(maxed, (b.n + 1) * (T + 1))
                    own.link(dve.scalar_tensor_tensor(tmp, m, low[:, 0:1], s1, ALU.add, ALU.add))
                    own.link(dve.scalar_tensor_tensor(m, tmp, ALPHA, tmp, ALU.mult, ALU.max))
                    dve.tensor_tensor(rcol[:, 0], s1, m, ALU.subtract)
                    own.link(dve.tensor_scalar(tmp, s1, ALPHA, None, ALU.mult))
                    own.link(dve.tensor_tensor(rcol[:, 1], tmp, m, ALU.subtract))

                def exponents(b, j):
                    if j == 0:
                        dve.wait_ge(r_in[b.par], b.pair * 32 + 32)
                    if j >= 2 or b.within(1, B):
                        dve.wait_ge(exped, b.n * T + j - 1)
                    dve.scalar_tensor_tensor(z[:, j % 2], rows[:, b.par, 1], cols[:, b.par, 1, j:j + 1],
                                             rows[:, b.par, 0], ALU.add, ALU.max).then_inc(z_ready, 1)

                def mask(b, j):
                    if j == 0 and b.off == 0 and b.i is None:
                        dve.wait_ge(shared["mT_in"], 16 * T)
                    dve.wait_ge(exped, b.n * T + j + 1)
                    if j >= 2 or b.within(1, B):
                        dve.wait_ge(used, b.n * T + j - 1)
                    dve.tensor_tensor(pr[:, j % 2].rearrange("p (c i) -> p c i", i=P),
                                      e[:, j % 2].rearrange("p (c i) -> p c i", i=P), mT[:, :, j],
                                      ALU.mult).then_inc(masked, 1)

                def divide(b):
                    own = Chain(dve, rec_own, NBANK)
                    own.step(b.n)
                    dve.wait_ge(used, b.n * T + T)
                    for k in range(NBANK):
                        n = min(BANK, T - k * BANK)
                        a3 = acc[:, k, 0:n * (D + 1)].rearrange("p (c j) -> p c j", j=D + 1)
                        own.link(dve.reciprocal(rec[:, k * BANK:k * BANK + n], a3[:, :, D]))
                        dve.tensor_tensor(u[:, k * BANK:k * BANK + n], a3[:, :, 0:D],
                                          over(rec[:, k * BANK:k * BANK + n], D), ALU.mult).then_inc(normed, 1)

                def add(b, q):
                    if q == 0:
                        dve.wait_ge(x_in, b.n * 16 + 16)
                    dve.wait_ge(projected, b.n * QUARTERS + q + 1)
                    xq = xt[:, QT * q:QT * q + QT]
                    dve.tensor_tensor(xq, pq[:, 1, :].rearrange("p (c j) -> p c j", j=D), xq, ALU.add)\
                       .then_inc(x_done, 1)

                for t in range(T):
                    dve.wait_ge(adj_in[t % 2], t // 2 * 16 + 16)
                    dve.tensor_scalar(mrow[:, t], pr[:, t % 2], 0.0, None, ALU.not_equal).then_inc(mrow_set, 1)
                dve.wait_ge(mrow_set, T)
                maxima(Tile(0))

                def slot(b):
                    for j in range(T):
                        if b.within(0, B):
                            exponents(b, j)
                            if j >= 2:
                                mask(b, j - 1)
                        if b.within(1, B + 1) and j == 0:
                            mask(b - 1, T - 1)
                        if b.within(1, B + 1) and j == 1:
                            divide(b - 1)
                        if b.within(0, B) and j == 1:
                            mask(b, 0)
                        if b.within(1, B + 1) and j in ADD:
                            add(b - 1, ADD.index(j))
                        if b.within(1, B + 1) and j == MEASURE:
                            dve.wait_ge(x_done, b.n * QUARTERS)
                            ln.vector(dve, b.n - 1, xt[:, :, :], b.within(2, B + 1))
                        if b.within(0, B - 1) and j == MAXIMA:
                            maxima(b + 1)
                batches(dve, slot)

        @block.tensor
        def _(pe):
            with pe.If(wide_flag(pe, shared) == 1):
                pe.wait_ge(shared["w_in"], 16)
                pe.wait_ge(ones_set, 1)

                def turn_rows(b):
                    pe.wait_ge(max_own, b.n * 5 + 5)
                    pe.transpose(pq[0:2 * T, 0, 0:P], rcol[:, :, :].rearrange("p k t -> p (k t)"),
                                 ident[:, :]).then_inc(r_turned, 1)

                def accumulate(b, j):
                    if j == 0:
                        pe.wait_ge(h_in[b.par], b.pair * 16 + 16)
                        if b.within(1, B):
                            pe.wait_ge(normed, b.n * NBANK)
                    pe.wait_ge(masked, b.n * T + j + 1)
                    for t in range(T):
                        k, o = t // BANK, (t % BANK) * (D + 1)
                        last = pe.matmul(acc[:, k, o:o + D + 1], pr[:, j % 2, t * P:(t + 1) * P],
                                         hb[:, b.par, j], start=(j == 0 and o == 0), stop=(j == T - 1),
                                         skip_group_check=True)
                    last.then_inc(used, 1)

                def turn(b, q):
                    if q == 0:
                        pe.wait_ge(normed, (b.n + 1) * NBANK)
                        pe.wait_ge(r_copied, b.n + 1)
                    for c in range(QT):
                        last = pe.transpose(pq[:, 0, c * P:(c + 1) * P], u[:, QT * q + c], ident[:, :])
                    last.then_inc(u_turned, 1)

                def project(b, q):
                    pe.wait_ge(ut_ready, b.n * QUARTERS + q + 1)
                    if q:
                        pe.wait_ge(x_done, b.n * QUARTERS + q)
                    for c in range(QT):
                        last = pe.matmul(pq[:, 1, c * D:(c + 1) * D], ut[:, c], wsb[:, :], start=True, stop=True)
                    last.then_inc(projected, 1)

                turn_rows(Tile(0))

                def slot(b):
                    for j in range(T):
                        if b.within(0, B):
                            accumulate(b, j)
                        if b.within(1, B + 1) and j in TURN:
                            turn(b - 1, TURN.index(j))
                        if b.within(1, B + 1) and j in PROJECT:
                            project(b - 1, PROJECT.index(j))
                        if b.within(0, B - 1) and j == TURN_ROWS:
                            turn_rows(b + 1)
                batches(pe, slot)


def lstm_units():
    units = []
    for p in range(1, SKIP + 1):
        windows = N // p
        parts = -(-windows // 512)
        size = -(-windows // parts)
        size += size % 2
        for w0 in range(0, windows, size):
            for q in range(p):
                units.append((p, w0, min(size, windows - w0), q))
    return units


def recurrences(prog, io, keep, weights):
    nc = prog.nc
    units = lstm_units()
    NU = len(units)
    GATES = {True: (2, 0, 3), False: (2, 0, 1, 3)}
    gates = [GATES[q == 0] for _, _, _, q in units]
    before = [sum(len(g) for g in gates[:k]) for k in range(NU + 1)]
    NG = before[NU]
    with ExitStack() as ctx:
        G4 = 4 * D
        w_hi = prog.sb(ctx, "r_w_hi", [P, 2, SKIP, G4], F32R)
        w_lo = prog.sb(ctx, "r_w_lo", [P, 2, SKIP, G4], F32R)
        bias = prog.sb(ctx, "r_bias", [P, 3, SKIP, 4])
        pair = range(2)
        raw = [prog.sb(ctx, f"r_raw{k}", [P, N]) for k in pair]
        raw_hi = [prog.sb(ctx, f"r_raw_hi{k}", [P, N], F32R) for k in pair]
        raw_lo = [prog.sb(ctx, f"r_raw_lo{k}", [P, N], F32R) for k in pair]
        hx = [prog.sb(ctx, f"r_hx{k}", [P, N]) for k in pair]
        hx_hi = [prog.sb(ctx, f"r_hx_hi{k}", [P, N], F32R) for k in pair]
        hx_lo = [prog.sb(ctx, f"r_hx_lo{k}", [P, N], F32R) for k in pair]
        gate = [prog.sb(ctx, f"r_gate{k}", [P, 4, 512]) for k in pair]
        cell = [prog.sb(ctx, f"r_cell{k}", [P, 2, 512]) for k in pair]
        tc = [prog.sb(ctx, f"r_tc{k}", [P, 512]) for k in pair]
        st = [prog.sb(ctx, f"r_st{k}", [P, 512]) for k in pair]
        st_hi = [prog.sb(ctx, f"r_st_hi{k}", [P, 512], F32R) for k in pair]
        st_lo = [prog.sb(ctx, f"r_st_lo{k}", [P, 512], F32R) for k in pair]
        xt = [prog.sb(ctx, f"r_xt{k}", [P, T, D]) for k in pair]
        hn = prog.sb(ctx, "r_hn", [P, T, D])[:, :, :]
        hn_last = raw[0][:, :].rearrange("p (t f) -> p t f", f=D)
        ps = [prog.ps(ctx, f"r_ps{k}", [P, 4, 512]) for k in pair]
        ident = keep["ident"]
        ln = LayerNorm(prog, ctx, "rln", T)
        sem, sems = (lambda s: prog.sem(f"r_{s}")), (lambda s: prog.sems(f"r_{s}"))
        w_in, b_in, w_high, w_split = sem("w_in"), sem("b_in"), sem("w_high"), sem("w_split")
        b_ready = sem("b_ready")
        h_in, raw_high, raw_split = sems("h_in"), sems("raw_high"), sems("raw_split")
        summed, activated = sems("summed"), sems("activated")
        own, cell_ready, squashed = sems("own"), sems("cell_ready"), sems("squashed")
        state, high, low = sems("state"), sems("high"), sems("low")
        x_in, x_out = sems("x_in"), sems("x_out")
        turned, x_done, h_done, h_out, last_out = (sem(s) for s in (
            "turned", "x_done", "h_done", "h_out", "last_out"))
        batch_view = lambda d: d.rearrange("t p b f -> b p t f")
        with ExitStack() as c1:
            block = c1.enter_context(nc.Block())

            @block.sync
            def _(sp):
                for k, name in enumerate(("wih", "whh")):
                    sp.dma_start(hx[k][:, :].rearrange("p (l g) -> p l g", g=G4), weights[name]).then_inc(w_in, 16)
                for k, name in enumerate(("bih", "bhh")):
                    sp.dma_start(bias[:, k], weights[name]).then_inc(b_in, 16)
                for k in pair:
                    sp.dma_start(raw[k][:, :], io["hT"][k]).then_inc(h_in[k], 16)

            @block.scalar
            def _(act):
                act.wait_ge(w_in, 32)
                for k in range(2):
                    act.activation(w_hi[:, k].rearrange("p l g -> p (l g)"), hx[k][:, :], ACT.Copy).then_inc(w_high, 1)
                for k in pair:
                    act.wait_ge(h_in[k], 16)
                    act.activation(raw_hi[k][:, :], raw[k][:, :], ACT.Copy).then_inc(raw_high[k], 1)

            @block.vector
            def _(dve):
                dve.wait_ge(b_in, 32)
                dve.tensor_tensor(bias[:, 2], bias[:, 0], bias[:, 1], ALU.add).then_inc(b_ready, 1)
                for k in range(2):
                    dve.wait_ge(w_high, k + 1)
                    dve.tensor_tensor(w_lo[:, k].rearrange("p l g -> p (l g)"), hx[k][:, :],
                                      w_hi[:, k].rearrange("p l g -> p (l g)").bitcast(F32),
                                      ALU.subtract).then_inc(w_split, 1)
                for k in pair:
                    dve.wait_ge(raw_high[k], 1)
                    dve.tensor_tensor(raw_lo[k][:, :], raw[k][:, :], raw_hi[k][:, :].bitcast(F32),
                                      ALU.subtract).then_inc(raw_split[k], 1)
        block = ctx.enter_context(nc.Block())
        NPAIR = B // 2
        NRAW = sum(u[0] == 1 for u in units)
        SPLIT = {NRAW + 5: 0, NRAW + 12: 1}
        NL = NU - 1
        PARTS = [(t, t + 4) for t in range(0, T, 4)]
        MEASURE = {n: (n // 4, PARTS[n % 4]) for n in range(8)}
        NORMALISE = {**{5 + n: (0, part) for n, part in enumerate(PARTS)},
                     **{12 + n: (1, part) for n, part in enumerate(PARTS)}}

        def pairs(eng, slot, peeled=2):
            for i in range(peeled):
                slot(i, True, i > 0)
            with eng.Fori(peeled, NPAIR) as i:
                slot(i, True, True)
            slot(NPAIR, False, True)

        def result(i, k):
            return hn_last if k and isinstance(i, int) and i == NPAIR - 1 else hn

        def later(i):
            return not isinstance(i, int) or i > 0

        def places(n):
            p, w0, size, q = units[n]
            return slice(w0 * p + q, w0 * p + q + (size - 1) * p + 1, p)

        def inputs_from(n):
            p, w0, size, _ = units[n]
            lo, hi = w0 * p, (w0 + size) * p
            return max(m for m, (p2, w2, s2, _) in enumerate(units)
                       if p2 == p - 1 and w2 * p2 < hi and (w2 + s2) * p2 > lo)

        def free(n):
            return units[n][3] == 0 and (units[n][0] == 1 or inputs_from(n) < n - 1)

        def turns(n):
            yield 0, ((n - 1, 1) if n and free(n) else None), free(n)
            yield 1, ((n, 0) if free(n) else None), n + 1 < NU and free(n + 1)

        @block.sync
        def _(sp):
            def load_x(i, k):
                sp.dma_start(xt[k][:, :, :], batch_view(io["x2"])[i * 2 + k]).then_inc(x_in[k], 16)

            def next_h(i):
                for k in pair:
                    sp.wait_ge(raw_split[k], i + 1)
                    sp.dma_start(raw[k][:, :], io["hT"][(i + 1) * 2 + k]).then_inc(h_in[k], 16)

            def store(i, load):
                for k in pair:
                    sp.wait_ge(x_done, i * 2 + k + 1)
                    sp.dma_start(batch_view(io["x3"])[i * 2 + k], xt[k][:, :, :]).then_inc(x_out[k], 16)
                for k in pair:
                    sp.wait_ge(h_done, i * 2 + k + 1)
                    out = h_out if result(i, k) is hn else last_out
                    sp.dma_start(batch_view(io["h3"])[i * 2 + k], result(i, k)).then_inc(out, 16)
                    if load:
                        sp.wait_ge(x_out[k], i * 16 + 16)
                        load_x(i + 1, k)

            for k in pair:
                load_x(0, k)
            next_h(0)
            with sp.Fori(1, NPAIR - 1) as i:
                next_h(i)
                store(i - 1, True)
            store(NPAIR - 2, True)
            store(NPAIR - 1, False)
            sp.wait_ge(h_out, 16 * (B - 1))
            sp.wait_ge(last_out, 16)
            for k in pair:
                sp.wait_ge(x_out[k], 16 * NPAIR)

        @block.gpsimd
        def _(pool):
            ln.pool_setup(pool)

            def split_next(i):
                for k in pair:
                    pool.wait_ge(summed[k], i * NG + before[NRAW])
                    pool.wait_ge(raw_high[k], i + 2)
                    pool.tensor_tensor(raw_lo[k][:, :], raw[k][:, :], raw_hi[k][:, :].bitcast(F32),
                                       ALU.subtract).then_inc(raw_split[k], 1)

            split_next(0)
            for b in range(2):
                ln.pool(pool, b, h_done, b > 0)
            split_next(1)
            with pool.Fori(2, NPAIR - 1) as i:
                for k in pair:
                    ln.pool(pool, i * 2 - 2 + k, h_done, True)
                split_next(i)
            for b in range(B - 4, B):
                ln.pool(pool, b, h_done, True)

        @block.scalar
        def _(act):
            def evaluate(i, n, k, late):
                size = units[n][2]
                for j, g in enumerate(gates[n]):
                    if n > 0 or later(i):
                        if j == 0:
                            act.wait_ge(cell_ready[k], i * NU + n)
                        if g == 3:
                            act.wait_ge(state[k], i * NU + n)
                    act.wait_ge(summed[k], i * NG + before[n] + j + 1)
                    act.activation(gate[k][:, g, 0:size], ps[k][:, g, 0:size],
                                   ACT.Tanh if g == 2 else ACT.Sigmoid,
                                   bias=bias[:, 2, units[n][0] - 1, g:g + 1]).then_inc(activated[k], 1)
                    if late and j == 1:
                        squash(i, *late)

            def squash(i, n, k):
                size = units[n][2]
                act.wait_ge(cell_ready[k], i * NU + n + 1)
                act.activation(tc[k][:, 0:size], cell[k][:, 0, 0:size], ACT.Tanh).then_inc(squashed[k], 1)

            def normalise(i, k, blocks):
                b = i * 2 + k
                if blocks[0] == 0 and (k or later(i)) and result(i, k) is hn:
                    act.wait_ge(h_out, b * 16)
                ln.scalar(act, b, xt[k][:, :, :], result(i, k), h_done, blocks)

            def split_next(i, k):
                act.wait_ge(h_in[k], i * 16 + 32)
                act.activation(raw_hi[k][:, :], raw[k][:, :], ACT.Copy).then_inc(raw_high[k], 1)

            def slot(i, stream, rest):
                for n in range(NU):
                    if stream:
                        for k, late, put_off in turns(n):
                            evaluate(i, n, k, late)
                            if not put_off:
                                squash(i, n, k)
                    if rest and n in NORMALISE:
                        normalise(i - 1, *NORMALISE[n])
                    if n in SPLIT and isinstance(i, int) and i < NPAIR - 1:
                        split_next(i, SPLIT[n])
                    if n in SPLIT and not isinstance(i, int):
                        with act.If(i < NPAIR - 1):
                            split_next(i, SPLIT[n])
            pairs(act, slot)

        @block.vector
        def _(dve):
            def update(i, n, k):
                p, _, size, q = units[n]
                c, ig = cell[k][:, 0, 0:size], cell[k][:, 1, 0:size]
                ga = lambda g: gate[k][:, g, 0:size]
                at = i * NG + before[n]
                dve.wait_ge(activated[k], at + 2)
                if q == 0:
                    dve.tensor_tensor(c, ga(0), ga(2), ALU.mult).then_inc(cell_ready[k], 1)
                else:
                    done = sum(1 for u in units[:n] if u[3])
                    total = sum(1 for u in units if u[3])
                    own_at = (i * total + done) * 2
                    dve.tensor_tensor(ig, ga(0), ga(2), ALU.mult).then_inc(own[k], 1)
                    dve.wait_ge(activated[k], at + 3)
                    dve.tensor_tensor(c, ga(1), c, ALU.mult).then_inc(own[k], 1)
                    dve.wait_ge(own[k], own_at + 2)
                    dve.tensor_tensor(c, c, ig, ALU.add).then_inc(cell_ready[k], 1)

            def output(i, n, k):
                p, _, size, q = units[n]
                o, c = gate[k][:, 3, 0:size], tc[k][:, 0:size]
                h, hi, lo = (t[k][:, places(n)] for t in (hx, hx_hi, hx_lo)) if q == p - 1 else \
                    (t[k][:, 0:size] for t in (st, st_hi, st_lo))
                if n == 0 and later(i):
                    dve.wait_ge(summed[k], i * NG)
                dve.wait_ge(activated[k], i * NG + before[n + 1])
                dve.wait_ge(squashed[k], i * NU + n + 1)
                if n < NL:
                    dve.tensor_tensor(hi, o, c, ALU.mult).then_inc(high[k], 1)
                dve.tensor_tensor(h, o, c, ALU.mult).then_inc(state[k], 1)
                if n < NL:
                    dve.wait_ge(high[k], i * NL + n + 1)
                    dve.wait_ge(state[k], i * NU + n + 1)
                    dve.tensor_tensor(lo, h, hi.bitcast(F32), ALU.subtract).then_inc(low[k], 1)

            def add(i, k):
                dve.wait_ge(x_in[k], i * 16 + 16)
                dve.wait_ge(turned, i * 2 + k + 1)
                dve.tensor_tensor(xt[k][:, :, :], ps[k][:, :, :].rearrange("p g (c f) -> p (g c) f", f=D),
                                  xt[k][:, :, :], ALU.add).then_inc(x_done, 1)

            def slot(i, stream, rest):
                if rest:
                    add(i - 1, 0)
                    if stream:
                        add(i - 1, 1)
                for n in range(NU):
                    if stream:
                        for k, late, put_off in turns(n):
                            update(i, n, k)
                            if late:
                                output(i, *late)
                            if not put_off:
                                output(i, n, k)
                    if rest and n in MEASURE:
                        k, part = MEASURE[n]
                        if not stream and n == 4:
                            add(i - 1, 1)
                        if part[0] == 0:
                            dve.wait_ge(x_done, i * 2 - 1 + k)
                        ln.vector(dve, i * 2 - 2 + k, xt[k][:, :, :], k > 0 or later(i - 1), part)
            pairs(dve, slot)

        @block.tensor
        def _(pe):
            def gates_of(i, n, k):
                p, _, size, q = units[n]
                if n == 0:
                    pe.wait_ge(raw_split[k], i + 1)
                elif q == 0 and p > 1:
                    pe.wait_ge(low[k], i * NL + inputs_from(n) + 1)
                x_hi, x_lo = (raw_hi, raw_lo) if p == 1 else (hx_hi, hx_lo)
                x_parts = [(w_hi, x_hi), (w_hi, x_lo), (w_lo, x_hi)]
                h_parts = [(w_hi, st_hi), (w_hi, st_lo), (w_lo, st_hi)]
                if n == 0:
                    if later(i):
                        pe.wait_ge(x_done, i * 2 - 1 + k)
                else:
                    pe.wait_ge(activated[k], i * NG + before[n])
                for g in gates[n]:
                    for m, (w, h) in enumerate(x_parts):
                        last = pe.matmul(ps[k][:, g, 0:size], w[:, 0, p - 1, g * D:(g + 1) * D],
                                         h[k][:, places(n)], start=(m == 0), stop=(q == 0 and m == 2))
                    if q == 0:
                        last.then_inc(summed[k], 1)
                if q:
                    pe.wait_ge(low[k], i * NL + n)
                    for g in gates[n]:
                        for m, (w, h) in enumerate(h_parts):
                            last = pe.matmul(ps[k][:, g, 0:size], w[:, 1, p - 1, g * D:(g + 1) * D],
                                             h[k][:, 0:size], start=False, stop=(m == 2))
                        last.then_inc(summed[k], 1)

            def slot(i, stream, rest):
                if not stream:
                    return
                for n in range(NU):
                    for k in pair:
                        gates_of(i, n, k)
                for k in pair:
                    pe.wait_ge(activated[k], i * NG + NG)
                    pe.wait_ge(state[k], i * NU + NU)
                    for t in range(T):
                        last = pe.transpose(ps[k][:, t // 4, (t % 4) * D:(t % 4 + 1) * D],
                                            hx[k][:, t * P:(t + 1) * P], ident[:, :])
                    last.then_inc(turned, 1)
            pairs(pe, slot, 1)


def perceptron(prog, io, keep, weights, out):
    nc = prog.nc
    with ExitStack() as ctx:
        w2 = prog.sb(ctx, "m_w2", [P, 2, D])
        vec = prog.sb(ctx, "m_vec", [P, 9])
        z = prog.sb(ctx, "m_z", [P, 2, 2, W])
        hid = prog.sb(ctx, "m_hid", [P, 2, 2, W])
        o2 = prog.sb(ctx, "m_o2", [P, T, W])
        bn2 = prog.sb(ctx, "m_bn2", [P, 2 * T, 6])
        mv = prog.sb(ctx, "m_mv", [P, 3, 2])
        var = prog.sb(ctx, "m_var", [P, 3])
        aff = prog.sb(ctx, "m_aff", [P, 3, 4])
        carrier = prog.sb(ctx, "m_carrier", [P, 2])
        y = prog.sb(ctx, "m_y", [P, 2, W])
        x_all = prog.sb(ctx, "m_x_all", [P, T, B, D])
        po = prog.ps(ctx, "m_po", [P, 2, 512])
        pt = prog.ps(ctx, "m_pt", [P, 2, B, D])
        sem, sems = (lambda s: prog.sem(f"m_{s}")), (lambda s: prog.sems(f"m_{s}"))
        w_in, v_in, powered, aff_own = (sem(s) for s in ("w_in", "v_in", "powered", "aff_own"))
        z_in, x_in, x_out = sems("z_in"), sems("x_in"), sem("x_out")
        h_ready, o_summed, o_read = (sem(s) for s in ("h_ready", "o_summed", "o_read"))
        y_ready, turned, x_done = (sem(s) for s in ("y_ready", "turned", "x_done"))
        out_tiles = out.rearrange("b (t p) f -> t p b f", p=P)
        ident = keep["ident"]
        block = ctx.enter_context(nc.Block())

        @block.sync
        def _(sp):
            sp.dma_start(vec[:, :], weights["vec"]).then_inc(v_in, 16)
            sp.dma_start(w2[:, :, :], weights["w2"]).then_inc(w_in, 16)

            def load(t):
                if t.within(2, T):
                    sp.wait_ge(h_ready, t.n * 2 - 2)
                sp.dma_start(z[:, t.par], io["z1"][t.n]).then_inc(z_in[t.par], 16)
                if t.par == 0:
                    sp.dma_start(x_all[:, t.pair], io["x3"][t.pair]).then_inc(x_in[0], 16)
            run_slots(sp, load, T, 2, 2)
            for t in range(HALF, T):
                sp.dma_start(x_all[:, t], io["x3"][t]).then_inc(x_in[1], 16)

            def store(t):
                sp.wait_ge(x_done, t.n + 1)
                sp.dma_start(out_tiles[t.n], x_all[:, t.n]).then_inc(x_out, 16)
            run_slots(sp, store, T, 2, 2)
            sp.wait_ge(x_out, 16 * T)

        def affine(dve, j, stats, k0):
            step = Chain(dve, aff_own, 6)
            step.step(j)
            step.link(dve.bn_aggr(mv[:, j], stats))
            step.link(dve.tensor_scalar(var[:, j:j + 1], mv[:, j, 1:2], EPS, None, ALU.add))
            step.link(dve.tensor_tensor(aff[:, j, 2:3], mv[:, j, 0:1], vec[:, k0:k0 + 1], ALU.add))
            step.link(dve.tensor_tensor(aff[:, j, 3:4], vec[:, k0:k0 + 1], aff[:, j, 2:3], ALU.subtract))
            dve.wait_ge(powered, j + 1)
            step.link(dve.tensor_tensor(aff[:, j, 0:1], var[:, j:j + 1], vec[:, k0 + 1:k0 + 2], ALU.mult))
            step.link(dve.scalar_tensor_tensor(aff[:, j, 1:2], aff[:, j, 0:1], aff[:, j, 3:4],
                                               vec[:, k0 + 2:k0 + 3], ALU.mult, ALU.add))

        @block.gpsimd
        def _(pool):
            half = keep["halves"]
            for j in range(3):
                pool.wait_ge(aff_own, 6 * j + 2)
                pool.tensor_tensor(var[:, j:j + 1], var[:, j:j + 1], half[:, 0:1], ALU.pow).then_inc(powered, 1)

        @block.scalar
        def _(act):
            act.wait_ge(aff_own, 12)

            def hidden(t):
                for k in range(2):
                    if k == 0 and t.within(2, T):
                        act.wait_ge(o_summed, t.n * 2 - 2)
                    act.wait_ge(z_in[t.par], t.pair * 16 + 16)
                    act.activation(hid[:, t.par, k], z[:, t.par, k], ACT.Relu, bias=aff[:, k, 1:2],
                                   scale=aff[:, k, 0:1]).then_inc(h_ready, 1)
            run_slots(act, hidden, T, 2, 2)

            def final(t):
                if t.within(2, T):
                    act.wait_ge(turned, t.n - 1)
                    act.activation(carrier[:, t.par:t.par + 1], keep["ones"][:, 0:1], ACT.Copy)
                if t.i is None and t.off == 0:
                    act.wait_ge(aff_own, 18)
                act.activation(y[:, t.par], o2[:, t.n], ACT.Identity, bias=aff[:, 2, 1:2],
                               scale=aff[:, 2, 0:1]).then_inc(y_ready, 1)
            run_slots(act, final, T, 2, 2)

        @block.vector
        def _(dve):
            dve.wait_ge(v_in, 16)
            for k in range(2):
                affine(dve, k, keep["bn1"][:, k].rearrange("p c s -> p (c s)"), 3 * k)

            def collect(t):
                for c in range(2):
                    n = t.n * 2 + c
                    dve.wait_ge(o_summed, n + 1)
                    dve.tensor_scalar(o2[:, t.n, c * 512:(c + 1) * 512], po[:, c], 1.0, None, ALU.mult)
                    dve.bn_stats(bn2[:, n], po[:, c]).then_inc(o_read, 1)
            run_slots(dve, collect, T, 2, 2)
            dve.wait_ge(o_read, 2 * T)
            affine(dve, 2, bn2[:, :, :].rearrange("p c s -> p (c s)"), 6)
            def final(t):
                dve.wait_ge(turned, t.n + 1)
                dve.tensor_tensor(x_all[:, t.n], pt[:, t.par], x_all[:, t.n], ALU.add).then_inc(x_done, 1)
            for half in range(2):
                dve.wait_ge(x_in[half], 16 * HALF)
                run_slots(dve, lambda t: final(t + half * HALF), HALF, 2, 2)

        @block.tensor
        def _(pe):
            pe.wait_ge(w_in, 16)

            def multiply(t):
                for c in range(2):
                    for k in range(2):
                        pe.wait_ge(h_ready, t.n * 2 + k + 1)
                        if k == 0 and t.within(1, T):
                            pe.wait_ge(o_read, t.n * 2 + c - 1)
                        last = pe.matmul(po[:, c], w2[:, k], hid[:, t.par, k, c * 512:(c + 1) * 512],
                                         start=(k == 0), stop=(k == 1))
                    last.then_inc(o_summed, 1)
            run_slots(pe, multiply, T, 2, 2)

            def final(t):
                pe.wait_ge(y_ready, t.n + 1)
                if t.within(2, T):
                    pe.wait_ge(x_done, t.n - 1)
                for b in range(B):
                    last = pe.transpose(pt[:, t.par, b], y[:, t.par, b * P:(b + 1) * P], ident[:, :])
                last.then_inc(turned, 1)
            run_slots(pe, final, T, 2, 2)


def network(nc, x, adj, w0, wa, wcT, wc, wg0, bg0, wg1, bg1, wih, whh, bih, bhh, w1, w2, vec, out):
    with ExitStack() as ctx:
        prog = Program(nc, ctx)
        io = {"adj": adj}
        for name in ("h0", "x1", "h1", "x2", "h2", "h2b", "x3", "h3"):
            io[name] = nc.dram_tensor(name, [T, P, B, D], F32).ap()
        for name in ("adjT", "anorm"):
            io[name] = nc.dram_tensor(name, [T, P, T, P], F32).ap()
        io["mT"] = nc.dram_tensor("mT", [T, P, T, P], U8).ap()
        io["hT"] = nc.dram_tensor("hT", [B, P, N], F32).ap()
        io["z1"] = nc.dram_tensor("z1", [T, P, 2, W], F32).ap()
        io["rsrow"] = nc.dram_tensor("rsrow", [T, P], F32).ap()
        io["s2row"] = nc.dram_tensor("s2row", [B * T, P], F32).ap()
        io["erow"] = nc.dram_tensor("erow", [B * T, P], F32).ap()
        io["rrow"] = nc.dram_tensor("rrow", [2 * T, P], F32).ap()
        keep = {k: prog.sb(ctx, f"k_{k}", s) for k, s in dict(
            ident=[P, P], ones=[P, 2], halves=[P, T], rs=[P, T], rsT=[P, P], dinv=[P, T], ndinv=[P, T],
            deg3=[P, T], dinv3=[P, T], wa=[P, 2, D], s1=[P, B, T], s2=[P, B, T], bn1=[P, 2, 2 * T, 6]).items()}
        prepare(prog, io, keep, x, adj, wa, wcT)
        product(prog, io, keep, "l0", io["anorm"], io["h0"], dict(w=w0), "L0",
                x.rearrange("b (t p) f -> t p b f", p=P))
        attention(prog, io, keep, wc)
        prog.retire()
        product(prog, io, keep, "l2a", io["adjT"], io["h2"], dict(w=wg0, b=bg0), "L2a")
        product(prog, io, keep, "l2b", io["adjT"], io["h2b"], dict(w=wg1, b=bg1), "L2b")
        recurrences(prog, io, keep, dict(wih=wih, whh=whh, bih=bih, bhh=bhh))
        product(prog, io, keep, "l3", io["adjT"], io["h3"], dict(w=w1), "L3")
        perceptron(prog, io, keep, dict(w2=w2, vec=vec), out)


def kernel(**inputs):
    import numpy as _np
    import concourse.bacc as _bacc
    from concourse.bass_utils import run_bass_kernel_spmd as _run

    a = {k: _np.asarray(v) for k, v in inputs.items()}
    lay = {
        "x": a["x"],
        "adj": a["adj"],
        "w0": a["L0_gnn_W"],
        "wcT": a["L1_gnn_W"].T,
        "wa": a["L1_gnn_a"].reshape(2, D).T,
        "wc": a["L1_gnn_W"],
        "wg0": a["L2_gnn_Wg0"],
        "bg0": a["L2_gnn_bg0"],
        "wg1": a["L2_gnn_Wg1"],
        "bg1": a["L2_gnn_bg1"].reshape(D, 1),
        "wih": a["L2_gnn_Wih"].transpose(2, 0, 1),
        "whh": a["L2_gnn_Whh"].transpose(2, 0, 1),
        "bih": a["L2_gnn_bih"].reshape(SKIP, 4, D).transpose(2, 0, 1),
        "bhh": a["L2_gnn_bhh"].reshape(SKIP, 4, D).transpose(2, 0, 1),
        "w1": a["L3_gnn_W1"].T,
        "w2": a["L3_gnn_W2"].T.reshape(2, P, D).transpose(1, 0, 2),
        "vec": _np.stack([a[f"L3_gnn_{n}1"].reshape(2, P)[k] for k in range(2) for n in ("b", "g", "be")]
                         + [a[f"L3_gnn_{n}2"] for n in ("b", "g", "be")], axis=1),
    }
    lay = {k: _np.ascontiguousarray(v) for k, v in lay.items()}
    nc = _bacc.Bacc("TRN2", target_bir_lowering=False, num_devices=1)
    args = {k: nc.dram_tensor(f"in_{k}_dram", v.shape, mybir.dt.from_np(v.dtype), kind="ExternalInput").ap()
            for k, v in lay.items()}
    out = nc.dram_tensor("out_0_dram", (B, N, D), F32, kind="ExternalOutput").ap()
    network(nc, out=out, **args)
    r = _run(nc, [{f"in_{k}_dram": v for k, v in lay.items()}], core_ids=[0])
    return r.results[0]["out_0_dram"]
```
